# Optimizing a Trainium2 kernel written in Bass

```python
import numpy as np
import jax
import jax.numpy as jnp

def _softmax(x, axis=-1):
    return jax.nn.softmax(x, axis=axis)

def _gelu(x):
    return jax.nn.gelu(x, approximate=True)

def _silu(x):
    return jax.nn.silu(x)

def _sigmoid(x):
    return jax.nn.sigmoid(x)

def _layernorm(x, axis=-1, eps=1e-05):
    m = jnp.mean(x, axis=axis, keepdims=True)
    v = jnp.var(x, axis=axis, keepdims=True)
    return (x - m) / jnp.sqrt(v + eps)

def _scatter_add(tgt, idx, src, axis=0):
    return tgt.at[idx].add(src)

def _segment_sum(src, seg, n):
    return jax.ops.segment_sum(src, seg, n)
kernel_name = 'mk_seq_preln_d2_jaxref_r8_2748ff'

def setup_inputs(seed: int=0):
    np.random.seed(seed)
    _w = jnp.asarray

    def _L0_attn_setup():
        import jax, jax.numpy as jnp
        import numpy as np
        B, T, E = (4, 256, 128)
        H, HS = (16, 64)
        key = jax.random.key(seed)
        ks = jax.random.split(key, 6)
        return {'x': jax.random.normal(ks[0], (B, T, E), dtype=jnp.float32), 'Wq': jax.random.normal(ks[1], (H, E, HS), dtype=jnp.float32) * 0.02, 'Wk': jax.random.normal(ks[2], (H, E, HS), dtype=jnp.float32) * 0.02, 'Wv': jax.random.normal(ks[3], (H, E, HS), dtype=jnp.float32) * 0.02, 'proj_w': jax.random.normal(ks[4], (E, H * HS), dtype=jnp.float32) * 0.02, 'proj_b': jax.random.normal(ks[5], (E,), dtype=jnp.float32) * 0.02}
    _L0_attn_in = _L0_attn_setup()

    def _L0_ffn_setup():
        import jax, jax.numpy as jnp
        import numpy as np
        E = 16
        K = 4
        NG = 4
        TG = 2
        SCALE = 2.5
        NORM_TOPK = True
        H = 128
        I = 64
        SH_I = I * 2
        B, S = (2, 256)
        key = jax.random.key(seed)
        ks = jax.random.split(key, 9)

        def w(k, shape, fan_in):
            return jax.random.normal(k, shape, jnp.float32) * (1.0 / np.sqrt(fan_in))
        return {'hidden_states': jax.random.normal(ks[0], (B, S, H), jnp.float32), 'gate_w': w(ks[1], (E, H), H), 'gate_bias': jnp.zeros((E,), jnp.float32), 'Wg': w(ks[2], (E, I, H), H), 'Wu': w(ks[3], (E, I, H), H), 'Wd': w(ks[4], (E, H, I), I), 'Ws_g': w(ks[5], (SH_I, H), H), 'Ws_u': w(ks[6], (SH_I, H), H), 'Ws_d': w(ks[7], (H, SH_I), SH_I)}
    _L0_ffn_in = _L0_ffn_setup()

    def _L1_attn_setup():
        import jax, jax.numpy as jnp
        import numpy as np
        D_MODEL, D_INNER, D_STATE, DT_RANK, D_CONV = (128, 256, 16, 64, 4)
        B, L = (2, 256)

        def _rmsnorm(x, w, eps=1e-05):
            return x * jax.lax.rsqrt(jnp.mean(x * x, axis=-1, keepdims=True) + eps) * w

        def _causal_depthwise_conv(x, conv_w, conv_b):
            K = conv_w.shape[1]
            xp = jnp.pad(x, ((0, 0), (K - 1, 0), (0, 0)))
            Lx = x.shape[1]
            out = conv_b
            for k in range(K):
                out = out + xp[:, k:k + Lx, :] * conv_w[:, k]
            return out

        def _selective_scan(x, delta, Bm, Cm, A):
            h0 = jnp.zeros((x.shape[0], A.shape[0], A.shape[1]), x.dtype)

            def step(h, inp):
                xt, dt, bt, ct = inp
                A_bar = jnp.exp(dt[..., None] * A)
                h = A_bar * h + (dt * xt)[..., None] * bt[:, None, :]
                y = jnp.einsum('ben,bn->be', h, ct)
                return (h, y)
            xs = tuple((jnp.swapaxes(a, 0, 1) for a in (x, delta, Bm, Cm)))
            _, ys = jax.lax.scan(step, h0, xs)
            return jnp.swapaxes(ys, 0, 1)
        key = jax.random.key(seed)
        ks = jax.random.split(key, 14)
        s = lambda k, shp, fan: jax.random.normal(k, shp, jnp.float32) / np.sqrt(fan)
        return {'resid': jax.random.normal(ks[0], (B, L, D_MODEL), jnp.float32), 'norm_w': jnp.ones((D_MODEL,), jnp.float32), 'skip_w': s(ks[1], (D_INNER, D_MODEL), D_MODEL), 'in_w': s(ks[2], (D_INNER, D_MODEL), D_MODEL), 'conv_w': s(ks[3], (D_INNER, D_CONV), D_CONV), 'conv_b': jnp.zeros((D_INNER,), jnp.float32), 'wd1': s(ks[4], (DT_RANK, D_INNER), D_INNER), 'wd2': s(ks[5], (D_INNER, DT_RANK), DT_RANK), 'wd2_b': jnp.zeros((D_INNER,), jnp.float32), 'wb': s(ks[6], (D_STATE, D_INNER), D_INNER), 'wc': s(ks[7], (D_STATE, D_INNER), D_INNER), 'A_log': jax.random.normal(ks[8], (D_INNER, D_STATE), jnp.float32), 'W_D': jnp.ones((D_INNER,), jnp.float32), 'out_w': s(ks[9], (D_MODEL, D_INNER), D_INNER)}
    _L1_attn_in = _L1_attn_setup()

    def _L1_ffn_setup():
        import jax, jax.numpy as jnp
        import numpy as np
        B, S, H, F, E = (4, 256, 128, 512, 8)
        key = jax.random.key(seed)
        ks = jax.random.split(key, 8)
        s = 1.0 / np.sqrt(H)
        sf = 1.0 / np.sqrt(F)
        return {'x': jax.random.normal(ks[0], (B, S, H), jnp.float32), 'wr': jax.random.uniform(ks[1], (H, E), jnp.float32, -s, s), 'br': jax.random.uniform(ks[2], (E,), jnp.float32, -s, s), 'w1': jax.random.uniform(ks[3], (E, H, F), jnp.float32, -s, s), 'b1': jax.random.uniform(ks[4], (E, F), jnp.float32, -s, s), 'w2': jax.random.uniform(ks[5], (E, F, H), jnp.float32, -sf, sf), 'b2': jax.random.uniform(ks[6], (E, H), jnp.float32, -sf, sf)}
    _L1_ffn_in = _L1_ffn_setup()
    _d = {'L0_attn_x': _L0_attn_in['x'], 'L0_attn_Wq': _L0_attn_in['Wq'], 'L0_attn_Wk': _L0_attn_in['Wk'], 'L0_attn_Wv': _L0_attn_in['Wv'], 'L0_attn_proj_w': _L0_attn_in['proj_w'], 'L0_attn_proj_b': _L0_attn_in['proj_b'], 'L0_ffn_gate_w': _L0_ffn_in['gate_w'], 'L0_ffn_gate_bias': _L0_ffn_in['gate_bias'], 'L0_ffn_Wg': _L0_ffn_in['Wg'], 'L0_ffn_Wu': _L0_ffn_in['Wu'], 'L0_ffn_Wd': _L0_ffn_in['Wd'], 'L0_ffn_Ws_g': _L0_ffn_in['Ws_g'], 'L0_ffn_Ws_u': _L0_ffn_in['Ws_u'], 'L0_ffn_Ws_d': _L0_ffn_in['Ws_d'], 'L1_attn_norm_w': _L1_attn_in['norm_w'], 'L1_attn_skip_w': _L1_attn_in['skip_w'], 'L1_attn_in_w': _L1_attn_in['in_w'], 'L1_attn_conv_w': _L1_attn_in['conv_w'], 'L1_attn_conv_b': _L1_attn_in['conv_b'], 'L1_attn_wd1': _L1_attn_in['wd1'], 'L1_attn_wd2': _L1_attn_in['wd2'], 'L1_attn_wd2_b': _L1_attn_in['wd2_b'], 'L1_attn_wb': _L1_attn_in['wb'], 'L1_attn_wc': _L1_attn_in['wc'], 'L1_attn_A_log': _L1_attn_in['A_log'], 'L1_attn_W_D': _L1_attn_in['W_D'], 'L1_attn_out_w': _L1_attn_in['out_w'], 'L1_ffn_wr': _L1_ffn_in['wr'], 'L1_ffn_br': _L1_ffn_in['br'], 'L1_ffn_w1': _L1_ffn_in['w1'], 'L1_ffn_b1': _L1_ffn_in['b1'], 'L1_ffn_w2': _L1_ffn_in['w2'], 'L1_ffn_b2': _L1_ffn_in['b2']}
    _x0 = _d['L0_attn_x']
    _d['L0_attn_x'] = jax.random.normal(jax.random.fold_in(jax.random.key(seed), 1), (4, 1024, 128), dtype=_x0.dtype)
    del _x0
    return _d

def reference(L0_attn_x, L0_attn_Wq, L0_attn_Wk, L0_attn_Wv, L0_attn_proj_w, L0_attn_proj_b, L0_ffn_gate_w, L0_ffn_gate_bias, L0_ffn_Wg, L0_ffn_Wu, L0_ffn_Wd, L0_ffn_Ws_g, L0_ffn_Ws_u, L0_ffn_Ws_d, L1_attn_norm_w, L1_attn_skip_w, L1_attn_in_w, L1_attn_conv_w, L1_attn_conv_b, L1_attn_wd1, L1_attn_wd2, L1_attn_wd2_b, L1_attn_wb, L1_attn_wc, L1_attn_A_log, L1_attn_W_D, L1_attn_out_w, L1_ffn_wr, L1_ffn_br, L1_ffn_w1, L1_ffn_b1, L1_ffn_w2, L1_ffn_b2):

    def _L0_attn_ref(x, Wq, Wk, Wv, proj_w, proj_b):
        import jax, jax.numpy as jnp
        import numpy as np
        B, T, E = (4, 256, 128)
        H, HS = (16, 64)
        b, t, e = x.shape
        h, _, hs = Wq.shape
        q = jnp.einsum('bxy,iyk->bxik', x, Wq).reshape(h, b, t, hs)
        k = jnp.einsum('bxy,iyk->bxik', x, Wk).reshape(h, b, t, hs)
        v = jnp.einsum('bxy,iyk->bxik', x, Wv).reshape(h, b, t, hs)
        wei = jnp.einsum('hbqd,hbkd->hbqk', q, k) * hs ** (-0.5)
        causal = jnp.tril(jnp.ones((t, t), dtype=bool))
        wei = jnp.where(causal, wei, -jnp.inf)
        wei = jax.nn.softmax(wei, axis=-1)
        out = jnp.einsum('hbqk,hbkd->hbqd', wei, v)
        out = out.reshape(b, t, h * hs)
        out = out @ proj_w.T + proj_b
        return out

    def _L0_ffn_ref(hidden_states, gate_w, gate_bias, Wg, Wu, Wd, Ws_g, Ws_u, Ws_d):
        import jax, jax.numpy as jnp
        import numpy as np
        E = 16
        K = 4
        NG = 4
        TG = 2
        SCALE = 2.5
        NORM_TOPK = True
        H = 128
        I = 64
        SH_I = I * 2
        B, S = (2, 256)
        x = hidden_states
        b, s, h = x.shape
        n = b * s
        xf = x.reshape(n, h)
        logits = xf @ gate_w.T
        scores = jax.nn.sigmoid(logits)
        sfc = scores + gate_bias
        epg = E // NG
        grp = sfc.reshape(n, NG, epg)
        g_scores = jax.lax.top_k(grp, 2)[0].sum(-1)
        _, gidx = jax.lax.top_k(g_scores, TG)
        gmask = jax.nn.one_hot(gidx, NG, dtype=sfc.dtype).sum(1)
        emask = jnp.repeat(gmask, epg, axis=1)
        masked = jnp.where(emask > 0, sfc, -jnp.inf)
        _, topk_idx = jax.lax.top_k(masked, K)
        topk_w = jnp.take_along_axis(scores, topk_idx, axis=1)
        if K > 1 and NORM_TOPK:
            topk_w = topk_w / (topk_w.sum(-1, keepdims=True) + 1e-20)
        topk_w = topk_w * SCALE
        cw = (jax.nn.one_hot(topk_idx, E, dtype=topk_w.dtype) * topk_w[..., None]).sum(1)
        hg = jnp.einsum('nh,eih->nei', xf, Wg)
        hu = jnp.einsum('nh,eih->nei', xf, Wu)
        act = jax.nn.silu(hg) * hu
        y = jnp.einsum('nei,ne,ehi->nh', act, cw, Wd)
        shared = jax.nn.silu(xf @ Ws_g.T) * (xf @ Ws_u.T) @ Ws_d.T
        y = y + shared
        return (x + y.reshape(b, s, h)).astype(hidden_states.dtype)

    def _L1_attn_ref(resid, norm_w, skip_w, in_w, conv_w, conv_b, wd1, wd2, wd2_b, wb, wc, A_log, W_D, out_w):
        import jax, jax.numpy as jnp
        import numpy as np
        D_MODEL, D_INNER, D_STATE, DT_RANK, D_CONV = (128, 256, 16, 64, 4)
        B, L = (2, 256)

        def _rmsnorm(x, w, eps=1e-05):
            return x * jax.lax.rsqrt(jnp.mean(x * x, axis=-1, keepdims=True) + eps) * w

        def _causal_depthwise_conv(x, conv_w, conv_b):
            K = conv_w.shape[1]
            xp = jnp.pad(x, ((0, 0), (K - 1, 0), (0, 0)))
            Lx = x.shape[1]
            out = conv_b
            for k in range(K):
                out = out + xp[:, k:k + Lx, :] * conv_w[:, k]
            return out

        def _selective_scan(x, delta, Bm, Cm, A):
            h0 = jnp.zeros((x.shape[0], A.shape[0], A.shape[1]), x.dtype)

            def step(h, inp):
                xt, dt, bt, ct = inp
                A_bar = jnp.exp(dt[..., None] * A)
                h = A_bar * h + (dt * xt)[..., None] * bt[:, None, :]
                y = jnp.einsum('ben,bn->be', h, ct)
                return (h, y)
            xs = tuple((jnp.swapaxes(a, 0, 1) for a in (x, delta, Bm, Cm)))
            _, ys = jax.lax.scan(step, h0, xs)
            return jnp.swapaxes(ys, 0, 1)
        x = _rmsnorm(resid, norm_w)
        skip = x @ skip_w.T
        x = x @ in_w.T
        x = _causal_depthwise_conv(x, conv_w, conv_b)
        x = jax.nn.silu(x)
        A = -jnp.exp(A_log)
        delta = jax.nn.softplus(x @ wd1.T @ wd2.T + wd2_b)
        Bm = x @ wb.T
        Cm = x @ wc.T
        y = _selective_scan(x, delta, Bm, Cm, A)
        y = y + x * W_D
        y = y * jax.nn.silu(skip)
        y = y @ out_w.T
        return resid + y

    def _L1_ffn_ref(x, wr, br, w1, b1, w2, b2):
        import jax, jax.numpy as jnp
        import numpy as np
        B, S, H, F, E = (4, 256, 128, 512, 8)
        scores = jnp.einsum('bsh,he->bse', x, wr) + br
        expert_id = jnp.argmax(scores, axis=-1)
        h = jnp.einsum('bsh,ehf->ebsf', x, w1) + b1[:, None, None, :]
        h = jax.nn.gelu(h, approximate=False)
        y = jnp.einsum('ebsf,efh->ebsh', h, w2) + b2[:, None, None, :]
        one_hot = jax.nn.one_hot(expert_id, E, dtype=x.dtype)
        out = jnp.einsum('ebsh,bse->bsh', y, one_hot)
        return out
    x = L0_attn_x
    x = x + _L0_attn_ref(_layernorm(x, axis=-1), L0_attn_Wq, L0_attn_Wk, L0_attn_Wv, L0_attn_proj_w, L0_attn_proj_b)
    x = x + _L0_ffn_ref(_layernorm(x, axis=-1), L0_ffn_gate_w, L0_ffn_gate_bias, L0_ffn_Wg, L0_ffn_Wu, L0_ffn_Wd, L0_ffn_Ws_g, L0_ffn_Ws_u, L0_ffn_Ws_d)
    x = x + _L1_attn_ref(_layernorm(x, axis=-1), L1_attn_norm_w, L1_attn_skip_w, L1_attn_in_w, L1_attn_conv_w, L1_attn_conv_b, L1_attn_wd1, L1_attn_wd2, L1_attn_wd2_b, L1_attn_wb, L1_attn_wc, L1_attn_A_log, L1_attn_W_D, L1_attn_out_w)
    x = x + _L1_ffn_ref(_layernorm(x, axis=-1), L1_ffn_wr, L1_ffn_br, L1_ffn_w1, L1_ffn_b1, L1_ffn_w2, L1_ffn_b2)
    return x

_drawn_inputs = setup_inputs


def setup_inputs(seed=0):
    import zlib

    import numpy as np

    out = dict(_drawn_inputs(seed))
    spreads = {'L0_ffn_gate_bias': (0.0, 0.1),
     'L1_attn_norm_w': (1.0, 0.2),
     'L1_attn_conv_b': (0.0, 0.1),
     'L1_attn_wd2_b': (0.0, 0.569),
     'L1_attn_W_D': (1.0, 0.6)}
    factors = {'L0_attn_Wq': 7.931,
     'L0_attn_Wk': 8.0,
     'L1_ffn_br': 2.955,
     'L1_ffn_b1': 8.0,
     'L1_ffn_b2': 7.259}
    for name, (base, spread) in spreads.items():
        noise = np.random.default_rng([zlib.crc32(name.encode()), seed]).standard_normal(out[name].shape)
        drawn = base * np.exp(spread * noise) if base else spread * noise
        out[name] = jnp.asarray(drawn.astype(out[name].dtype))
    for name, factor in factors.items():
        out[name] = (out[name] * factor).astype(out[name].dtype)
    return out
```

```python
from contextlib import ExitStack

import numpy as np

import concourse.bass as bass
from concourse import mybir

ALU = mybir.AluOpType
ACT = mybir.ActivationFunctionType
AX = mybir.AxisListType
F32 = mybir.dt.float32
BF16 = mybir.dt.bfloat16

P = 128
B, S, E = 4, 1024, 128
NTOK = B * S
TILES = NTOK // P
EPS = 1e-5

HEADS, HD = 16, 64
GROUP_TOK = 64
POS = GROUP_TOK * HEADS
PT = POS // P
TT = GROUP_TOK // PT
PAIRS = HEADS // 2
PARTS = 3
MROWS = PARTS * PT
KAUG = HD + MROWS


class Chain:

    def __init__(self, eng, sem, base=0):
        self.eng, self.sem, self.base, self.n = eng, sem, base, 0

    def __call__(self, ins):
        ins.then_inc(self.sem, 1)
        self.n += 1
        self.eng.wait_ge(self.sem, self.base + self.n)


def bc(ap, n):
    return ap.unsqueeze(len(ap.shape)).broadcast_to([*ap.shape, n])


def start_at_one(sp, *sems):
    for s in sems:
        sp.sem_inc(s, 1)


LN_CHUNKS = 4
CT = TILES // LN_CHUNKS


def layernorm_block(nc, tag, x, xT, half, ident, keep_norm, loads, x_dram=None, rms_w=None):
    with ExitStack() as ctx:
        sb = lambda n, s, d=F32: ctx.enter_context(nc.sbuf_tensor(f"{tag}_{n}", s, d))
        sem = lambda n: ctx.enter_context(nc.semaphore(f"{tag}_{n}"))
        xn = sb("xn", [P, 2, CT, E])
        sq = sb("sq", [P, CT, E])
        st = sb("st", [P, 4, TILES])
        ps = ctx.enter_context(nc.psum_tensor(f"{tag}_ps", [P, 4, 512], F32))
        steps, var_ready, rstd_ready, norm_ready = sem("steps"), sem("var_ready"), sem("rstd_ready"), sem("norm_ready")
        turned, evicted, weights_loaded = sem("turned"), sem("evicted"), sem("weights_loaded")
        x_loaded = [sem(f"x_loaded{c}") for c in range(LN_CHUNKS)]
        block = ctx.enter_context(nc.Block())
        rounds = 2 if rms_w is not None else 1

        @block.sync
        def _(sp):
            if x_dram is not None:
                for c in range(LN_CHUNKS):
                    sl = slice(c * CT, (c + 1) * CT)
                    sp.dma_start(x[:, sl], x_dram.rearrange("(t p) e -> p t e", p=P)[:, sl]).then_inc(x_loaded[c], 16)
            for dst, src in loads:
                sp.dma_start(dst, src).then_inc(weights_loaded, 16)
            sp.wait_ge(weights_loaded, 16 * len(loads))

        @block.vector
        def _(dve):
            step = Chain(dve, steps)
            for c in range(LN_CHUNKS):
                if x_dram is not None:
                    dve.wait_ge(x_loaded[c], 16)
                if c >= 2:
                    dve.wait_ge(turned, (c - 1) * CT)
                xc = x[:, c * CT:(c + 1) * CT, :]
                y = xn[:, c % 2]
                s0, s1, s2, s3 = (st[:, k, c * CT:(c + 1) * CT] for k in range(4))
                step(dve.tensor_reduce(s0, xc, AX.X, ALU.add))
                step(dve.tensor_scalar(s0, s0, -1.0 / E, None, ALU.mult))
                step(dve.tensor_tensor(y, xc, bc(s0, E), ALU.add))
                for r in range(rounds):
                    step(dve.tensor_tensor(sq[:], y, y, ALU.mult))
                    step(dve.tensor_reduce(s1, sq[:], AX.X, ALU.add))
                    dve.tensor_scalar(s2, s1, 1.0 / E, EPS, ALU.mult, ALU.add).then_inc(var_ready, 1)
                    dve.wait_ge(rstd_ready, c * rounds + r + 1)
                    last = r == rounds - 1
                    ins = dve.tensor_tensor(y, y, bc(s3, E), ALU.mult)
                    if last:
                        ins.then_inc(norm_ready, 1)
                        dve.wait_ge(norm_ready, c + 1)
                    else:
                        step(ins)
                    if r == 0 and keep_norm:
                        step(dve.tensor_tensor(xc, xc, y, ALU.add))

        @block.gpsimd
        def _(pool):
            for c in range(LN_CHUNKS):
                for r in range(rounds):
                    pool.wait_ge(var_ready, c * rounds + r + 1)
                    sl = slice(c * CT, (c + 1) * CT)
                    pool.tensor_tensor(st[:, 3, sl], st[:, 2, sl], half[:, 0:CT], ALU.pow).then_inc(rstd_ready, 1)

        @block.tensor
        def _(pe):
            for c in range(LN_CHUNKS):
                pe.wait_ge(norm_ready, c + 1)
                for k in range(CT):
                    n = c * CT + k
                    if k % 4 == 0 and n >= 16:
                        pe.wait_ge(evicted, n // 4 - 3)
                    pe.transpose(ps[:, (n // 4) % 4, (k % 4) * P:(k % 4 + 1) * P], xn[:, c % 2, k, :], ident[:]).then_inc(turned, 1)

        @block.scalar
        def _(act):
            if rms_w is not None:
                act.wait_ge(weights_loaded, 16 * len(loads))
            for q in range(TILES // 4):
                act.wait_ge(turned, 4 * q + 4)
                scale = 1.0 if rms_w is None else rms_w[:, 0:1]
                act.activation(xT[:, q * 512:(q + 1) * 512], ps[:, q % 4, :], ACT.Copy if rms_w is None else ACT.Identity, scale=scale).then_inc(evicted, 1)


def attention_block(nc, xT, wq, wk, wv, identb, mask_qk, mask_kq, row_mask, vd, od):
    with ExitStack() as ctx:
        sb = lambda n, s, d=F32: ctx.enter_context(nc.sbuf_tensor(f"at_{n}", s, d))
        sem = lambda n: ctx.enter_context(nc.semaphore(f"at_{n}"))
        pst = lambda n, s, d=F32: ctx.enter_context(nc.psum_tensor(f"at_{n}", s, d))
        xs = sb("xs", [P, P])
        high = sb("high", [P, 2, 2 * PT, PAIRS, TT], BF16)
        low = sb("low", [P, 2, 2 * PT, PAIRS, TT], BF16)
        q1 = sb("q1", [P, 4, PT, P], BF16)
        q2 = sb("q2", [P, 4, PT, P], BF16)
        k1 = sb("k1", [P, 4, PT, P], BF16)
        k2 = sb("k2", [P, 4, PT, P], BF16)
        zeros = sb("zeros", [P, PT, P], BF16)
        vs = sb("vs", [P, HEADS * HD])
        vp = sb("vp", [P, 4, PT, HD + 1])
        rmax = sb("rmax", [P, PT])
        rest = sb("rest", [P, PT])
        mparts = sb("mparts", [P, PARTS, PT], BF16)
        prob = sb("prob", [P, 2, PT * P])
        rden = sb("rden", [P, 4])
        outs = sb("outs", [P, 2, PT, HD])
        psP = pst("psP", [P, 1024])
        psM = pst("psM", [P, 1024])
        psS = pst("psS", [P, 1024])
        psO = pst("psO", [P, 2, 512])

        setup = sem("setup")
        xs_ready = sem("xs_ready")
        q_ps, k_ps, v_ps = sem("q_ps"), sem("k_ps"), sem("v_ps")
        q_high, k_high, v_out = sem("q_high"), sem("k_high"), sem("v_out")
        q_low, k_low = sem("q_low"), sem("k_low")
        packed = sem("packed")
        rows_clear = sem("rows_clear")
        max_ps, tile_max = sem("max_ps"), sem("tile_max")
        max_split = sem("max_split")
        max_turned, max_rows = sem("max_turned"), sem("max_rows")
        score_ps, probs = sem("score_ps"), sem("probs")
        pv_done = sem("pv_done")
        recip, out_ready = sem("recip"), sem("out_ready")
        o_stored = [[sem(f"o_stored{a}{b}") for b in range(2)] for a in range(2)]
        v_stored = sem("v_stored")
        v_loaded = [sem(f"v_loaded{a}") for a in range(2)]
        block = ctx.enter_context(nc.Block())

        FREE = [0, 0, 1, 2, 4, 5, 6, 7]
        ROUNDS = TILES // 2

        def banks(t):
            return 512 * (t % 2) if t < 4 else 0

        def project(pe, what, tile):
            if what == "q":
                pe.wait_ge(xs_ready, tile + 1)
                if not isinstance(tile, int):
                    pe.wait_ge(max_rows, 2 * tile - 1)
                    pe.wait_ge(v_out, tile)
            elif what == "k":
                pe.wait_ge(q_low, tile + 1)
            else:
                pe.wait_ge(k_low, tile + 1)
            if what == "v":
                for h in range(2):
                    ins = pe.matmul(psP[:, h * 512:(h + 1) * 512], xs[:], wv[:, h * 512:(h + 1) * 512], start=True, stop=True)
            else:
                w = wq if what == "q" else wk
                for j in range(PAIRS):
                    ins = pe.matmul(psP[:, j * P:(j + 1) * P], w[:, j, :], xs[:], start=j % 4 == 0, stop=j % 4 == 3,
                                    skip_group_check=True)
            ins.then_inc({"q": q_ps, "k": k_ps, "v": v_ps}[what], 1)

        def max_pass(pe, slot, g, t):
            if t == 0:
                pe.wait_ge(rows_clear, g + 1)
                if isinstance(g, int):
                    pe.wait_ge(packed, 1)
            pe.wait_ge(tile_max, PT * g + FREE[t])
            for lo in range(0, t + 1, 4):
                hi = min(t + 1, lo + 4)
                c = banks(t) + lo * P
                out = psM[:, c:c + (hi - lo) * P]
                diag = hi == t + 1
                pe.matmul(out, q1[:, slot, t, :], k1[:, slot, lo:hi, :], start=True, stop=False, skip_group_check=True)
                ins = pe.matmul(out, q2[0:KAUG, slot, t, :], k2[0:KAUG, slot, lo:hi, :], start=False, stop=not diag,
                                skip_group_check=True)
                if diag:
                    ins = pe.matmul(out[:, (t - lo) * P:], identb, mask_qk, start=False, stop=True, skip_group_check=True)
            ins.then_inc(max_ps, 1)

        def turn_max(pe, g):
            pe.wait_ge(max_split, 4 * g + 4)
            pe.transpose(psP[0:MROWS, 0:P // 2].bitcast(BF16), mparts[:].rearrange("p a b -> p (a b)"),
                         identb).then_inc(max_turned, 1)

        def score_pass(pe, slot, g, t):
            if t == 0:
                pe.wait_ge(max_rows, g + 1)
            pe.wait_ge(probs, PT * g + FREE[t] + 1)
            for j in range(t + 1):
                c = banks(t) + j * P
                out = psS[:, c:c + P]
                pe.matmul(out, k1[:, slot, j, :], q1[:, slot, t, :], start=j % 4 == 0, stop=False, skip_group_check=True)
                pe.matmul(out, k2[0:KAUG, slot, j, :], q2[0:KAUG, slot, t, :], start=False, stop=j < t,
                          skip_group_check=True)
            pe.matmul(out, identb, mask_kq, start=False, stop=True, skip_group_check=True).then_inc(score_ps, 1)

        def pv_pass(pe, slot, g, loads, t):
            pe.wait_ge(probs, PT * g + t + 2)
            if t == 0:
                pe.wait_ge(v_loaded[slot // 2], loads)
            if t % 4 == 0:
                pe.wait_ge(out_ready, 2 * g + t // 4 + 1)
            for j in range(t + 1):
                c = (t % 4) * (HD + 1)
                ins = pe.matmul(psO[:, t // 4, c:c + HD + 1], prob[:, t % 2, j * P:(j + 1) * P], vp[:, slot, j, :],
                                start=j == 0 and t % 4 == 0, stop=j == t, skip_group_check=True)
            ins.then_inc(pv_done, 1)

        @block.tensor
        def _(pe):
            pe.wait_ge(setup, 4)
            for what in "qkv":
                project(pe, what, 0)
            for t in range(PT):
                max_pass(pe, 0, 0, t)
            pe.wait_ge(v_out, 1)
            turn_max(pe, 0)
            with pe.Fori(0, ROUNDS) as r:
                for s in range(4):
                    g, tile = 4 * r + s, 2 * r + (s // 2 + 1)
                    for t in range(PT):
                        if t == 0 and s % 2:
                            pe.wait_ge(packed, tile + 1)
                        max_pass(pe, (s + 1) % 4, g + 1, t)
                        if s % 2 == 0 and t in (1, 3, 5):
                            project(pe, "qkv"[t // 2], tile)
                        score_pass(pe, s, g, t)
                        if t:
                            pv_pass(pe, s, g, V_LOADS * (r + 1), t - 1)
                    if s % 2 == 0:
                        pe.wait_ge(v_out, tile + 1)
                    turn_max(pe, g + 1)
                    pv_pass(pe, s, g, 0, PT - 1)

        def lower_part(dve, which, tile):
            dve.wait_ge((q_high, k_high)[which], tile + 1)
            src = psP[:].rearrange("p (j g x) -> p g j x", j=PAIRS, x=TT)
            dve.tensor_tensor(low[:, which], src, high[:, which], ALU.subtract).then_inc((q_low, k_low)[which], 1)

        def pack(dve, slot, tile):
            dve.wait_ge(k_low, tile + 1)
            if not isinstance(tile, int):
                dve.wait_ge(pv_done, 2 * PT * (tile - 1) + 2)
            for (dst, rows), (part, which) in (((q1, 0), (high, 0)), ((q1, HD), (low, 0)), ((q2, 0), (high, 0)),
                                               ((k1, 0), (high, 1)), ((k1, HD), (high, 1)), ((k2, 0), (low, 1))):
                for side in range(2):
                    ins = dve.tensor_copy(dst[rows:rows + HD, slot:slot + 2, :, side * HD:(side + 1) * HD].rearrange("p s t c -> p (s t) c"),
                                          part[side * HD:(side + 1) * HD, which].rearrange("p g j x -> p g (j x)"))
            ins.then_inc(packed, 1)

        def reduce_tile(dve, g, t):
            dve.wait_ge(max_ps, PT * g + t + 1)
            dve.tensor_reduce(rmax[:, t:t + 1], psM[:, banks(t):banks(t) + (t + 1) * P], AX.X, ALU.max).then_inc(tile_max, 1)

        def split_max(dve, g):
            dve.wait_ge(tile_max, PT * g + PT)
            if not isinstance(g, int):
                dve.wait_ge(max_turned, g)
            h, m, l = (mparts[:, k, :] for k in range(PARTS))
            dve.tensor_scalar(h, rmax[:], -1.0, None, ALU.mult).then_inc(max_split, 1)
            dve.wait_ge(max_split, 4 * g + 1)
            dve.scalar_tensor_tensor(rest[:], rmax[:], -1.0, h, ALU.mult, ALU.subtract).then_inc(max_split, 1)
            dve.wait_ge(max_split, 4 * g + 2)
            dve.tensor_copy(m, rest[:]).then_inc(max_split, 1)
            dve.wait_ge(max_split, 4 * g + 3)
            dve.tensor_tensor(l, rest[:], m, ALU.subtract).then_inc(max_split, 1)

        def place_max(dve, slot, g):
            dve.wait_ge(max_turned, g + 1)
            src = psP[0:MROWS, 0:P // 2].bitcast(BF16).unsqueeze(1).broadcast_to([MROWS, PT, P])
            dve.tensor_tensor(q2[HD:KAUG, slot], src, row_mask, ALU.mult).then_inc(max_rows, 1)

        def normalise(dve, s, g, uses, h):
            dve.wait_ge(pv_done, PT * g + 4 * h + 6)
            dve.wait_ge(o_stored[s % 2][h], 64 * uses + 1)
            acc = psO[:, h, 0:4 * (HD + 1)].rearrange("p (t c) -> p t c", t=4)
            dve.reciprocal(rden[:], acc[:, :, HD]).then_inc(recip, 1)
            dve.wait_ge(recip, 2 * g + h + 1)
            dve.tensor_tensor(outs[:, s % 2, 4 * h:4 * h + 4, :], acc[:, :, 0:HD], bc(rden[:], HD), ALU.mult).then_inc(out_ready, 1)
            dve.wait_ge(out_ready, 2 * g + h + 3)

        @block.vector
        def _(dve):
            dve.wait_ge(setup, 4)
            lower_part(dve, 0, 0)
            lower_part(dve, 1, 0)
            pack(dve, 0, 0)
            for t in range(PT):
                reduce_tile(dve, 0, t)
            split_max(dve, 0)
            place_max(dve, 0, 0)
            with dve.Fori(0, ROUNDS) as r:
                for s in range(4):
                    g, tile = 4 * r + s, 2 * r + (s // 2 + 1)
                    for t in range(PT):
                        reduce_tile(dve, g + 1, t)
                        if s % 2 == 0 and t in (2, 5):
                            lower_part(dve, t // 5, tile)
                        if t == 4:
                            normalise(dve, s, g, 2 * r + s // 2, 0)
                    if s % 2 == 0:
                        pack(dve, (s + 2) % 4, tile)
                    split_max(dve, g + 1)
                    place_max(dve, (s + 1) % 4, g + 1)
                    normalise(dve, s, g, 2 * r + s // 2, 1)

        def exp_tile(act, g, t):
            act.wait_ge(score_ps, PT * g + t + 1)
            act.wait_ge(pv_done, PT * g + t + 1)
            act.activation(prob[:, t % 2, 0:(t + 1) * P], psS[:, banks(t):banks(t) + (t + 1) * P], ACT.Exp,
                           scale=HD ** -0.5).then_inc(probs, 1)

        def upper_part(act, which, tile):
            act.wait_ge((q_ps, k_ps)[which], tile + 1)
            if not isinstance(tile, int):
                act.wait_ge(packed, tile)
            src = psP[:].rearrange("p (j g x) -> p g j x", j=PAIRS, x=TT)
            act.activation(high[:, which], src, ACT.Copy).then_inc((q_high, k_high)[which], 1)

        def v_to_sbuf(act, tile):
            act.wait_ge(v_ps, tile + 1)
            act.wait_ge(v_stored, 16 * tile)
            act.activation(vs[:], psP[:], ACT.Copy).then_inc(v_out, 1)
            act.activation(xs[:], xT[:, bass.ds((tile + 1) * P, P)], ACT.Copy).then_inc(xs_ready, 1)

        @block.scalar
        def _(act):
            act.activation(xs[:], xT[:, 0:P], ACT.Copy).then_inc(xs_ready, 1)
            upper_part(act, 0, 0)
            upper_part(act, 1, 0)
            v_to_sbuf(act, 0)
            with act.Fori(0, ROUNDS) as r:
                for s in range(4):
                    g, tile = 4 * r + s, 2 * r + (s // 2 + 1)
                    for t in range(PT):
                        exp_tile(act, g, t)
                        if s % 2 == 0 and t in (1, 3):
                            upper_part(act, t // 2, tile)
                        if s % 2 == 0 and t == 5:
                            v_to_sbuf(act, tile)

        def turn_v(sp, slot, tile):
            sp.wait_ge(v_out, tile + 1)
            rows = vd[bass.ds(tile * P, P), :]
            sp.dma_start(rows, vs[:]).then_inc(v_stored, 16)
            sp.wait_ge(v_stored, 16 * tile + 16)
            for h in range(2):
                for t in range(PT):
                    src = vd[bass.ds(tile * P + (h * GROUP_TOK + t * TT), TT), :].rearrange("x (i d) -> i x d", i=HEADS)
                    sp.dma_start(vp[:, slot + h, t, 0:HD], src).then_inc(v_loaded[slot // 2], 16)

        def store_outs(sp, s, g, h):
            sp.wait_ge(out_ready, 2 * g + h + 3)
            for t in range(4 * h, 4 * h + 4):
                dst = od[bass.ds(g * GROUP_TOK + t * TT, TT), :].rearrange("x (i d) -> i x d", i=HEADS)
                sp.dma_start(dst, outs[:, s % 2, t, :]).then_inc(o_stored[s % 2][h], 16)

        @block.sync
        def _(sp):
            start_at_one(sp, probs, *o_stored[0], *o_stored[1])
            sp.wait_ge(setup, 4)
            turn_v(sp, 0, 0)
            with sp.Fori(0, ROUNDS) as r:
                for s in range(4):
                    g, tile = 4 * r + s, 2 * r + (s // 2 + 1)
                    store_outs(sp, s, g, 0)
                    if s % 2 == 0:
                        turn_v(sp, (s + 2) % 4, tile)
                    store_outs(sp, s, g, 1)
            for a in range(2):
                for b in range(2):
                    sp.wait_ge(o_stored[a][b], 64 * 2 * ROUNDS + 1)
            for a in range(2):
                sp.wait_ge(v_loaded[a], V_LOADS * (ROUNDS + (a == 0)))

        @block.gpsimd
        def _(pool):
            pool.memset(k2[HD:KAUG], 1.0).then_inc(setup, 1)
            pool.wait_ge(setup, 1)
            pool.memset(q2[HD:KAUG], 0.0).then_inc(setup, 1)
            pool.wait_ge(setup, 2)
            pool.memset(zeros[HD:KAUG], 0.0).then_inc(setup, 1)
            pool.wait_ge(setup, 3)
            pool.memset(vp[:, :, :, HD:HD + 1], 1.0).then_inc(setup, 1)
            pool.sem_inc(pv_done, 2)
            pool.sem_inc(out_ready, 2)
            pool.wait_ge(setup, 4)
            pool.sem_inc(rows_clear, 4)
            with pool.Fori(0, ROUNDS) as r:
                for s in range(4):
                    pool.wait_ge(score_ps, PT * (4 * r + s) + PT)
                    pool.tensor_tensor(q2[HD:KAUG, s], zeros[HD:KAUG], zeros[HD:KAUG], ALU.add).then_inc(rows_clear, 1)
                    pool.wait_ge(rows_clear, 4 * r + s + 5)


V_LOADS = 2 * PT * 16


def projection_block(nc, x, wp, bias, od, ident):
    with ExitStack() as ctx:
        sb = lambda n, s, d=F32: ctx.enter_context(nc.sbuf_tensor(f"pr_{n}", s, d))
        sem = lambda n: ctx.enter_context(nc.semaphore(f"pr_{n}"))
        KC = HEADS * HD // P
        o = sb("o", [P, 2, KC, P])
        oT = sb("oT", [P, 2, KC, P])
        psT = ctx.enter_context(nc.psum_tensor("pr_psT", [P, 2, KC * P], F32))
        psY = ctx.enter_context(nc.psum_tensor("pr_psY", [P, 2, 512], F32))
        loaded = [sem("loaded0"), sem("loaded1")]
        turned, o_turned, y_ps, added, biased = sem("turned"), sem("o_turned"), sem("y_ps"), sem("added"), sem("biased")
        block = ctx.enter_context(nc.Block())
        ROUNDS = TILES // 2

        @block.sync
        def _(sp):
            start_at_one(sp, added, turned, y_ps)
            with sp.Fori(0, ROUNDS) as r:
                for s in range(2):
                    sp.wait_ge(turned, 2 * r + 1)
                    sp.dma_start(o[:, s], od[bass.ds((2 * r + s) * P, P), :].rearrange("p (k c) -> p k c", c=P)).then_inc(loaded[s], 16)
            for s in range(2):
                sp.wait_ge(loaded[s], 16 * ROUNDS)

        @block.tensor
        def _(pe):
            with pe.Fori(0, ROUNDS) as r:
                for s in range(2):
                    pe.wait_ge(loaded[s], 16 * r + 16)
                    for k in range(KC):
                        ins = pe.transpose(psT[:, s, k * P:(k + 1) * P], o[:, s, k, :], ident[:])
                    ins.then_inc(turned, 1)
                for s in range(2):
                    pe.wait_ge(o_turned, 2 * r + s + 1)
                    pe.wait_ge(added, 2 * r + 1)
                    for k in range(KC):
                        ins = pe.matmul(psY[:, s, 0:E], oT[:, s, k, :], wp[:, k, :], start=k == 0, stop=k == KC - 1)
                    ins.then_inc(y_ps, 1)

        @block.scalar
        def _(act):
            with act.Fori(0, ROUNDS) as r:
                for s in range(2):
                    act.wait_ge(turned, 2 * r + s + 2)
                    act.wait_ge(y_ps, 2 * r + 1)
                    act.activation(oT[:, s], psT[:, s, :], ACT.Copy).then_inc(o_turned, 1)

        @block.vector
        def _(dve):
            dve.tensor_tensor(x[:], x[:], bias.unsqueeze(1).broadcast_to([P, TILES, E]), ALU.add).then_inc(biased, 1)
            dve.wait_ge(biased, 1)
            with dve.Fori(0, ROUNDS) as r:
                for s in range(2):
                    dve.wait_ge(y_ps, 2 * r + s + 2)
                    xt = x[:, bass.ds(2 * r + s, 1), :]
                    dve.tensor_tensor(xt, xt, psY[:, s:s + 1, 0:E], ALU.add).then_inc(added, 1)


def rank_steps(step, dve, cnt, t, v, n, lower):
    sh = list(v.shape)[:-1]
    step(dve.tensor_copy(cnt, lower.unsqueeze(1).broadcast_to([*sh, n])))
    for d in range(1, n):
        ge = t[..., 0:n - d]
        step(dve.tensor_tensor(ge, v[..., 0:n - d], v[..., d:n], ALU.is_ge))
        step(dve.tensor_tensor(cnt[..., d:n], cnt[..., d:n], ge, ALU.add))
        step(dve.tensor_tensor(cnt[..., 0:n - d], cnt[..., 0:n - d], ge, ALU.subtract))


def split_parts(step, dve, parts, v, rest):
    step(dve.tensor_copy(parts[0], v))
    step(dve.tensor_tensor(rest, v, parts[0], ALU.subtract))
    step(dve.tensor_copy(parts[1], rest))
    step(dve.tensor_tensor(parts[2], rest, parts[1], ALU.subtract))


TB = 512
BLOCKS = NTOK // TB
BT = TB // P


def moe0_block(nc, x, xT, wgate, gbias, lower4, lower16, wg, wu, wd, sel, ident, identb):
    NE, TOPK, SCALE = 16, 4, 2.5
    NP_ = NE // 2
    NC = NP_ + 1
    with ExitStack() as ctx:
        sb = lambda n, s, d=F32: ctx.enter_context(nc.sbuf_tensor(f"m0_{n}", s, d))
        sem = lambda n: ctx.enter_context(nc.semaphore(f"m0_{n}"))
        cwT = sb("cwT", [PARTS * NE, NTOK], BF16)
        with ExitStack() as rc:
            rb = lambda n, s, d=F32: rc.enter_context(nc.sbuf_tensor(f"r0_{n}", s, d))
            scores, v, cnt, t = (rb(n, [P, TILES, NE]) for n in ("scores", "v", "cnt", "t"))
            pa, pb, pc, pd, gs, gcnt, gt = (rb(n, [P, TILES, 4]) for n in ("pa", "pb", "pc", "pd", "gs", "gcnt", "gt"))
            den = rb("den", [P, TILES])
            parts = rb("parts", [P, TILES, PARTS, NE], BF16)
            psL = rc.enter_context(nc.psum_tensor("r0_psL", [P, TILES, NE], F32))
            psW = rc.enter_context(nc.psum_tensor("r0_psW", [P, 4, 512], F32))
            logits, scored, steps, turned, evicted, parts_ready = (rc.enter_context(nc.semaphore(f"r0_{n}")) for n in (
                "logits", "scored", "steps", "turned", "evicted", "parts_ready"))
            block = rc.enter_context(nc.Block())

            @block.tensor
            def _(pe):
                for k in range(TILES):
                    ins = pe.matmul(psL[:, k, :], xT[:, k * P:(k + 1) * P], wgate[:], start=k == 0, stop=k == TILES - 1, skip_group_check=True)
                ins.then_inc(logits, 1)
                pe.wait_ge(parts_ready, 1)
                for k in range(TILES):
                    if k % 8 == 0 and k >= 32:
                        pe.wait_ge(evicted, k // 8 - 3)
                    out = psW[0:PARTS * NE, k // 8, :].bitcast(BF16)[:, (k % 8) * P:(k % 8 + 1) * P]
                    pe.transpose(out, parts[:, k].rearrange("p a b -> p (a b)"), identb).then_inc(turned, 1)

            @block.scalar
            def _(act):
                act.wait_ge(logits, 1)
                act.activation(scores[:], psL[:], ACT.Sigmoid).then_inc(scored, 1)
                for q in range(TILES // 8):
                    act.wait_ge(turned, 8 * q + 8)
                    act.activation(cwT[:, q * 1024:(q + 1) * 1024], psW[0:PARTS * NE, q, :].bitcast(BF16), ACT.Copy).then_inc(evicted, 1)

            @block.vector
            def _(dve):
                step = Chain(dve, steps)
                dve.wait_ge(scored, 1)
                step(dve.tensor_tensor(v[:], scores[:], gbias.unsqueeze(1).broadcast_to([P, TILES, NE]), ALU.add))
                v4 = v[:].rearrange("p t (g k) -> p t g k", k=4)
                step(dve.tensor_tensor(pa[:], v4[..., 0], v4[..., 1], ALU.max))
                step(dve.tensor_tensor(pb[:], v4[..., 0], v4[..., 1], ALU.min))
                step(dve.tensor_tensor(pc[:], v4[..., 2], v4[..., 3], ALU.max))
                step(dve.tensor_tensor(pd[:], v4[..., 2], v4[..., 3], ALU.min))
                step(dve.tensor_tensor(gs[:], pa[:], pc[:], ALU.add))
                step(dve.tensor_tensor(pb[:], pa[:], pb[:], ALU.add))
                step(dve.tensor_tensor(pd[:], pc[:], pd[:], ALU.add))
                step(dve.tensor_tensor(gs[:], gs[:], pb[:], ALU.max))
                step(dve.tensor_tensor(gs[:], gs[:], pd[:], ALU.max))
                rank_steps(step, dve, gcnt[:], gt[:], gs[:], 4, lower4)
                step(dve.tensor_scalar(gt[:], gcnt[:], 1.5, None, ALU.is_lt))
                step(dve.tensor_scalar(gt[:], gt[:], 1e30, -1e30, ALU.mult, ALU.add))
                step(dve.tensor_tensor(v4.rearrange("p t g k -> p (t g) k"), v4.rearrange("p t g k -> p (t g) k"),
                                       bc(gt[:].rearrange("p t g -> p (t g)"), 4), ALU.add))
                rank_steps(step, dve, cnt[:], t[:], v[:], NE, lower16)
                step(dve.tensor_scalar(cnt[:], cnt[:], TOPK - 0.5, None, ALU.is_lt))
                step(dve.tensor_tensor(v[:], scores[:], cnt[:], ALU.mult))
                step(dve.tensor_reduce(den[:], v[:], AX.X, ALU.add))
                step(dve.tensor_scalar(den[:], den[:], 1e-20, None, ALU.add))
                step(dve.reciprocal(den[:], den[:]))
                step(dve.tensor_scalar(den[:], den[:], SCALE, None, ALU.mult))
                step(dve.tensor_tensor(v[:], v[:], bc(den[:], NE), ALU.mult))
                split_parts(step, dve, [parts[:, :, k, :] for k in range(PARTS)], v[:], t[:])
                dve.sem_inc(parts_ready, 1)

        act_s = sb("silu", [P, 2, TB])
        prod = sb("prod", [P, TB])
        hid = sb("hid", [P, 2, TB])
        yT = sb("yT", [P, 2, TB])
        psG, psU, psC = (ctx.enter_context(nc.psum_tensor(f"m0_{n}", [P, 2, TB], F32)) for n in ("psG", "psU", "psC"))
        psY = ctx.enter_context(nc.psum_tensor("m0_psY", [P, TB], F32))
        psT = ctx.enter_context(nc.psum_tensor("m0_psT", [P, TB], F32))
        up_ps, silu_ready, prod_ready, hid_ready, y_ps, y_out, y_turned, added = (sem(n) for n in (
            "up_ps", "silu_ready", "prod_ready", "hid_ready", "y_ps", "y_out", "y_turned", "added"))
        block = ctx.enter_context(nc.Block())

        @block.sync
        def _(sp):
            start_at_one(sp, added, hid_ready, prod_ready, y_out, y_ps, y_turned)

        @block.tensor
        def _(pe):
            with pe.Fori(0, BLOCKS) as r:
                tok = xT[:, bass.ds(r * TB, TB)]
                for c in range(NC + 1):
                    if c < NC:
                        pe.wait_ge(hid_ready, NC * r + c) if c else pe.wait_ge(hid_ready, NC * r + 1)
                        pe.matmul(psG[:, c % 2, :], wg[:, c, :], tok, start=True, stop=True)
                        ins = pe.matmul(psU[:, c % 2, :], wu[:, c, :], tok, start=True, stop=True)
                        if c < NP_:
                            ins = pe.matmul(psC[:, c % 2, :], sel[:, c, :], cwT[:, bass.ds(r * TB, TB)], start=True, stop=True)
                        ins.then_inc(up_ps, 1)
                    if c == 0:
                        pe.wait_ge(y_out, r + 1)
                    else:
                        pe.wait_ge(hid_ready, NC * r + c + 1)
                        ins = pe.matmul(psY[:], wd[:, c - 1, :], hid[:, (c - 1) % 2, :], start=c == 1, stop=c == NC)
                        ins.then_inc(y_ps, 1)
                pe.wait_ge(y_out, r + 2)
                pe.wait_ge(added, r + 1)
                for k in range(BT):
                    ins = pe.transpose(psT[:, k * P:(k + 1) * P], yT[:, 0, k * P:(k + 1) * P], ident[:])
                ins.then_inc(y_turned, 1)

        @block.scalar
        def _(act):
            with act.Fori(0, BLOCKS) as r:
                for c in range(NC):
                    act.wait_ge(up_ps, NC * r + c + 1)
                    act.wait_ge(prod_ready, NC * r + c) if c else act.wait_ge(prod_ready, NC * r + 1)
                    act.activation(act_s[:, c % 2, :], psG[:, c % 2, :], ACT.Silu).then_inc(silu_ready, 1)
                act.wait_ge(y_ps, NC * r + NC + 1)
                act.wait_ge(y_turned, r + 1)
                act.activation(yT[:, 0, :], psY[:], ACT.Copy).then_inc(y_out, 1)

        @block.vector
        def _(dve):
            with dve.Fori(0, BLOCKS) as r:
                for c in range(NC):
                    n = NC * r + c
                    dve.wait_ge(silu_ready, n + 1)
                    if c < NP_:
                        dve.wait_ge(hid_ready, n + 1)
                        dve.tensor_tensor(prod[:], act_s[:, c % 2, :], psU[:, c % 2, :], ALU.mult).then_inc(prod_ready, 1)
                        dve.wait_ge(prod_ready, n + 2)
                        dve.wait_ge(y_ps, n) if c else dve.wait_ge(y_ps, n + 1)
                        dve.tensor_tensor(hid[:, c % 2, :], prod[:], psC[:, c % 2, :], ALU.mult).then_inc(hid_ready, 1)
                    else:
                        dve.wait_ge(y_ps, n)
                        dve.tensor_tensor(hid[:, c % 2, :], act_s[:, c % 2, :], psU[:, c % 2, :], ALU.mult).then_inc(hid_ready, 1)
                        dve.wait_ge(hid_ready, n + 2)
                        dve.sem_inc(prod_ready, 1)
                dve.wait_ge(y_turned, r + 2)
                xt = x[:, bass.ds(BT * r, BT), :]
                dve.tensor_tensor(xt, xt, psT[:].rearrange("p (t e) -> p t e", e=E), ALU.add).then_inc(added, 1)


MAMBA = ["skip_w", "in_w", "conv_w", "conv_b", "wdbc", "wd2", "wd2_b", "a_log", "w_d", "out_w", "sel32", "ident"]


def mamba_block(nc, x, xT, skip_w, in_w, conv_w, conv_b, wdbc, wd2, wd2_b, a_log, w_d, out_w, sel32, ident, passed):
    CH, NS, KW, RANK = 2, 16, 4, 64
    PAD = KW - 1
    with ExitStack() as ctx:
        sb = lambda n, s, d=F32: ctx.enter_context(nc.sbuf_tensor(f"mb_{n}", s, d))
        u = sb("u", [P, CH, NTOK])
        gate = sb("gate", [P, CH, NTOK])
        delta = sb("delta", [P, CH, NTOK])
        bcT = sb("bcT", [PARTS * 2 * NS, NTOK], BF16)
        aneg = sb("aneg", [P, CH, NS])

        with ExitStack() as c1:
            sb1 = lambda n, s, d=F32: c1.enter_context(nc.sbuf_tensor(f"mc_{n}", s, d))
            sem = lambda n: c1.enter_context(nc.semaphore(f"mc_{n}"))
            xin = sb1("xin", [P, CH, PAD + S])
            conv = sb1("conv", [P, 2, S])
            ps = c1.enter_context(nc.psum_tensor("mc_ps", [P, 2, CH, TB], F32))
            psi = c1.enter_context(nc.psum_tensor("mc_psi", [P, 2, CH, TB], F32))
            pads, skip_ps, gate_ready, in_ps, in_ready, taps, conv_ready, u_ready, a_exp = (sem(n) for n in (
                "pads", "skip_ps", "gate_ready", "in_ps", "in_ready", "taps", "conv_ready", "u_ready", "a_exp"))
            block = c1.enter_context(nc.Block())

            @block.sync
            def _(sp):
                start_at_one(sp, conv_ready, gate_ready, in_ready, u_ready)

            @block.tensor
            def _(pe):
                with pe.Fori(0, B) as b:
                    for h in range(2):
                        tok = xT[:, bass.ds(b * S + h * TB, TB)]
                        pe.wait_ge(in_ready, 2 * b + 1)
                        for c in range(CH):
                            ins = pe.matmul(psi[:, h, c, :], in_w[:, c * P:(c + 1) * P], tok, start=True, stop=True)
                        ins.then_inc(in_ps, 1)
                    for h in range(2):
                        tok = xT[:, bass.ds(b * S + h * TB, TB)]
                        pe.wait_ge(gate_ready, 2 * b + 1)
                        for c in range(CH):
                            ins = pe.matmul(ps[:, h, c, :], skip_w[:, c * P:(c + 1) * P], tok, start=True, stop=True)
                        ins.then_inc(skip_ps, 1)

            @block.scalar
            def _(act):
                act.wait_ge(pads, 1)
                with act.Fori(0, B) as b:
                    for h in range(2):
                        act.wait_ge(in_ps, 2 * b + h + 1)
                        act.wait_ge(conv_ready, 2 * b + 1)
                        act.activation(xin[:, :, PAD + h * TB:PAD + (h + 1) * TB], psi[:, h], ACT.Copy).then_inc(in_ready, 1)
                    for h in range(2):
                        act.wait_ge(skip_ps, 2 * b + h + 1)
                        act.sem_inc(passed, 1)
                        act.activation(gate[:, :, bass.ds(b * S + h * TB, TB)], ps[:, h], ACT.Silu).then_inc(gate_ready, 1)
                    for c in range(CH):
                        act.wait_ge(conv_ready, 2 * b + c + 2)
                        act.sem_inc(passed, 1)
                        act.activation(u[:, c, bass.ds(b * S, S)], conv[:, c, :], ACT.Silu, bias=conv_b[:, c, 0:1]).then_inc(u_ready, 1)
                act.activation(aneg[:], a_log, ACT.Exp).then_inc(a_exp, 1)

            @block.vector
            def _(dve):
                dve.memset(xin[:, :, 0:PAD], 0.0).then_inc(pads, 1)
                with dve.Fori(0, B) as b:
                    dve.wait_ge(in_ready, 2 * b + 3)
                    dve.wait_ge(u_ready, 2 * b + 1)
                    for k in range(KW):
                        for c in range(CH):
                            src, w, out = xin[:, c, k:k + S], conv_w[:, c, k:k + 1], conv[:, c, :]
                            if k == 0:
                                ins = dve.tensor_scalar(out, src, w, None, ALU.mult)
                            else:
                                dve.wait_ge(taps, 6 * b + 2 * (k - 1) + c + 1)
                                ins = dve.scalar_tensor_tensor(out, src, w, out, ALU.mult, ALU.add)
                            ins.then_inc(conv_ready if k == KW - 1 else taps, 1)
                dve.wait_ge(a_exp, 1)
                dve.tensor_scalar(aneg[:], aneg[:], -1.0, None, ALU.mult).then_inc(a_exp, 1)
                dve.wait_ge(a_exp, 2)

        with ExitStack() as c2:
            sb2 = lambda n, s, d=F32: c2.enter_context(nc.sbuf_tensor(f"md_{n}", s, d))
            sem = lambda n: c2.enter_context(nc.semaphore(f"md_{n}"))
            z1 = sb2("z1", [RANK, 2, TB])
            pos, mag = sb2("pos", [P, 2, CH, TB]), sb2("mag", [P, 2, CH, TB])
            middle, rest = sb2("middle", [2 * NS, TB], BF16), sb2("rest", [2 * NS, TB])
            psA = c2.enter_context(nc.psum_tensor("md_psA", [P, TB], F32))
            psZ = c2.enter_context(nc.psum_tensor("md_psZ", [P, 2, CH, TB], F32))
            z1_ps, z1_ready, bc_steps, z2_ps, mag_ready, pos_ready, exp_ready, log_ready, delta_ready = (sem(n) for n in (
                "z1_ps", "z1_ready", "bc_steps", "z2_ps", "mag_ready", "pos_ready", "exp_ready", "log_ready", "delta_ready"))
            block = c2.enter_context(nc.Block())

            @block.sync
            def _(sp):
                start_at_one(sp, bc_steps, delta_ready, pos_ready, z1_ready, z2_ps)

            @block.tensor
            def _(pe):
                with pe.Fori(0, BLOCKS // 2) as r:
                    for s in range(2):
                        n = 2 * r + s
                        pe.wait_ge(z1_ready, n + 1)
                        pe.wait_ge(bc_steps, 4 * n + 1)
                        for c in range(CH):
                            ins = pe.matmul(psA[0:RANK + 2 * NS, :], wdbc[:, c, :], u[:, c, bass.ds(n * TB, TB)], start=c == 0, stop=c == CH - 1)
                        ins.then_inc(z1_ps, 1)
                        pe.wait_ge(z1_ready, n + 2)
                        pe.wait_ge(pos_ready, 2 * r + 1)
                        for c in range(CH):
                            ins = pe.matmul(psZ[:, s, c, :], wd2[:, c * P:(c + 1) * P], z1[:, s, :], start=True, stop=True)
                        ins.then_inc(z2_ps, 1)

            @block.scalar
            def _(act):
                with act.Fori(0, BLOCKS // 2) as r:
                    for s in range(2):
                        n = 2 * r + s
                        act.wait_ge(z1_ps, n + 1)
                        act.wait_ge(z2_ps, 2 * r + 1)
                        act.activation(z1[:, s, :], psA[0:RANK, :], ACT.Copy).then_inc(z1_ready, 1)
                        act.wait_ge(mag_ready, n + 1)
                        act.activation(mag[:, s], mag[:, s], ACT.Exp, scale=-1.0).then_inc(exp_ready, 1)
                        act.wait_ge(exp_ready, n + 1)
                        act.activation(mag[:, s], mag[:, s], ACT.Ln, bias=1.0).then_inc(log_ready, 1)

            @block.vector
            def _(dve):
                with dve.Fori(0, BLOCKS // 2) as r:
                    for s in range(2):
                        n = 2 * r + s
                        dve.wait_ge(z2_ps, n + 2)
                        for c in range(CH):
                            dve.wait_ge(delta_ready, 2 * r + 1)
                            dve.tensor_scalar(mag[:, s, c, :], psZ[:, s, c, :], wd2_b[:, c, 0:1], 0.0, ALU.add, ALU.min)
                        for c in range(CH):
                            ins = dve.tensor_scalar(pos[:, s, c, :], psZ[:, s, c, :], wd2_b[:, c, 0:1], 0.0, ALU.add, ALU.max)
                        ins.then_inc(pos_ready, 1)
                        dve.wait_ge(pos_ready, n + 2)
                        dve.tensor_tensor(mag[:, s], pos[:, s], mag[:, s], ALU.subtract).then_inc(mag_ready, 1)
                        dve.wait_ge(z1_ps, n + 1)
                        part = [bcT[k * 2 * NS:(k + 1) * 2 * NS, bass.ds(n * TB, TB)] for k in range(PARTS)]
                        dve.tensor_copy(part[0], psA[RANK:RANK + 2 * NS, :]).then_inc(bc_steps, 1)
                        dve.wait_ge(bc_steps, 4 * n + 2)
                        dve.tensor_tensor(rest[:], psA[RANK:RANK + 2 * NS, :], part[0], ALU.subtract).then_inc(bc_steps, 1)
                        dve.wait_ge(bc_steps, 4 * n + 3)
                        dve.tensor_copy(middle[:], rest[:]).then_inc(bc_steps, 1)
                        dve.wait_ge(bc_steps, 4 * n + 4)
                        dve.tensor_copy(part[1], middle[:])
                        dve.tensor_tensor(part[2], rest[:], middle[:], ALU.subtract).then_inc(bc_steps, 1)
                        dve.wait_ge(bc_steps, 4 * n + 5)
                        dve.wait_ge(log_ready, n + 1)
                        dve.tensor_tensor(delta[:, :, bass.ds(n * TB, TB)], pos[:, s], mag[:, s], ALU.add).then_inc(delta_ready, 1)


        with ExitStack() as c3:
            sb3 = lambda n, s, d=F32: c3.enter_context(nc.sbuf_tensor(f"ms_{n}", s, d))
            sem = lambda n: c3.enter_context(nc.semaphore(f"ms_{n}"))
            du = sb3("du", [P, CH, S])
            decay, inject, state, part_y = (sb3(n, [P, 2, S]) for n in ("decay", "inject", "state", "part_y"))
            y = sb3("y", [P, CH, S])
            psB = c3.enter_context(nc.psum_tensor("ms_psB", [P, 2, S], F32))
            psC = c3.enter_context(nc.psum_tensor("ms_psC", [P, 2, S], F32))
            bc_ready, du_ready, decay_ready, inject_ready, state_ready, read_out, summed, ends = (sem(n) for n in (
                "bc_ready", "du_ready", "decay_ready", "inject_ready", "state_ready", "read_out", "summed", "ends"))
            block = c3.enter_context(nc.Block())

            @block.sync
            def _(sp):
                start_at_one(sp, read_out, state_ready, summed)
            UNITS = CH * NS

            @block.tensor
            def _(pe):
                with pe.Fori(0, B) as b:
                    for n in range(NS):
                        pe.wait_ge(read_out, UNITS * b + max(0, CH * (n - 1)) + 1)
                        for bank, row in ((psB, n), (psC, NS + n)):
                            for h in range(2):
                                ins = pe.matmul(bank[:, n % 2, h * TB:(h + 1) * TB], sel32[:, row, :],
                                                bcT[:, bass.ds(b * S + h * TB, TB)], start=True, stop=True)
                        ins.then_inc(bc_ready, 1)

            @block.scalar
            def _(act):
                with act.Fori(0, B) as b:
                    for w in range(UNITS):
                        n, c = w // CH, w % CH
                        act.wait_ge(state_ready, UNITS * b + max(0, w - 1) + 1)
                        act.sem_inc(passed, 1)
                        act.activation(decay[:, w % 2, :], delta[:, c, bass.ds(b * S, S)], ACT.Exp,
                                       scale=aneg[:, c, n:n + 1]).then_inc(decay_ready, 1)

            @block.vector
            def _(dve):
                with dve.Fori(0, B) as b:
                    seq = bass.ds(b * S, S)
                    base = UNITS * b
                    dve.tensor_tensor(du[:], delta[:, :, seq], u[:, :, seq], ALU.mult).then_inc(du_ready, 1)
                    dve.wait_ge(du_ready, b + 1)
                    for i in range(UNITS + 2):
                        w = i
                        if w < UNITS:
                            n, c = w // CH, w % CH
                            if c == 0:
                                dve.wait_ge(bc_ready, NS * b + n + 1)
                            dve.wait_ge(state_ready, base + max(0, w - 1) + 1)
                            dve.tensor_tensor(inject[:, w % 2, :], du[:, c, :], psB[:, n % 2, :], ALU.mult).then_inc(inject_ready, 1)
                        w = i - 1
                        if 0 <= w < UNITS:
                            dve.wait_ge(inject_ready, base + w + 1)
                            dve.wait_ge(decay_ready, base + w + 1)
                            dve.wait_ge(read_out, base + max(0, w - 1) + 1)
                            dve.tensor_tensor_scan(state[:, w % 2, :], decay[:, w % 2, :], inject[:, w % 2, :], 0.0,
                                                   ALU.mult, ALU.add).then_inc(state_ready, 1)
                        w = i - 2
                        if 0 <= w:
                            n, c = w // CH, w % CH
                            dve.wait_ge(state_ready, base + w + 2)
                            if n:
                                dve.wait_ge(summed, (UNITS - CH) * b + max(0, w - CH - 1) + 1)
                            out = part_y[:, w % 2, :] if n else y[:, c, :]
                            dve.tensor_tensor(out, state[:, w % 2, :], psC[:, n % 2, :], ALU.mult).then_inc(read_out, 1)
                    dve.wait_ge(summed, (UNITS - CH) * b + UNITS - CH + 1)
                    for c in range(CH):
                        dve.scalar_tensor_tensor(y[:, c, :], u[:, c, seq], w_d[:, c, 0:1], y[:, c, :], ALU.mult, ALU.add).then_inc(ends, 1)
                    dve.wait_ge(ends, 3 * b + 2)
                    dve.tensor_tensor(u[:, :, seq], y[:], gate[:, :, seq], ALU.mult).then_inc(ends, 1)
                    dve.wait_ge(ends, 3 * b + 3)

            @block.gpsimd
            def _(pool):
                with pool.Fori(0, B) as b:
                    for w in range(CH, UNITS):
                        pool.wait_ge(read_out, UNITS * b + w + 2)
                        pool.wait_ge(summed, (UNITS - CH) * b + max(0, w - CH - 1) + 1)
                        pool.tensor_tensor(y[:, w % CH, :], y[:, w % CH, :], part_y[:, w % 2, :], ALU.add).then_inc(summed, 1)

        with ExitStack() as c4:
            sem = lambda n: c4.enter_context(nc.semaphore(f"mo_{n}"))
            yT = c4.enter_context(nc.sbuf_tensor("mo_yT", [P, 2, TB], F32))
            psY = c4.enter_context(nc.psum_tensor("mo_psY", [P, 2, TB], F32))
            psT = c4.enter_context(nc.psum_tensor("mo_psT", [P, 2, TB], F32))
            y_ps, y_out, y_turned, added = (sem(n) for n in ("y_ps", "y_out", "y_turned", "added"))
            block = c4.enter_context(nc.Block())

            @block.sync
            def _(sp):
                start_at_one(sp, added, y_out, y_turned)

            @block.tensor
            def _(pe):
                with pe.Fori(0, BLOCKS // 2) as r:
                    for s in range(2):
                        pe.wait_ge(y_out, 2 * r + 1)
                        for c in range(CH):
                            ins = pe.matmul(psY[:, s, :], out_w[:, c, :], u[:, c, bass.ds((2 * r + s) * TB, TB)], start=c == 0, stop=c == CH - 1)
                        ins.then_inc(y_ps, 1)
                    for s in range(2):
                        pe.wait_ge(y_out, 2 * r + s + 2)
                        pe.wait_ge(added, 2 * r + 1)
                        for k in range(BT):
                            ins = pe.transpose(psT[:, s, k * P:(k + 1) * P], yT[:, s, k * P:(k + 1) * P], ident[:])
                        ins.then_inc(y_turned, 1)

            @block.scalar
            def _(act):
                with act.Fori(0, BLOCKS // 2) as r:
                    for s in range(2):
                        act.wait_ge(y_ps, 2 * r + s + 1)
                        act.wait_ge(y_turned, 2 * r + 1)
                        act.activation(yT[:, s, :], psY[:, s, :], ACT.Copy).then_inc(y_out, 1)

            @block.vector
            def _(dve):
                with dve.Fori(0, BLOCKS // 2) as r:
                    for s in range(2):
                        dve.wait_ge(y_turned, 2 * r + s + 2)
                        xt = x[:, bass.ds(BT * (2 * r + s), BT), :]
                        dve.tensor_tensor(xt, xt, psT[:, s, :].rearrange("p (t e) -> p t e", e=E), ALU.add).then_inc(added, 1)


MOE1 = ["wr", "br", "lower8", "w1", "b1", "w2", "b2", "sel8", "ident", "identb"]


def moe1_block(nc, x, xT, wr, br, lower8, w1, b1, w2, b2, sel8, ident, identb):
    NE, NC = 8, 32
    with ExitStack() as ctx:
        sb = lambda n, s, d=F32: ctx.enter_context(nc.sbuf_tensor(f"m1_{n}", s, d))
        sem = lambda n: ctx.enter_context(nc.semaphore(f"m1_{n}"))
        hotT = sb("hotT", [NE, NTOK], BF16)
        hotF = sb("hotF", [NE, NTOK])
        with ExitStack() as rc:
            rb = lambda n, s, d=F32: rc.enter_context(nc.sbuf_tensor(f"r1_{n}", s, d))
            v, cnt, t = (rb(n, [P, TILES, NE]) for n in ("v", "cnt", "t"))
            psL = rc.enter_context(nc.psum_tensor("r1_psL", [P, TILES, NE], F32))
            psW = rc.enter_context(nc.psum_tensor("r1_psW", [P, 4, 512], F32))
            logits, steps, turned, evicted, hot_ready = (rc.enter_context(nc.semaphore(f"r1_{n}")) for n in (
                "logits", "steps", "turned", "evicted", "hot_ready"))
            block = rc.enter_context(nc.Block())

            @block.tensor
            def _(pe):
                for k in range(TILES):
                    ins = pe.matmul(psL[:, k, :], xT[:, k * P:(k + 1) * P], wr[:], start=k == 0, stop=k == TILES - 1, skip_group_check=True)
                ins.then_inc(logits, 1)
                pe.wait_ge(hot_ready, 1)
                for k in range(TILES):
                    if k % 4 == 0 and k >= 16:
                        pe.wait_ge(evicted, 2 * (k // 4 - 3))
                    pe.transpose(psW[0:NE, (k // 4) % 4, (k % 4) * P:(k % 4 + 1) * P], v[:, k, :], ident[:]).then_inc(turned, 1)

            @block.scalar
            def _(act):
                for q in range(TILES // 4):
                    act.wait_ge(turned, 4 * q + 4)
                    src = psW[0:NE, q % 4, :]
                    act.activation(hotT[:, q * 512:(q + 1) * 512], src, ACT.Copy).then_inc(evicted, 1)
                    act.activation(hotF[:, q * 512:(q + 1) * 512], src, ACT.Copy).then_inc(evicted, 1)

            @block.vector
            def _(dve):
                step = Chain(dve, steps)
                dve.wait_ge(logits, 1)
                step(dve.tensor_tensor(v[:], psL[:], br.unsqueeze(1).broadcast_to([P, TILES, NE]), ALU.add))
                rank_steps(step, dve, cnt[:], t[:], v[:], NE, lower8)
                step(dve.tensor_scalar(v[:], cnt[:], 0.5, None, ALU.is_lt))
                dve.sem_inc(hot_ready, 1)

        g = sb("g", [P, 3, TB])
        hid = sb("hid", [P, 2, TB])
        yT = sb("yT", [P, TB])
        psH = ctx.enter_context(nc.psum_tensor("m1_psH", [P, 2, TB], F32))
        psC = ctx.enter_context(nc.psum_tensor("m1_psC", [P, 2, TB], F32))
        psY = ctx.enter_context(nc.psum_tensor("m1_psY", [P, TB], F32))
        psT = ctx.enter_context(nc.psum_tensor("m1_psT", [P, TB], F32))
        h_ps, gelu_ready, hid_ready, y_ps, y_out, y_turned, added = (sem(n) for n in (
            "h_ps", "gelu_ready", "hid_ready", "y_ps", "y_out", "y_turned", "added"))
        block = ctx.enter_context(nc.Block())

        @block.sync
        def _(sp):
            start_at_one(sp, added, gelu_ready, hid_ready, y_out, y_ps, y_turned)
        LAG = 2

        @block.tensor
        def _(pe):
            with pe.Fori(0, BLOCKS) as r:
                sl = bass.ds(r * TB, TB)
                for i in range(NC + LAG):
                    c = i
                    if c < NC:
                        pe.wait_ge(gelu_ready, NC * r + max(0, c - 1) + 1)
                        if c % 4 == 0:
                            pe.wait_ge(hid_ready, NC * r + max(0, c - 4) + 1)
                        ins = pe.matmul(psH[:, c % 2, :], w1[:, c * P:(c + 1) * P], xT[:, sl], start=True, stop=True)
                        if c % 4 == 0:
                            ins = pe.matmul(psC[:, (c // 4) % 2, :], sel8[:, c // 4, :], hotT[:, sl], start=True, stop=True)
                        ins.then_inc(h_ps, 1)
                    c = i - LAG
                    if c == 0:
                        pe.wait_ge(y_out, r + 1)
                    if c >= 0:
                        pe.wait_ge(hid_ready, NC * r + c + 2)
                        ins = pe.matmul(psY[:], w2[:, c, :], hid[:, c % 2, :], start=c == 0, stop=c == NC - 1)
                        ins.then_inc(y_ps, 1)
                    if c == 0:
                        pe.matmul(psY[:], b2[:], hotF[:, sl], start=False, stop=False)
                pe.wait_ge(y_out, r + 2)
                pe.wait_ge(added, r + 1)
                for k in range(BT):
                    ins = pe.transpose(psT[:, k * P:(k + 1) * P], yT[:, k * P:(k + 1) * P], ident[:])
                ins.then_inc(y_turned, 1)

        @block.scalar
        def _(act):
            with act.Fori(0, BLOCKS) as r:
                for c in range(NC):
                    act.wait_ge(h_ps, NC * r + c + 1)
                    act.wait_ge(hid_ready, NC * r + max(0, c - 2) + 1)
                    act.activation(g[:, c % 3, :], psH[:, c % 2, :], ACT.Gelu, bias=b1[:, c:c + 1]).then_inc(gelu_ready, 1)
                act.wait_ge(y_ps, NC * r + NC + 1)
                act.wait_ge(y_turned, r + 1)
                act.activation(yT[:], psY[:], ACT.Copy).then_inc(y_out, 1)

        @block.vector
        def _(dve):
            with dve.Fori(0, BLOCKS) as r:
                for c in range(NC):
                    dve.wait_ge(gelu_ready, NC * r + c + 2)
                    dve.wait_ge(y_ps, NC * r + max(0, c - 1) + 1)
                    dve.tensor_tensor(hid[:, c % 2, :], g[:, c % 3, :], psC[:, (c // 4) % 2, :], ALU.mult).then_inc(hid_ready, 1)
                dve.wait_ge(y_turned, r + 2)
                xt = x[:, bass.ds(BT * r, BT), :]
                dve.tensor_tensor(xt, xt, psT[:].rearrange("p (t e) -> p t e", e=E), ALU.add).then_inc(added, 1)


def four_layers(nc, a, out):
    with ExitStack() as ctx:
        sb = lambda n, s, d=F32: ctx.enter_context(nc.sbuf_tensor(n, s, d))
        x = sb("x", [P, TILES, E])
        xT = sb("xT", [P, NTOK + 2 * P])
        ident = sb("ident", [P, P])
        identb = sb("identb", [P, P], BF16)
        half = sb("half", [P, CT])
        vd = nc.dram_tensor("v_by_token", [NTOK + P, HEADS * HD], F32).ap()
        od = nc.dram_tensor("heads_out", [NTOK, HEADS * HD], F32).ap()
        const_ready = ctx.enter_context(nc.semaphore("const_ready"))
        const_loaded = ctx.enter_context(nc.semaphore("const_loaded"))
        passed = ctx.enter_context(nc.semaphore("act_passed"))
        stored = ctx.enter_context(nc.semaphore("stored"))

        with nc.Block() as block:
            @block.sync
            def _(sp):
                sp.dma_start(ident[:], a["ident"]).then_inc(const_loaded, 16)
                sp.dma_start(identb[:], a["identb"]).then_inc(const_loaded, 16)
                sp.wait_ge(const_loaded, 32)

            @block.vector
            def _(dve):
                dve.memset(half[:], -0.5).then_inc(const_ready, 1)
                dve.memset(xT[:, NTOK:], 0.0).then_inc(const_ready, 1)
                dve.wait_ge(const_ready, 2)

        def weights(c, names):
            held = {n: c.enter_context(nc.sbuf_tensor(f"w_{n}", list(a[n].shape), a[n].dtype))[:] for n in names}
            return held, [(held[n], a[n]) for n in names]

        with ExitStack() as c:
            w, loads = weights(c, ["wq", "wk", "wv", "mask_qk", "mask_kq", "row_mask", "wp", "bp"])
            layernorm_block(nc, "ln0", x, xT, half, ident, False, loads, x_dram=a["L0_attn_x"])
            attention_block(nc, xT, w["wq"], w["wk"], w["wv"], identb[:], w["mask_qk"], w["mask_kq"], w["row_mask"], vd, od)
            projection_block(nc, x, w["wp"], w["bp"], od, ident)
        with ExitStack() as c:
            names = ["wgate", "gbias", "lower4", "lower16", "wg", "wu", "wd", "sel"]
            w, loads = weights(c, names)
            layernorm_block(nc, "ln1", x, xT, half, ident, True, loads)
            moe0_block(nc, x, xT, *[w[n] for n in names], ident, identb[:])
        with ExitStack() as c:
            names = [n for n in MAMBA if n != "ident"]
            w, loads = weights(c, names + ["norm_w"])
            layernorm_block(nc, "ln2", x, xT, half, ident, True, loads, rms_w=w["norm_w"])
            mamba_block(nc, x, xT, *[w[n] for n in names], ident, passed)
        with ExitStack() as c:
            names = [n for n in MOE1 if n not in ("ident", "identb")]
            w, loads = weights(c, names)
            layernorm_block(nc, "ln3", x, xT, half, ident, False, loads)
            moe1_block(nc, x, xT, *[w[n] for n in names], ident, identb[:])

        with nc.Block() as block:
            @block.sync
            def _(sp):
                sp.dma_start(out.rearrange("(t p) e -> p t e", p=P), x[:]).then_inc(stored, 16)
                sp.wait_ge(stored, 16)


def host_constants():
    bf16 = np.dtype("bfloat16")
    c = {"ident": np.eye(P, dtype=np.float32), "identb": np.eye(P, dtype=np.float32).astype(bf16)}
    at = np.arange(P) % TT * HEADS + np.arange(P) // TT
    mask = np.where(at[None, :] <= at[:, None], 0.0, -1e30).astype(bf16)
    c["mask_qk"], c["mask_kq"] = mask, np.ascontiguousarray(mask.T)
    rows = np.zeros((MROWS, PT, P), np.float32)
    for r in range(MROWS):
        rows[r, r % PT] = 1
    c["row_mask"] = rows.astype(bf16)
    for n in (4, 8, 16):
        c[f"lower{n}"] = np.tile(np.arange(n - 1, -1, -1, dtype=np.float32), (P, 1))
    sel = np.zeros((3, 16, 8, P), np.float32)
    for e in range(16):
        sel[:, e, e // 2, (e % 2) * 64:(e % 2 + 1) * 64] = 1
    c["sel"] = sel.reshape(48, 8, P).astype(bf16)
    sel = np.zeros((8, 8, P), np.float32)
    for e in range(8):
        sel[e, e] = 1
    c["sel8"] = sel.astype(bf16)
    sel = np.zeros((3, 32, 32, P), np.float32)
    for e in range(32):
        sel[:, e, e] = 1
    c["sel32"] = sel.reshape(96, 32, P).astype(bf16)
    return c


def host_weights(d):
    ca = np.ascontiguousarray
    pair = lambda w: ca(np.stack([np.concatenate([w[j], w[j + PAIRS]], 1) for j in range(PAIRS)], 1))
    w = {"wq": pair(d["L0_attn_Wq"]), "wk": pair(d["L0_attn_Wk"]),
         "wv": ca(d["L0_attn_Wv"].transpose(1, 0, 2).reshape(E, HEADS * HD)),
         "wp": ca(d["L0_attn_proj_w"].T.reshape(8, P, E).transpose(1, 0, 2)),
         "bp": ca(np.broadcast_to(d["L0_attn_proj_b"], (P, E)))}
    w["wgate"] = ca(d["L0_ffn_gate_w"].T)
    w["gbias"] = ca(np.broadcast_to(d["L0_ffn_gate_bias"], (P, 16)))
    up = lambda we, ws: ca(np.concatenate([we.reshape(1024, E), ws]).reshape(9, P, E).transpose(2, 0, 1))
    w["wg"], w["wu"] = up(d["L0_ffn_Wg"], d["L0_ffn_Ws_g"]), up(d["L0_ffn_Wu"], d["L0_ffn_Ws_u"])
    w["wd"] = ca(np.concatenate([d["L0_ffn_Wd"].transpose(0, 2, 1).reshape(1024, E), d["L0_ffn_Ws_d"].T]).reshape(9, P, E).transpose(1, 0, 2))
    chan = lambda a: ca(a.reshape(2, P, -1).transpose(1, 0, 2))
    w["norm_w"] = ca(d["L1_attn_norm_w"].reshape(P, 1))
    w["skip_w"], w["in_w"] = ca(d["L1_attn_skip_w"].T), ca(d["L1_attn_in_w"].T)
    w["conv_w"], w["conv_b"] = chan(d["L1_attn_conv_w"]), chan(d["L1_attn_conv_b"])
    w["wdbc"] = chan(np.concatenate([d["L1_attn_wd1"], d["L1_attn_wb"], d["L1_attn_wc"]]).T)
    w["wd2"], w["wd2_b"] = ca(d["L1_attn_wd2"].T), chan(d["L1_attn_wd2_b"])
    w["a_log"], w["w_d"] = chan(d["L1_attn_A_log"]), chan(d["L1_attn_W_D"])
    w["out_w"] = chan(d["L1_attn_out_w"].T)
    w["wr"], w["br"] = ca(d["L1_ffn_wr"]), ca(np.broadcast_to(d["L1_ffn_br"], (P, 8)))
    w["w1"] = ca(d["L1_ffn_w1"].transpose(1, 0, 2).reshape(E, 4096))
    w["b1"] = ca(d["L1_ffn_b1"].reshape(32, P).T)
    w["w2"] = ca(d["L1_ffn_w2"].reshape(32, P, E).transpose(1, 0, 2))
    w["b2"] = ca(d["L1_ffn_b2"])
    return w


def kernel(**inputs):
    import concourse.bacc as bacc
    from concourse.bass_utils import run_bass_kernel_spmd

    data = {n: np.asarray(v) for n, v in inputs.items()}
    arrays = {**host_constants(), **host_weights(data)}
    arrays["L0_attn_x"] = np.ascontiguousarray(data["L0_attn_x"].reshape(NTOK, E))
    nc = bacc.Bacc("TRN2", target_bir_lowering=False, num_devices=1)
    arrays = {f"in_{n}": v for n, v in arrays.items()}
    aps = {n[3:]: nc.dram_tensor(n, v.shape, mybir.dt.from_np(v.dtype), kind="ExternalInput").ap() for n, v in arrays.items()}
    out = nc.dram_tensor("out_0", (NTOK, E), F32, kind="ExternalOutput").ap()
    four_layers(nc, aps, out)
    r = run_bass_kernel_spmd(nc, [arrays], core_ids=[0])
    return r.results[0]["out_0"].reshape(B, S, E)
```

```python
from contextlib import ExitStack

import numpy as np

import concourse.bass as bass
from concourse import mybir

ALU = mybir.AluOpType
ACT = mybir.ActivationFunctionType
AX = mybir.AxisListType
F32 = mybir.dt.float32
BF16 = mybir.dt.bfloat16

P = 128
B, S, E = 4, 1024, 128
NTOK = B * S
TILES = NTOK // P
EPS = 1e-5

HEADS, HD = 16, 64
GROUP_TOK = 64
POS = GROUP_TOK * HEADS
PT = POS // P
TT = GROUP_TOK // PT
PAIRS = HEADS // 2
PARTS = 3
MROWS = PARTS * PT
KAUG = HD + MROWS


class Chain:

    def __init__(self, eng, sem, base=0):
        self.eng, self.sem, self.base, self.n = eng, sem, base, 0

    def __call__(self, ins):
        ins.then_inc(self.sem, 1)
        self.n += 1
        self.eng.wait_ge(self.sem, self.base + self.n)


def bc(ap, n):
    return ap.unsqueeze(len(ap.shape)).broadcast_to([*ap.shape, n])


def start_at_one(sp, *sems):
    for s in sems:
        sp.sem_inc(s, 1)


LN_CHUNKS = 4
CT = TILES // LN_CHUNKS


def layernorm_block(nc, tag, x, xT, half, ident, keep_norm, loads, xh=None, xl=None, splits=(), x_dram=None, rms_w=None):
    with ExitStack() as ctx:
        sb = lambda n, s, d=F32: ctx.enter_context(nc.sbuf_tensor(f"{tag}_{n}", s, d))
        sem = lambda n: ctx.enter_context(nc.semaphore(f"{tag}_{n}"))
        xn = sb("xn", [P, 2, CT, E])
        sq = sb("sq", [P, CT, E])
        st = sb("st", [P, 4, TILES])
        ps = ctx.enter_context(nc.psum_tensor(f"{tag}_ps", [P, 4, 512], F32))
        steps, var_ready, rstd_ready, norm_ready = sem("steps"), sem("var_ready"), sem("rstd_ready"), sem("norm_ready")
        turned, evicted, weights_loaded = sem("turned"), sem("evicted"), sem("weights_loaded")
        high_ready, low_ready = sem("high_ready"), sem("low_ready")
        x_loaded = [sem(f"x_loaded{c}") for c in range(LN_CHUNKS)]
        block = ctx.enter_context(nc.Block())
        rounds = 2 if rms_w is not None else 1
        outs = (xT,) if xh is None else (xT, xh)

        @block.sync
        def _(sp):
            if x_dram is not None:
                for c in range(LN_CHUNKS):
                    sl = slice(c * CT, (c + 1) * CT)
                    sp.dma_start(x[:, sl], x_dram.rearrange("(t p) e -> p t e", p=P)[:, sl]).then_inc(x_loaded[c], 16)
            for dst, src in loads:
                sp.dma_start(dst, src).then_inc(weights_loaded, 16)
            sp.wait_ge(weights_loaded, 16 * len(loads))

        @block.vector
        def _(dve):
            step = Chain(dve, steps)
            for c in range(LN_CHUNKS):
                if x_dram is not None:
                    dve.wait_ge(x_loaded[c], 16)
                if c >= 2:
                    dve.wait_ge(turned, (c - 1) * CT)
                xc = x[:, c * CT:(c + 1) * CT, :]
                y = xn[:, c % 2]
                s0, s1, s2, s3 = (st[:, k, c * CT:(c + 1) * CT] for k in range(4))
                step(dve.tensor_reduce(s0, xc, AX.X, ALU.add))
                step(dve.tensor_scalar(s0, s0, -1.0 / E, None, ALU.mult))
                step(dve.tensor_tensor(y, xc, bc(s0, E), ALU.add))
                for r in range(rounds):
                    step(dve.tensor_tensor(sq[:], y, y, ALU.mult))
                    step(dve.tensor_reduce(s1, sq[:], AX.X, ALU.add))
                    dve.tensor_scalar(s2, s1, 1.0 / E, EPS, ALU.mult, ALU.add).then_inc(var_ready, 1)
                    dve.wait_ge(rstd_ready, c * rounds + r + 1)
                    last = r == rounds - 1
                    ins = dve.tensor_tensor(y, y, bc(s3, E), ALU.mult)
                    if last:
                        ins.then_inc(norm_ready, 1)
                        dve.wait_ge(norm_ready, c + 1)
                    else:
                        step(ins)
                    if r == 0 and keep_norm:
                        step(dve.tensor_tensor(xc, xc, y, ALU.add))
            for z in (xh, xl) if xh is not None else ():
                dve.memset(z[:, NTOK:], 0.0).then_inc(low_ready, 1)
            for i, (w, high, low) in enumerate(splits):
                dve.wait_ge(high_ready, i + 1)
                dve.tensor_tensor(low, w, high, ALU.subtract).then_inc(low_ready, 1)
            for q in range(TILES // 4 if xl is not None else 0):
                dve.wait_ge(evicted, 2 * q + 2)
                sl = slice(q * 512, (q + 1) * 512)
                dve.tensor_tensor(xl[:, sl], xT[:, sl], xh[:, sl], ALU.subtract).then_inc(low_ready, 1)

        @block.gpsimd
        def _(pool):
            for c in range(LN_CHUNKS):
                for r in range(rounds):
                    pool.wait_ge(var_ready, c * rounds + r + 1)
                    sl = slice(c * CT, (c + 1) * CT)
                    pool.tensor_tensor(st[:, 3, sl], st[:, 2, sl], half[:, 0:CT], ALU.pow).then_inc(rstd_ready, 1)

        @block.tensor
        def _(pe):
            for c in range(LN_CHUNKS):
                pe.wait_ge(norm_ready, c + 1)
                for k in range(CT):
                    n = c * CT + k
                    if k % 4 == 0 and n >= 16:
                        pe.wait_ge(evicted, len(outs) * (n // 4 - 3))
                    pe.transpose(ps[:, (n // 4) % 4, (k % 4) * P:(k % 4 + 1) * P], xn[:, c % 2, k, :], ident[:]).then_inc(turned, 1)

        @block.scalar
        def _(act):
            if rms_w is not None:
                act.wait_ge(weights_loaded, 16 * len(loads))
            for q in range(TILES // 4):
                act.wait_ge(turned, 4 * q + 4)
                scale = 1.0 if rms_w is None else rms_w[:, 0:1]
                func = ACT.Copy if rms_w is None else ACT.Identity
                for dst in outs:
                    act.activation(dst[:, q * 512:(q + 1) * 512], ps[:, q % 4, :], func, scale=scale).then_inc(evicted, 1)
            act.wait_ge(weights_loaded, 16 * len(loads))
            for w, high, low in splits:
                act.activation(high, w, ACT.Copy).then_inc(high_ready, 1)


def attention_block(nc, xh, xl, wq, wk, wv, identb, mask_qk, mask_kq, row_mask, vd, od):
    with ExitStack() as ctx:
        sb = lambda n, s, d=F32: ctx.enter_context(nc.sbuf_tensor(f"at_{n}", s, d))
        sem = lambda n: ctx.enter_context(nc.semaphore(f"at_{n}"))
        pst = lambda n, s, d=F32: ctx.enter_context(nc.psum_tensor(f"at_{n}", s, d))
        xs = [sb(f"xs{k}", [P, P], BF16) for k in range(2)]
        high = sb("high", [P, 2, 2 * PT, PAIRS, TT], BF16)
        low = sb("low", [P, 2, 2 * PT, PAIRS, TT], BF16)
        q1 = sb("q1", [P, 4, PT, P], BF16)
        q2 = sb("q2", [P, 4, PT, P], BF16)
        k1 = sb("k1", [P, 4, PT, P], BF16)
        k2 = sb("k2", [P, 4, PT, P], BF16)
        vs = sb("vs", [P, HEADS, 2 * HD], BF16)
        vp = sb("vp", [P, 4, PT, 2 * HD + 2], BF16)
        rpart = sb("rpart", [P, 2, PT])
        rmax = sb("rmax", [P, PT])
        rest = sb("rest", [P, PT])
        mparts = sb("mparts", [P, PARTS, PT], BF16)
        prob = sb("prob", [P, PBUFS, PT * P])
        prob_h = sb("prob_h", [P, PBUFS, PT * P], BF16)
        prob_l = sb("prob_l", [P, PBUFS, PT * P], BF16)
        rden = sb("rden", [P, 4])
        outs = sb("outs", [P, 2, PT, HD])
        psP = pst("psP", [P, 1024])
        psM = pst("psM", [P, 1024])
        psS = pst("psS", [P, 1024])
        psO = pst("psO", [P, 2, 512])

        setup = sem("setup")
        xs_ready = sem("xs_ready")
        q_ps, k_ps, v_ps = sem("q_ps"), sem("k_ps"), sem("v_ps")
        q_high, k_high, v_out = sem("q_high"), sem("k_high"), sem("v_out")
        q_low, k_low = sem("q_low"), sem("k_low")
        packed = sem("packed")
        max_ps, reduced = sem("max_ps"), sem("reduced")
        max_split = sem("max_split")
        max_turned, max_rows = sem("max_turned"), sem("max_rows")
        score_ps, probs = sem("score_ps"), sem("probs")
        high_probs, low_probs, v_low = sem("high_probs"), sem("low_probs"), sem("v_low")
        pv_done = sem("pv_done")
        recip, out_ready = sem("recip"), sem("out_ready")
        o_stored = [[sem(f"o_stored{a}{b}") for b in range(2)] for a in range(2)]
        v_stored = sem("v_stored")
        v_loaded = [sem(f"v_loaded{a}") for a in range(2)]
        block = ctx.enter_context(nc.Block())

        SCORE_ORDER = [7, 6, 5, 4, 3, 2, 1, 0]
        MAX_ORDER = [7, 6, 5, 4, 0, 3, 2, 1]

        def pieces(order):
            cut = [(t, lo, min(t + 1, lo + 4)) for t in order for lo in range(0, t + 1, 4)]
            return {t: [(n, lo, hi) for n, (u, lo, hi) in enumerate(cut) if u == t] for t in order}

        SCORE_PIECES, MAX_PIECES = pieces(SCORE_ORDER), pieces(MAX_ORDER)
        PIECES = sum(len(v) for v in SCORE_PIECES.values())
        MAX_STEPS = {0: [3], 1: [2, 1], 4: [7], 5: [6], 6: [5], 7: [4, 0]}
        ROUNDS = TILES // 2

        PARTS_OF = ((0, 0), (0, 1), (1, 0))

        def project(pe, what, tile, rows=None):
            if what == "q":
                pe.wait_ge(xs_ready, 2 * tile + 2)
                if rows is not None:
                    pe.wait_ge(max_rows, rows)
                elif tile:
                    pe.wait_ge(v_low, tile)
            elif what == "k":
                pe.wait_ge(q_low, tile + 1)
            elif rows is not None:
                pe.wait_ge(max_rows, rows)
            else:
                pe.wait_ge(k_low, tile + 1)
            if what == "v":
                for h in range(2):
                    for a, b in PARTS_OF:
                        ins = pe.matmul(psP[:, h * 512:(h + 1) * 512], xs[a][:], wv[b][:, h * 512:(h + 1) * 512],
                                        start=a + b == 0, stop=a == 1)
            else:
                w = wq if what == "q" else wk
                for j in range(PAIRS):
                    for a, b in PARTS_OF:
                        ins = pe.matmul(psP[:, j * P:(j + 1) * P], w[a][:, j, :], xs[b][:], start=j % 4 == 0 and a + b == 0,
                                        stop=j % 4 == 3 and a == 1, skip_group_check=True)
            ins.then_inc({"q": q_ps, "k": k_ps, "v": v_ps}[what], 1)

        def max_pass(pe, slot, g, t):
            for n, lo, hi in MAX_PIECES[t]:
                pe.wait_ge(reduced, PIECES * g + n + 1)
                out = psM[:, n % 2 * 512:n % 2 * 512 + (hi - lo) * P]
                diag = hi == t + 1
                pe.matmul(out, q1[:, slot, t, :], k1[:, slot, lo:hi, :], start=True, stop=False, skip_group_check=True)
                ins = pe.matmul(out, q1[0:HD, slot, t, :], k2[0:HD, slot, lo:hi, :], start=False, stop=not diag,
                                skip_group_check=True)
                if diag:
                    ins = pe.matmul(out[:, (t - lo) * P:], identb, mask_qk, start=False, stop=True, skip_group_check=True)
                ins.then_inc(max_ps, 1)

        def turn_max(pe, g):
            pe.wait_ge(max_split, 5 * g + 5)
            pe.transpose(psP[0:MROWS, 0:P // 2].bitcast(BF16), mparts[:].rearrange("p a b -> p (a b)"),
                         identb).then_inc(max_turned, 1)

        def score_pass(pe, slot, g, i):
            t = SCORE_ORDER[i]
            if i == 0:
                pe.wait_ge(max_rows, g + 1)
            for n, lo, hi in SCORE_PIECES[t]:
                pe.wait_ge(probs, PIECES * g + n + 1)
                for j in range(lo, hi):
                    out = psS[:, n % 2 * 512 + (j - lo) * P:n % 2 * 512 + (j - lo + 1) * P]
                    pe.matmul(out, k1[:, slot, j, :], q1[:, slot, t, :], start=j == lo, stop=False, skip_group_check=True)
                    ins = pe.matmul(out, k2[0:KAUG, slot, j, :], q2[0:KAUG, slot, t, :], start=False, stop=j < t,
                                    skip_group_check=True)
                if hi == t + 1:
                    ins = pe.matmul(out, identb, mask_kq, start=False, stop=True, skip_group_check=True)
                ins.then_inc(score_ps, 1)

        def pv_pass(pe, slot, g, loads, i):
            t = PT - 1 - i
            pe.wait_ge(low_probs, PT * g + i + 1)
            if i == 0:
                pe.wait_ge(v_loaded[slot // 2], loads)
            if i % 4 == 0:
                pe.wait_ge(out_ready, 2 * g + i // 4 + 1)
            c = (t % 4) * (HD + 1)
            both, low = psO[:, t // 4, c:c + HD + 1], psO[:, t // 4, c:c + HD]
            for j in range(t + 1):
                ph, pl = (z[:, i % PBUFS, j * P:(j + 1) * P] for z in (prob_h, prob_l))
                v1, vl = vp[:, slot, j, HD:2 * HD + 1], vp[:, slot, j, 0:HD]
                pe.matmul(both, ph, v1, start=j == 0 and i % 4 == 0, stop=False, skip_group_check=True)
                pe.matmul(low, ph, vl, start=False, stop=False, skip_group_check=True)
                ins = pe.matmul(both, pl, v1, start=False, stop=j == t, skip_group_check=True)
            ins.then_inc(pv_done, 1)

        @block.tensor
        def _(pe):
            pe.wait_ge(setup, 3)
            for what in "qkv":
                project(pe, what, 0)
            for what in "qk":
                project(pe, what, 1)
            pe.wait_ge(packed, 2)
            for t in MAX_ORDER:
                max_pass(pe, 0, 0, t)
            pe.wait_ge(k_low, 2)
            turn_max(pe, 0)
            for i in range(4, PT):
                if i + LAG >= PT:
                    score_pass(pe, 0, 0, i + LAG - PT)
                for t in MAX_STEPS[i]:
                    max_pass(pe, 1, 1, t)
            with pe.Fori(0, ROUNDS) as r:
                for s in range(4):
                    g, tile = 4 * r + s, 2 * r + (s // 2 + 1)
                    for i in range(PT):
                        ahead = int(i + LAG >= PT)
                        score_pass(pe, (s + ahead) % 4, g + ahead, (i + LAG) % PT)
                        if i == 2:
                            pe.wait_ge((k_low, v_low)[s % 2], tile + 1)
                            turn_max(pe, g + 1)
                        if i == 4:
                            pe.wait_ge(packed, g + 3)
                        ahead = 1 + (i >= 4)
                        for t in MAX_STEPS.get(i, ()):
                            max_pass(pe, (s + ahead) % 4, g + ahead, t)
                        if s % 2 == 0 and i == 4:
                            project(pe, "v", tile, g + 2)
                        if s % 2 and i == 3:
                            project(pe, "q", tile + 1, g + 2)
                        if s % 2 and i == 5:
                            project(pe, "k", tile + 1)
                        pv_pass(pe, s, g, V_LOADS * (r + 1), i)

        def lower_part(dve, which, tile):
            dve.wait_ge((q_high, k_high)[which], tile + 1)
            src = psP[:].rearrange("p (j g x) -> p g j x", j=PAIRS, x=TT)
            dve.tensor_tensor(low[:, which], src, high[:, which], ALU.subtract).then_inc((q_low, k_low)[which], 1)

        def pack_half(slot):
            return slice((slot % 2) * PT, (slot % 2 + 1) * PT)

        def pack_q(dve, slot, *sides):
            for side in sides:
                for dst, rows, part in ((q1, 0, high), (q1, HD, low), (q2, 0, high)):
                    dve.tensor_copy(dst[rows:rows + HD, slot, :, side * HD:(side + 1) * HD],
                                    part[side * HD:(side + 1) * HD, 0, pack_half(slot)].rearrange("p g j x -> p g (j x)"))

        def pack_k(dve, slot):
            for dst, rows, part in ((k1, 0, high), (k1, HD, high), (k2, 0, low)):
                for side in range(2):
                    ins = dve.tensor_copy(dst[rows:rows + HD, slot, :, side * HD:(side + 1) * HD],
                                          part[side * HD:(side + 1) * HD, 1, pack_half(slot)].rearrange("p g j x -> p g (j x)"))
            ins.then_inc(packed, 1)

        def reduce_tile(dve, g, t):
            for n, lo, hi in MAX_PIECES[t]:
                dve.wait_ge(max_ps, PIECES * g + n + 1)
                dve.tensor_reduce(rpart[:, lo // 4, t:t + 1], psM[:, n % 2 * 512:n % 2 * 512 + (hi - lo) * P], AX.X,
                                  ALU.max).then_inc(reduced, 1)

        def split_max(dve, g):
            dve.wait_ge(reduced, PIECES * g + PIECES + 2)
            dve.tensor_tensor(rmax[:], rpart[:, 0, :], rpart[:, 1, :], ALU.max).then_inc(max_split, 1)
            dve.wait_ge(max_split, 5 * g + 1)
            if not isinstance(g, int):
                dve.wait_ge(max_turned, g)
            h, m, l = (mparts[:, k, :] for k in range(PARTS))
            dve.tensor_scalar(h, rmax[:], -1.0, None, ALU.mult).then_inc(max_split, 1)
            dve.wait_ge(max_split, 5 * g + 2)
            dve.scalar_tensor_tensor(rest[:], rmax[:], -1.0, h, ALU.mult, ALU.subtract).then_inc(max_split, 1)
            dve.wait_ge(max_split, 5 * g + 3)
            dve.tensor_copy(m, rest[:]).then_inc(max_split, 1)
            dve.wait_ge(max_split, 5 * g + 4)
            dve.tensor_tensor(l, rest[:], m, ALU.subtract).then_inc(max_split, 1)

        def place_max(dve, slot, g):
            dve.wait_ge(max_turned, g + 1)
            src = psP[0:MROWS, 0:P // 2].bitcast(BF16).unsqueeze(1).broadcast_to([MROWS, PT, P])
            dve.tensor_tensor(q2[HD:KAUG, slot], src, row_mask, ALU.mult).then_inc(max_rows, 1)

        def low_v(dve, tile):
            dve.wait_ge(v_out, tile + 1)
            dve.tensor_tensor(vs[:, :, 0:HD], psP[:].rearrange("p (i d) -> p i d", d=HD), vs[:, :, HD:2 * HD],
                              ALU.subtract).then_inc(v_low, 1)

        def normalise(dve, s, g, uses, n):
            h = 1 - n
            dve.wait_ge(pv_done, PT * g + 4 * n + 4 + PBUFS)
            dve.wait_ge(o_stored[s % 2][h], 64 * uses + 1)
            acc = psO[:, h, 0:4 * (HD + 1)].rearrange("p (t c) -> p t c", t=4)
            dve.reciprocal(rden[:], acc[:, :, HD]).then_inc(recip, 1)
            dve.wait_ge(recip, 2 * g + n + 1)
            dve.tensor_tensor(outs[:, s % 2, 4 * h:4 * h + 4, :], acc[:, :, 0:HD], bc(rden[:], HD), ALU.mult).then_inc(out_ready, 1)
            dve.wait_ge(out_ready, 2 * g + n + 3)

        @block.vector
        def _(dve):
            dve.wait_ge(setup, 3)
            lower_part(dve, 0, 0)
            lower_part(dve, 1, 0)
            dve.wait_ge(k_low, 1)
            for slot in range(2):
                pack_q(dve, slot, 0, 1)
                pack_k(dve, slot)
            low_v(dve, 0)
            lower_part(dve, 0, 1)
            dve.wait_ge(q_low, 2)
            pack_q(dve, 2, 0, 1)
            lower_part(dve, 1, 1)
            for t in MAX_ORDER:
                reduce_tile(dve, 0, t)
            split_max(dve, 0)
            place_max(dve, 0, 0)
            for i in range(4, PT):
                for t in MAX_STEPS[i]:
                    reduce_tile(dve, 1, t)
            with dve.Fori(0, ROUNDS) as r:
                for s in range(4):
                    g, tile = 4 * r + s, 2 * r + (s // 2 + 1)
                    for i in range(4):
                        for t in MAX_STEPS.get(i, ()):
                            reduce_tile(dve, g + 1, t)
                    split_max(dve, g + 1)
                    place_max(dve, (s + 1) % 4, g + 1)
                    dve.wait_ge(k_low, tile + 1)
                    pack_k(dve, (s + 2) % 4)
                    for i in range(4, PT):
                        for t in MAX_STEPS[i]:
                            reduce_tile(dve, g + 2, t)
                        if i == 4:
                            normalise(dve, s, g, 2 * r + s // 2, 0)
                            if s % 2:
                                lower_part(dve, 0, tile + 1)
                                dve.wait_ge(q_low, tile + 2)
                        if i in (5, 6):
                            pack_q(dve, (s + 3) % 4, i - 5)
                        if i == 7 and s % 2:
                            lower_part(dve, 1, tile + 1)
                        if i == 7 and s % 2 == 0:
                            low_v(dve, tile)
                    normalise(dve, s, g, 2 * r + s // 2, 1)

        def exp_tile(act, g, i):
            t = SCORE_ORDER[i]
            act.wait_ge(pv_done, PT * g + i + 1)
            for n, lo, hi in SCORE_PIECES[t]:
                act.wait_ge(score_ps, PIECES * g + n + 1)
                act.activation(prob[:, i % PBUFS, lo * P:hi * P], psS[:, n % 2 * 512:n % 2 * 512 + (hi - lo) * P], ACT.Exp,
                               scale=HD ** -0.5).then_inc(probs, 1)

        def high_prob(act, g, i):
            t = SCORE_ORDER[i]
            act.wait_ge(probs, PIECES * g + SCORE_PIECES[t][-1][0] + 3)
            act.activation(prob_h[:, i % PBUFS, 0:(t + 1) * P], prob[:, i % PBUFS, 0:(t + 1) * P], ACT.Copy).then_inc(high_probs, 1)

        def upper_part(act, which, tile, before=None):
            act.wait_ge((q_ps, k_ps)[which], tile + 1)
            if which == 0 and before is not None:
                act.wait_ge(packed, before)
            src = psP[:].rearrange("p (j g x) -> p g j x", j=PAIRS, x=TT)
            act.activation(high[:, which], src, ACT.Copy).then_inc((q_high, k_high)[which], 1)

        def v_to_sbuf(act, tile):
            act.wait_ge(v_ps, tile + 1)
            act.wait_ge(v_stored, 16 * tile)
            act.activation(vs[:, :, HD:2 * HD], psP[:].rearrange("p (i d) -> p i d", d=HD), ACT.Copy).then_inc(v_out, 1)
            for k in range(2):
                act.activation(xs[k][:], (xh, xl)[k][:, bass.ds((tile + 1) * P, P)], ACT.Copy).then_inc(xs_ready, 1)

        @block.scalar
        def _(act):
            for k in range(2):
                act.activation(xs[k][:], (xh, xl)[k][:, 0:P], ACT.Copy).then_inc(xs_ready, 1)
            upper_part(act, 0, 0)
            upper_part(act, 1, 0)
            v_to_sbuf(act, 0)
            upper_part(act, 0, 1, 2)
            upper_part(act, 1, 1)
            for i in range(LAG):
                exp_tile(act, 0, i)
                if i:
                    high_prob(act, 0, i - 1)
            with act.Fori(0, ROUNDS) as r:
                for s in range(4):
                    g, tile = 4 * r + s, 2 * r + (s // 2 + 1)
                    for i in range(PT):
                        ahead, ahead_high = int(i + LAG >= PT), int(i + LAG > PT)
                        exp_tile(act, g + ahead, (i + LAG) % PT)
                        high_prob(act, g + ahead_high, (i + LAG - 1) % PT)
                        if s % 2 and i in (4, 6):
                            upper_part(act, i // 6, tile + 1, g + 3)
                        if s % 2 == 0 and i == 5:
                            v_to_sbuf(act, tile)

        def turn_v(sp, slot, tile):
            sp.wait_ge(v_low, tile + 1)
            rows = vd[bass.ds(tile * P, P), :]
            sp.dma_start(rows, vs[:].rearrange("p i c -> p (i c)")).then_inc(v_stored, 16)
            sp.wait_ge(v_stored, 16 * tile + 16)
            for h in range(2):
                for t in range(PT):
                    src = vd[bass.ds(tile * P + (h * GROUP_TOK + t * TT), TT), :].rearrange("x (i d) -> i x d", i=HEADS)
                    sp.dma_start(vp[:, slot + h, t, 0:2 * HD], src).then_inc(v_loaded[slot // 2], 16)

        def store_outs(sp, s, g, n):
            h = 1 - n
            sp.wait_ge(out_ready, 2 * g + n + 3)
            for t in range(4 * h, 4 * h + 4):
                dst = od[bass.ds(g * GROUP_TOK + t * TT, TT), :].rearrange("x (i d) -> i x d", i=HEADS)
                sp.dma_start(dst, outs[:, s % 2, t, :]).then_inc(o_stored[s % 2][h], 16)

        @block.sync
        def _(sp):
            start_at_one(sp, *o_stored[0], *o_stored[1])
            sp.wait_ge(setup, 3)
            turn_v(sp, 0, 0)
            with sp.Fori(0, ROUNDS) as r:
                for s in range(4):
                    g, tile = 4 * r + s, 2 * r + (s // 2 + 1)
                    store_outs(sp, s, g, 0)
                    if s % 2 == 0:
                        turn_v(sp, (s + 2) % 4, tile)
                    store_outs(sp, s, g, 1)
            for a in range(2):
                for b in range(2):
                    sp.wait_ge(o_stored[a][b], 64 * 2 * ROUNDS + 1)
            for a in range(2):
                sp.wait_ge(v_loaded[a], V_LOADS * (ROUNDS + (a == 0)))

        @block.gpsimd
        def _(pool):
            pool.memset(k2[HD:KAUG], 1.0).then_inc(setup, 1)
            pool.wait_ge(setup, 1)
            pool.memset(vp[:, :, :, 2 * HD:2 * HD + 1], 1.0).then_inc(setup, 1)
            pool.wait_ge(setup, 2)
            pool.memset(rpart[:, 1, :], -3e38).then_inc(setup, 1)
            pool.sem_inc(reduced, 2)
            pool.sem_inc(probs, 2)
            pool.sem_inc(pv_done, PBUFS)
            pool.sem_inc(out_ready, 2)
            with pool.Fori(0, ROUNDS) as r:
                for s in range(4):
                    for i in range(PT):
                        n = (PT - i) * P
                        pool.wait_ge(high_probs, PT * (4 * r + s) + i + 1)
                        pool.tensor_tensor(prob_l[:, i % PBUFS, 0:n], prob[:, i % PBUFS, 0:n], prob_h[:, i % PBUFS, 0:n],
                                           ALU.subtract).then_inc(low_probs, 1)


PBUFS = 4
LAG = 3
V_LOADS = 2 * PT * 16


def projection_block(nc, x, wp, bias, od, ident):
    with ExitStack() as ctx:
        sb = lambda n, s, d=F32: ctx.enter_context(nc.sbuf_tensor(f"pr_{n}", s, d))
        sem = lambda n: ctx.enter_context(nc.semaphore(f"pr_{n}"))
        KC = HEADS * HD // P
        o = sb("o", [P, 2, KC, P])
        oT = sb("oT", [P, 2, KC, P])
        psT = ctx.enter_context(nc.psum_tensor("pr_psT", [P, 2, KC * P], F32))
        psY = ctx.enter_context(nc.psum_tensor("pr_psY", [P, 2, 512], F32))
        loaded = [sem("loaded0"), sem("loaded1")]
        turned, o_turned, y_ps, added, biased = sem("turned"), sem("o_turned"), sem("y_ps"), sem("added"), sem("biased")
        block = ctx.enter_context(nc.Block())
        ROUNDS = TILES // 2

        @block.sync
        def _(sp):
            start_at_one(sp, added, turned, y_ps)
            with sp.Fori(0, ROUNDS) as r:
                for s in range(2):
                    sp.wait_ge(turned, 2 * r + 1)
                    sp.dma_start(o[:, s], od[bass.ds((2 * r + s) * P, P), :].rearrange("p (k c) -> p k c", c=P)).then_inc(loaded[s], 16)
            for s in range(2):
                sp.wait_ge(loaded[s], 16 * ROUNDS)

        @block.tensor
        def _(pe):
            with pe.Fori(0, ROUNDS) as r:
                for s in range(2):
                    pe.wait_ge(loaded[s], 16 * r + 16)
                    for k in range(KC):
                        ins = pe.transpose(psT[:, s, k * P:(k + 1) * P], o[:, s, k, :], ident[:])
                    ins.then_inc(turned, 1)
                for s in range(2):
                    pe.wait_ge(o_turned, 2 * r + s + 1)
                    pe.wait_ge(added, 2 * r + 1)
                    for k in range(KC):
                        ins = pe.matmul(psY[:, s, 0:E], oT[:, s, k, :], wp[:, k, :], start=k == 0, stop=k == KC - 1)
                    ins.then_inc(y_ps, 1)

        @block.scalar
        def _(act):
            with act.Fori(0, ROUNDS) as r:
                for s in range(2):
                    act.wait_ge(turned, 2 * r + s + 2)
                    act.wait_ge(y_ps, 2 * r + 1)
                    act.activation(oT[:, s], psT[:, s, :], ACT.Copy).then_inc(o_turned, 1)

        @block.vector
        def _(dve):
            dve.tensor_tensor(x[:], x[:], bias.unsqueeze(1).broadcast_to([P, TILES, E]), ALU.add).then_inc(biased, 1)
            dve.wait_ge(biased, 1)
            with dve.Fori(0, ROUNDS) as r:
                for s in range(2):
                    dve.wait_ge(y_ps, 2 * r + s + 2)
                    xt = x[:, bass.ds(2 * r + s, 1), :]
                    dve.tensor_tensor(xt, xt, psY[:, s:s + 1, 0:E], ALU.add).then_inc(added, 1)


def rank_steps(step, dve, cnt, t, v, n, lower):
    sh = list(v.shape)[:-1]
    step(dve.tensor_copy(cnt, lower.unsqueeze(1).broadcast_to([*sh, n])))
    for d in range(1, n):
        ge = t[..., 0:n - d]
        step(dve.tensor_tensor(ge, v[..., 0:n - d], v[..., d:n], ALU.is_ge))
        step(dve.tensor_tensor(cnt[..., d:n], cnt[..., d:n], ge, ALU.add))
        step(dve.tensor_tensor(cnt[..., 0:n - d], cnt[..., 0:n - d], ge, ALU.subtract))


def split_parts(step, dve, parts, v, rest):
    step(dve.tensor_copy(parts[0], v))
    step(dve.tensor_tensor(rest, v, parts[0], ALU.subtract))
    step(dve.tensor_copy(parts[1], rest))
    step(dve.tensor_tensor(parts[2], rest, parts[1], ALU.subtract))


TB = 512
BLOCKS = NTOK // TB
BT = TB // P


def moe0_block(nc, x, xT, wgate, gbias, lower4, lower16, wg, wu, wd, sel, ident, identb):
    NE, TOPK, SCALE = 16, 4, 2.5
    NP_ = NE // 2
    NC = NP_ + 1
    with ExitStack() as ctx:
        sb = lambda n, s, d=F32: ctx.enter_context(nc.sbuf_tensor(f"m0_{n}", s, d))
        sem = lambda n: ctx.enter_context(nc.semaphore(f"m0_{n}"))
        cwT = sb("cwT", [PARTS * NE, NTOK], BF16)
        with ExitStack() as rc:
            rb = lambda n, s, d=F32: rc.enter_context(nc.sbuf_tensor(f"r0_{n}", s, d))
            scores, v, cnt, t = (rb(n, [P, TILES, NE]) for n in ("scores", "v", "cnt", "t"))
            pa, pb, pc, pd, gs, gcnt, gt = (rb(n, [P, TILES, 4]) for n in ("pa", "pb", "pc", "pd", "gs", "gcnt", "gt"))
            den = rb("den", [P, TILES])
            parts = rb("parts", [P, TILES, PARTS, NE], BF16)
            psL = rc.enter_context(nc.psum_tensor("r0_psL", [P, TILES, NE], F32))
            psW = rc.enter_context(nc.psum_tensor("r0_psW", [P, 4, 512], F32))
            logits, scored, steps, turned, evicted, parts_ready = (rc.enter_context(nc.semaphore(f"r0_{n}")) for n in (
                "logits", "scored", "steps", "turned", "evicted", "parts_ready"))
            block = rc.enter_context(nc.Block())

            @block.tensor
            def _(pe):
                for k in range(TILES):
                    ins = pe.matmul(psL[:, k, :], xT[:, k * P:(k + 1) * P], wgate[:], start=k == 0, stop=k == TILES - 1, skip_group_check=True)
                ins.then_inc(logits, 1)
                pe.wait_ge(parts_ready, 1)
                for k in range(TILES):
                    if k % 8 == 0 and k >= 32:
                        pe.wait_ge(evicted, k // 8 - 3)
                    out = psW[0:PARTS * NE, k // 8, :].bitcast(BF16)[:, (k % 8) * P:(k % 8 + 1) * P]
                    pe.transpose(out, parts[:, k].rearrange("p a b -> p (a b)"), identb).then_inc(turned, 1)

            @block.scalar
            def _(act):
                act.wait_ge(logits, 1)
                act.activation(scores[:], psL[:], ACT.Sigmoid).then_inc(scored, 1)
                for q in range(TILES // 8):
                    act.wait_ge(turned, 8 * q + 8)
                    act.activation(cwT[:, q * 1024:(q + 1) * 1024], psW[0:PARTS * NE, q, :].bitcast(BF16), ACT.Copy).then_inc(evicted, 1)

            @block.vector
            def _(dve):
                step = Chain(dve, steps)
                dve.wait_ge(scored, 1)
                step(dve.tensor_tensor(v[:], scores[:], gbias.unsqueeze(1).broadcast_to([P, TILES, NE]), ALU.add))
                v4 = v[:].rearrange("p t (g k) -> p t g k", k=4)
                step(dve.tensor_tensor(pa[:], v4[..., 0], v4[..., 1], ALU.max))
                step(dve.tensor_tensor(pb[:], v4[..., 0], v4[..., 1], ALU.min))
                step(dve.tensor_tensor(pc[:], v4[..., 2], v4[..., 3], ALU.max))
                step(dve.tensor_tensor(pd[:], v4[..., 2], v4[..., 3], ALU.min))
                step(dve.tensor_tensor(gs[:], pa[:], pc[:], ALU.add))
                step(dve.tensor_tensor(pb[:], pa[:], pb[:], ALU.add))
                step(dve.tensor_tensor(pd[:], pc[:], pd[:], ALU.add))
                step(dve.tensor_tensor(gs[:], gs[:], pb[:], ALU.max))
                step(dve.tensor_tensor(gs[:], gs[:], pd[:], ALU.max))
                rank_steps(step, dve, gcnt[:], gt[:], gs[:], 4, lower4)
                step(dve.tensor_scalar(gt[:], gcnt[:], 1.5, None, ALU.is_lt))
                step(dve.tensor_scalar(gt[:], gt[:], 1e30, -1e30, ALU.mult, ALU.add))
                step(dve.tensor_tensor(v4.rearrange("p t g k -> p (t g) k"), v4.rearrange("p t g k -> p (t g) k"),
                                       bc(gt[:].rearrange("p t g -> p (t g)"), 4), ALU.add))
                rank_steps(step, dve, cnt[:], t[:], v[:], NE, lower16)
                step(dve.tensor_scalar(cnt[:], cnt[:], TOPK - 0.5, None, ALU.is_lt))
                step(dve.tensor_tensor(v[:], scores[:], cnt[:], ALU.mult))
                step(dve.tensor_reduce(den[:], v[:], AX.X, ALU.add))
                step(dve.tensor_scalar(den[:], den[:], 1e-20, None, ALU.add))
                step(dve.reciprocal(den[:], den[:]))
                step(dve.tensor_scalar(den[:], den[:], SCALE, None, ALU.mult))
                step(dve.tensor_tensor(v[:], v[:], bc(den[:], NE), ALU.mult))
                split_parts(step, dve, [parts[:, :, k, :] for k in range(PARTS)], v[:], t[:])
                dve.sem_inc(parts_ready, 1)

        act_s = sb("silu", [P, 2, TB])
        prod = sb("prod", [P, TB])
        hid = sb("hid", [P, 2, TB])
        yT = sb("yT", [P, 2, TB])
        psG, psU, psC = (ctx.enter_context(nc.psum_tensor(f"m0_{n}", [P, 2, TB], F32)) for n in ("psG", "psU", "psC"))
        psY = ctx.enter_context(nc.psum_tensor("m0_psY", [P, TB], F32))
        psT = ctx.enter_context(nc.psum_tensor("m0_psT", [P, TB], F32))
        up_ps, silu_ready, prod_ready, hid_ready, y_ps, y_out, y_turned, added = (sem(n) for n in (
            "up_ps", "silu_ready", "prod_ready", "hid_ready", "y_ps", "y_out", "y_turned", "added"))
        block = ctx.enter_context(nc.Block())

        @block.sync
        def _(sp):
            start_at_one(sp, added, hid_ready, prod_ready, y_out, y_ps, y_turned)

        @block.tensor
        def _(pe):
            with pe.Fori(0, BLOCKS) as r:
                tok = xT[:, bass.ds(r * TB, TB)]
                for c in range(NC + 1):
                    if c < NC:
                        pe.wait_ge(hid_ready, NC * r + c) if c else pe.wait_ge(hid_ready, NC * r + 1)
                        pe.matmul(psG[:, c % 2, :], wg[:, c, :], tok, start=True, stop=True)
                        ins = pe.matmul(psU[:, c % 2, :], wu[:, c, :], tok, start=True, stop=True)
                        if c < NP_:
                            ins = pe.matmul(psC[:, c % 2, :], sel[:, c, :], cwT[:, bass.ds(r * TB, TB)], start=True, stop=True)
                        ins.then_inc(up_ps, 1)
                    if c == 0:
                        pe.wait_ge(y_out, r + 1)
                    else:
                        pe.wait_ge(hid_ready, NC * r + c + 1)
                        ins = pe.matmul(psY[:], wd[:, c - 1, :], hid[:, (c - 1) % 2, :], start=c == 1, stop=c == NC)
                        ins.then_inc(y_ps, 1)
                pe.wait_ge(y_out, r + 2)
                pe.wait_ge(added, r + 1)
                for k in range(BT):
                    ins = pe.transpose(psT[:, k * P:(k + 1) * P], yT[:, 0, k * P:(k + 1) * P], ident[:])
                ins.then_inc(y_turned, 1)

        @block.scalar
        def _(act):
            with act.Fori(0, BLOCKS) as r:
                for c in range(NC):
                    act.wait_ge(up_ps, NC * r + c + 1)
                    act.wait_ge(prod_ready, NC * r + c) if c else act.wait_ge(prod_ready, NC * r + 1)
                    act.activation(act_s[:, c % 2, :], psG[:, c % 2, :], ACT.Silu).then_inc(silu_ready, 1)
                act.wait_ge(y_ps, NC * r + NC + 1)
                act.wait_ge(y_turned, r + 1)
                act.activation(yT[:, 0, :], psY[:], ACT.Copy).then_inc(y_out, 1)

        @block.vector
        def _(dve):
            with dve.Fori(0, BLOCKS) as r:
                for c in range(NC):
                    n = NC * r + c
                    dve.wait_ge(silu_ready, n + 1)
                    if c < NP_:
                        dve.wait_ge(hid_ready, n + 1)
                        dve.tensor_tensor(prod[:], act_s[:, c % 2, :], psU[:, c % 2, :], ALU.mult).then_inc(prod_ready, 1)
                        dve.wait_ge(prod_ready, n + 2)
                        dve.wait_ge(y_ps, n) if c else dve.wait_ge(y_ps, n + 1)
                        dve.tensor_tensor(hid[:, c % 2, :], prod[:], psC[:, c % 2, :], ALU.mult).then_inc(hid_ready, 1)
                    else:
                        dve.wait_ge(y_ps, n)
                        dve.tensor_tensor(hid[:, c % 2, :], act_s[:, c % 2, :], psU[:, c % 2, :], ALU.mult).then_inc(hid_ready, 1)
                        dve.wait_ge(hid_ready, n + 2)
                        dve.sem_inc(prod_ready, 1)
                dve.wait_ge(y_turned, r + 2)
                xt = x[:, bass.ds(BT * r, BT), :]
                dve.tensor_tensor(xt, xt, psT[:].rearrange("p (t e) -> p t e", e=E), ALU.add).then_inc(added, 1)


MAMBA = ["skip_w", "in_w", "conv_w", "conv_b", "wdbc", "wd2", "wd2_b", "a_log", "w_d", "out_w", "sel32", "ident"]


def mamba_block(nc, x, xT, skip_w, in_w, conv_w, conv_b, wdbc, wd2, wd2_b, a_log, w_d, out_w, sel32, ident, passed):
    CH, NS, KW, RANK = 2, 16, 4, 64
    PAD = KW - 1
    with ExitStack() as ctx:
        sb = lambda n, s, d=F32: ctx.enter_context(nc.sbuf_tensor(f"mb_{n}", s, d))
        u = sb("u", [P, CH, NTOK])
        gate = sb("gate", [P, CH, NTOK])
        delta = sb("delta", [P, CH, NTOK])
        bcT = sb("bcT", [PARTS * 2 * NS, NTOK], BF16)
        aneg = sb("aneg", [P, CH, NS])

        with ExitStack() as c1:
            sb1 = lambda n, s, d=F32: c1.enter_context(nc.sbuf_tensor(f"mc_{n}", s, d))
            sem = lambda n: c1.enter_context(nc.semaphore(f"mc_{n}"))
            xin = sb1("xin", [P, CH, PAD + S])
            conv = sb1("conv", [P, 2, S])
            ps = c1.enter_context(nc.psum_tensor("mc_ps", [P, 2, CH, TB], F32))
            psi = c1.enter_context(nc.psum_tensor("mc_psi", [P, 2, CH, TB], F32))
            pads, skip_ps, gate_ready, in_ps, in_ready, taps, conv_ready, u_ready, a_exp = (sem(n) for n in (
                "pads", "skip_ps", "gate_ready", "in_ps", "in_ready", "taps", "conv_ready", "u_ready", "a_exp"))
            block = c1.enter_context(nc.Block())

            @block.sync
            def _(sp):
                start_at_one(sp, conv_ready, gate_ready, in_ready, u_ready)

            @block.tensor
            def _(pe):
                with pe.Fori(0, B) as b:
                    for h in range(2):
                        tok = xT[:, bass.ds(b * S + h * TB, TB)]
                        pe.wait_ge(in_ready, 2 * b + 1)
                        for c in range(CH):
                            ins = pe.matmul(psi[:, h, c, :], in_w[:, c * P:(c + 1) * P], tok, start=True, stop=True)
                        ins.then_inc(in_ps, 1)
                    for h in range(2):
                        tok = xT[:, bass.ds(b * S + h * TB, TB)]
                        pe.wait_ge(gate_ready, 2 * b + 1)
                        for c in range(CH):
                            ins = pe.matmul(ps[:, h, c, :], skip_w[:, c * P:(c + 1) * P], tok, start=True, stop=True)
                        ins.then_inc(skip_ps, 1)

            @block.scalar
            def _(act):
                act.wait_ge(pads, 1)
                with act.Fori(0, B) as b:
                    for h in range(2):
                        act.wait_ge(in_ps, 2 * b + h + 1)
                        act.wait_ge(conv_ready, 2 * b + 1)
                        act.activation(xin[:, :, PAD + h * TB:PAD + (h + 1) * TB], psi[:, h], ACT.Copy).then_inc(in_ready, 1)
                    for h in range(2):
                        act.wait_ge(skip_ps, 2 * b + h + 1)
                        act.sem_inc(passed, 1)
                        act.activation(gate[:, :, bass.ds(b * S + h * TB, TB)], ps[:, h], ACT.Silu).then_inc(gate_ready, 1)
                    for c in range(CH):
                        act.wait_ge(conv_ready, 2 * b + c + 2)
                        act.sem_inc(passed, 1)
                        act.activation(u[:, c, bass.ds(b * S, S)], conv[:, c, :], ACT.Silu, bias=conv_b[:, c, 0:1]).then_inc(u_ready, 1)
                act.activation(aneg[:], a_log, ACT.Exp).then_inc(a_exp, 1)

            @block.vector
            def _(dve):
                dve.memset(xin[:, :, 0:PAD], 0.0).then_inc(pads, 1)
                with dve.Fori(0, B) as b:
                    dve.wait_ge(in_ready, 2 * b + 3)
                    dve.wait_ge(u_ready, 2 * b + 1)
                    for k in range(KW):
                        for c in range(CH):
                            src, w, out = xin[:, c, k:k + S], conv_w[:, c, k:k + 1], conv[:, c, :]
                            if k == 0:
                                ins = dve.tensor_scalar(out, src, w, None, ALU.mult)
                            else:
                                dve.wait_ge(taps, 6 * b + 2 * (k - 1) + c + 1)
                                ins = dve.scalar_tensor_tensor(out, src, w, out, ALU.mult, ALU.add)
                            ins.then_inc(conv_ready if k == KW - 1 else taps, 1)
                dve.wait_ge(a_exp, 1)
                dve.tensor_scalar(aneg[:], aneg[:], -1.0, None, ALU.mult).then_inc(a_exp, 1)
                dve.wait_ge(a_exp, 2)

        with ExitStack() as c2:
            sb2 = lambda n, s, d=F32: c2.enter_context(nc.sbuf_tensor(f"md_{n}", s, d))
            sem = lambda n: c2.enter_context(nc.semaphore(f"md_{n}"))
            z1 = sb2("z1", [RANK, 2, TB])
            pos, mag = sb2("pos", [P, 2, CH, TB]), sb2("mag", [P, 2, CH, TB])
            middle, rest = sb2("middle", [2 * NS, TB], BF16), sb2("rest", [2 * NS, TB])
            psA = c2.enter_context(nc.psum_tensor("md_psA", [P, TB], F32))
            psZ = c2.enter_context(nc.psum_tensor("md_psZ", [P, 2, CH, TB], F32))
            z1_ps, z1_ready, bc_steps, z2_ps, mag_ready, pos_ready, exp_ready, log_ready, delta_ready = (sem(n) for n in (
                "z1_ps", "z1_ready", "bc_steps", "z2_ps", "mag_ready", "pos_ready", "exp_ready", "log_ready", "delta_ready"))
            block = c2.enter_context(nc.Block())

            @block.sync
            def _(sp):
                start_at_one(sp, bc_steps, delta_ready, pos_ready, z1_ready, z2_ps)

            @block.tensor
            def _(pe):
                with pe.Fori(0, BLOCKS // 2) as r:
                    for s in range(2):
                        n = 2 * r + s
                        pe.wait_ge(z1_ready, n + 1)
                        pe.wait_ge(bc_steps, 4 * n + 1)
                        for c in range(CH):
                            ins = pe.matmul(psA[0:RANK + 2 * NS, :], wdbc[:, c, :], u[:, c, bass.ds(n * TB, TB)], start=c == 0, stop=c == CH - 1)
                        ins.then_inc(z1_ps, 1)
                        pe.wait_ge(z1_ready, n + 2)
                        pe.wait_ge(pos_ready, 2 * r + 1)
                        for c in range(CH):
                            ins = pe.matmul(psZ[:, s, c, :], wd2[:, c * P:(c + 1) * P], z1[:, s, :], start=True, stop=True)
                        ins.then_inc(z2_ps, 1)

            @block.scalar
            def _(act):
                with act.Fori(0, BLOCKS // 2) as r:
                    for s in range(2):
                        n = 2 * r + s
                        act.wait_ge(z1_ps, n + 1)
                        act.wait_ge(z2_ps, 2 * r + 1)
                        act.activation(z1[:, s, :], psA[0:RANK, :], ACT.Copy).then_inc(z1_ready, 1)
                        act.wait_ge(mag_ready, n + 1)
                        act.activation(mag[:, s], mag[:, s], ACT.Exp, scale=-1.0).then_inc(exp_ready, 1)
                        act.wait_ge(exp_ready, n + 1)
                        act.activation(mag[:, s], mag[:, s], ACT.Ln, bias=1.0).then_inc(log_ready, 1)

            @block.vector
            def _(dve):
                with dve.Fori(0, BLOCKS // 2) as r:
                    for s in range(2):
                        n = 2 * r + s
                        dve.wait_ge(z2_ps, n + 2)
                        for c in range(CH):
                            dve.wait_ge(delta_ready, 2 * r + 1)
                            dve.tensor_scalar(mag[:, s, c, :], psZ[:, s, c, :], wd2_b[:, c, 0:1], 0.0, ALU.add, ALU.min)
                        for c in range(CH):
                            ins = dve.tensor_scalar(pos[:, s, c, :], psZ[:, s, c, :], wd2_b[:, c, 0:1], 0.0, ALU.add, ALU.max)
                        ins.then_inc(pos_ready, 1)
                        dve.wait_ge(pos_ready, n + 2)
                        dve.tensor_tensor(mag[:, s], pos[:, s], mag[:, s], ALU.subtract).then_inc(mag_ready, 1)
                        dve.wait_ge(z1_ps, n + 1)
                        part = [bcT[k * 2 * NS:(k + 1) * 2 * NS, bass.ds(n * TB, TB)] for k in range(PARTS)]
                        dve.tensor_copy(part[0], psA[RANK:RANK + 2 * NS, :]).then_inc(bc_steps, 1)
                        dve.wait_ge(bc_steps, 4 * n + 2)
                        dve.tensor_tensor(rest[:], psA[RANK:RANK + 2 * NS, :], part[0], ALU.subtract).then_inc(bc_steps, 1)
                        dve.wait_ge(bc_steps, 4 * n + 3)
                        dve.tensor_copy(middle[:], rest[:]).then_inc(bc_steps, 1)
                        dve.wait_ge(bc_steps, 4 * n + 4)
                        dve.tensor_copy(part[1], middle[:])
                        dve.tensor_tensor(part[2], rest[:], middle[:], ALU.subtract).then_inc(bc_steps, 1)
                        dve.wait_ge(bc_steps, 4 * n + 5)
                        dve.wait_ge(log_ready, n + 1)
                        dve.tensor_tensor(delta[:, :, bass.ds(n * TB, TB)], pos[:, s], mag[:, s], ALU.add).then_inc(delta_ready, 1)


        with ExitStack() as c3:
            sb3 = lambda n, s, d=F32: c3.enter_context(nc.sbuf_tensor(f"ms_{n}", s, d))
            sem = lambda n: c3.enter_context(nc.semaphore(f"ms_{n}"))
            du = sb3("du", [P, CH, S])
            decay, inject, state, part_y = (sb3(n, [P, 2, S]) for n in ("decay", "inject", "state", "part_y"))
            y = sb3("y", [P, CH, S])
            psB = c3.enter_context(nc.psum_tensor("ms_psB", [P, 2, S], F32))
            psC = c3.enter_context(nc.psum_tensor("ms_psC", [P, 2, S], F32))
            bc_ready, du_ready, decay_ready, inject_ready, state_ready, read_out, summed, ends = (sem(n) for n in (
                "bc_ready", "du_ready", "decay_ready", "inject_ready", "state_ready", "read_out", "summed", "ends"))
            block = c3.enter_context(nc.Block())

            @block.sync
            def _(sp):
                start_at_one(sp, read_out, state_ready, summed)
            UNITS = CH * NS

            @block.tensor
            def _(pe):
                with pe.Fori(0, B) as b:
                    for n in range(NS):
                        pe.wait_ge(read_out, UNITS * b + max(0, CH * (n - 1)) + 1)
                        for bank, row in ((psB, n), (psC, NS + n)):
                            for h in range(2):
                                ins = pe.matmul(bank[:, n % 2, h * TB:(h + 1) * TB], sel32[:, row, :],
                                                bcT[:, bass.ds(b * S + h * TB, TB)], start=True, stop=True)
                        ins.then_inc(bc_ready, 1)

            @block.scalar
            def _(act):
                with act.Fori(0, B) as b:
                    for w in range(UNITS):
                        n, c = w // CH, w % CH
                        act.wait_ge(state_ready, UNITS * b + max(0, w - 1) + 1)
                        act.sem_inc(passed, 1)
                        act.activation(decay[:, w % 2, :], delta[:, c, bass.ds(b * S, S)], ACT.Exp,
                                       scale=aneg[:, c, n:n + 1]).then_inc(decay_ready, 1)

            @block.vector
            def _(dve):
                with dve.Fori(0, B) as b:
                    seq = bass.ds(b * S, S)
                    base = UNITS * b
                    dve.tensor_tensor(du[:], delta[:, :, seq], u[:, :, seq], ALU.mult).then_inc(du_ready, 1)
                    dve.wait_ge(du_ready, b + 1)
                    for i in range(UNITS + 2):
                        w = i
                        if w < UNITS:
                            n, c = w // CH, w % CH
                            if c == 0:
                                dve.wait_ge(bc_ready, NS * b + n + 1)
                            dve.wait_ge(state_ready, base + max(0, w - 1) + 1)
                            dve.tensor_tensor(inject[:, w % 2, :], du[:, c, :], psB[:, n % 2, :], ALU.mult).then_inc(inject_ready, 1)
                        w = i - 1
                        if 0 <= w < UNITS:
                            dve.wait_ge(inject_ready, base + w + 1)
                            dve.wait_ge(decay_ready, base + w + 1)
                            dve.wait_ge(read_out, base + max(0, w - 1) + 1)
                            dve.tensor_tensor_scan(state[:, w % 2, :], decay[:, w % 2, :], inject[:, w % 2, :], 0.0,
                                                   ALU.mult, ALU.add).then_inc(state_ready, 1)
                        w = i - 2
                        if 0 <= w:
                            n, c = w // CH, w % CH
                            dve.wait_ge(state_ready, base + w + 2)
                            if n:
                                dve.wait_ge(summed, (UNITS - CH) * b + max(0, w - CH - 1) + 1)
                            out = part_y[:, w % 2, :] if n else y[:, c, :]
                            dve.tensor_tensor(out, state[:, w % 2, :], psC[:, n % 2, :], ALU.mult).then_inc(read_out, 1)
                    dve.wait_ge(summed, (UNITS - CH) * b + UNITS - CH + 1)
                    for c in range(CH):
                        dve.scalar_tensor_tensor(y[:, c, :], u[:, c, seq], w_d[:, c, 0:1], y[:, c, :], ALU.mult, ALU.add).then_inc(ends, 1)
                    dve.wait_ge(ends, 3 * b + 2)
                    dve.tensor_tensor(u[:, :, seq], y[:], gate[:, :, seq], ALU.mult).then_inc(ends, 1)
                    dve.wait_ge(ends, 3 * b + 3)

            @block.gpsimd
            def _(pool):
                with pool.Fori(0, B) as b:
                    for w in range(CH, UNITS):
                        pool.wait_ge(read_out, UNITS * b + w + 2)
                        pool.wait_ge(summed, (UNITS - CH) * b + max(0, w - CH - 1) + 1)
                        pool.tensor_tensor(y[:, w % CH, :], y[:, w % CH, :], part_y[:, w % 2, :], ALU.add).then_inc(summed, 1)

        with ExitStack() as c4:
            sem = lambda n: c4.enter_context(nc.semaphore(f"mo_{n}"))
            yT = c4.enter_context(nc.sbuf_tensor("mo_yT", [P, 2, TB], F32))
            psY = c4.enter_context(nc.psum_tensor("mo_psY", [P, 2, TB], F32))
            psT = c4.enter_context(nc.psum_tensor("mo_psT", [P, 2, TB], F32))
            y_ps, y_out, y_turned, added = (sem(n) for n in ("y_ps", "y_out", "y_turned", "added"))
            block = c4.enter_context(nc.Block())

            @block.sync
            def _(sp):
                start_at_one(sp, added, y_out, y_turned)

            @block.tensor
            def _(pe):
                with pe.Fori(0, BLOCKS // 2) as r:
                    for s in range(2):
                        pe.wait_ge(y_out, 2 * r + 1)
                        for c in range(CH):
                            ins = pe.matmul(psY[:, s, :], out_w[:, c, :], u[:, c, bass.ds((2 * r + s) * TB, TB)], start=c == 0, stop=c == CH - 1)
                        ins.then_inc(y_ps, 1)
                    for s in range(2):
                        pe.wait_ge(y_out, 2 * r + s + 2)
                        pe.wait_ge(added, 2 * r + 1)
                        for k in range(BT):
                            ins = pe.transpose(psT[:, s, k * P:(k + 1) * P], yT[:, s, k * P:(k + 1) * P], ident[:])
                        ins.then_inc(y_turned, 1)

            @block.scalar
            def _(act):
                with act.Fori(0, BLOCKS // 2) as r:
                    for s in range(2):
                        act.wait_ge(y_ps, 2 * r + s + 1)
                        act.wait_ge(y_turned, 2 * r + 1)
                        act.activation(yT[:, s, :], psY[:, s, :], ACT.Copy).then_inc(y_out, 1)

            @block.vector
            def _(dve):
                with dve.Fori(0, BLOCKS // 2) as r:
                    for s in range(2):
                        dve.wait_ge(y_turned, 2 * r + s + 2)
                        xt = x[:, bass.ds(BT * (2 * r + s), BT), :]
                        dve.tensor_tensor(xt, xt, psT[:, s, :].rearrange("p (t e) -> p t e", e=E), ALU.add).then_inc(added, 1)


MOE1 = ["wr", "br", "lower8", "w1", "b1", "w2", "b2", "sel8", "ident", "identb"]


def moe1_block(nc, x, xT, wr, br, lower8, w1, b1, w2, b2, sel8, ident, identb):
    NE, NC = 8, 32
    with ExitStack() as ctx:
        sb = lambda n, s, d=F32: ctx.enter_context(nc.sbuf_tensor(f"m1_{n}", s, d))
        sem = lambda n: ctx.enter_context(nc.semaphore(f"m1_{n}"))
        hotT = sb("hotT", [NE, NTOK], BF16)
        hotF = sb("hotF", [NE, NTOK])
        with ExitStack() as rc:
            rb = lambda n, s, d=F32: rc.enter_context(nc.sbuf_tensor(f"r1_{n}", s, d))
            v, cnt, t = (rb(n, [P, TILES, NE]) for n in ("v", "cnt", "t"))
            psL = rc.enter_context(nc.psum_tensor("r1_psL", [P, TILES, NE], F32))
            psW = rc.enter_context(nc.psum_tensor("r1_psW", [P, 4, 512], F32))
            logits, steps, turned, evicted, hot_ready = (rc.enter_context(nc.semaphore(f"r1_{n}")) for n in (
                "logits", "steps", "turned", "evicted", "hot_ready"))
            block = rc.enter_context(nc.Block())

            @block.tensor
            def _(pe):
                for k in range(TILES):
                    ins = pe.matmul(psL[:, k, :], xT[:, k * P:(k + 1) * P], wr[:], start=k == 0, stop=k == TILES - 1, skip_group_check=True)
                ins.then_inc(logits, 1)
                pe.wait_ge(hot_ready, 1)
                for k in range(TILES):
                    if k % 4 == 0 and k >= 16:
                        pe.wait_ge(evicted, 2 * (k // 4 - 3))
                    pe.transpose(psW[0:NE, (k // 4) % 4, (k % 4) * P:(k % 4 + 1) * P], v[:, k, :], ident[:]).then_inc(turned, 1)

            @block.scalar
            def _(act):
                for q in range(TILES // 4):
                    act.wait_ge(turned, 4 * q + 4)
                    src = psW[0:NE, q % 4, :]
                    act.activation(hotT[:, q * 512:(q + 1) * 512], src, ACT.Copy).then_inc(evicted, 1)
                    act.activation(hotF[:, q * 512:(q + 1) * 512], src, ACT.Copy).then_inc(evicted, 1)

            @block.vector
            def _(dve):
                step = Chain(dve, steps)
                dve.wait_ge(logits, 1)
                step(dve.tensor_tensor(v[:], psL[:], br.unsqueeze(1).broadcast_to([P, TILES, NE]), ALU.add))
                rank_steps(step, dve, cnt[:], t[:], v[:], NE, lower8)
                step(dve.tensor_scalar(v[:], cnt[:], 0.5, None, ALU.is_lt))
                dve.sem_inc(hot_ready, 1)

        g = sb("g", [P, 3, TB])
        hid = sb("hid", [P, 2, TB])
        yT = sb("yT", [P, TB])
        psH = ctx.enter_context(nc.psum_tensor("m1_psH", [P, 2, TB], F32))
        psC = ctx.enter_context(nc.psum_tensor("m1_psC", [P, 2, TB], F32))
        psY = ctx.enter_context(nc.psum_tensor("m1_psY", [P, TB], F32))
        psT = ctx.enter_context(nc.psum_tensor("m1_psT", [P, TB], F32))
        h_ps, gelu_ready, hid_ready, y_ps, y_out, y_turned, added = (sem(n) for n in (
            "h_ps", "gelu_ready", "hid_ready", "y_ps", "y_out", "y_turned", "added"))
        block = ctx.enter_context(nc.Block())

        @block.sync
        def _(sp):
            start_at_one(sp, added, gelu_ready, hid_ready, y_out, y_ps, y_turned)
        LAG = 2

        @block.tensor
        def _(pe):
            with pe.Fori(0, BLOCKS) as r:
                sl = bass.ds(r * TB, TB)
                for i in range(NC + LAG):
                    c = i
                    if c < NC:
                        pe.wait_ge(gelu_ready, NC * r + max(0, c - 1) + 1)
                        if c % 4 == 0:
                            pe.wait_ge(hid_ready, NC * r + max(0, c - 4) + 1)
                        ins = pe.matmul(psH[:, c % 2, :], w1[:, c * P:(c + 1) * P], xT[:, sl], start=True, stop=True)
                        if c % 4 == 0:
                            ins = pe.matmul(psC[:, (c // 4) % 2, :], sel8[:, c // 4, :], hotT[:, sl], start=True, stop=True)
                        ins.then_inc(h_ps, 1)
                    c = i - LAG
                    if c == 0:
                        pe.wait_ge(y_out, r + 1)
                    if c >= 0:
                        pe.wait_ge(hid_ready, NC * r + c + 2)
                        ins = pe.matmul(psY[:], w2[:, c, :], hid[:, c % 2, :], start=c == 0, stop=c == NC - 1)
                        ins.then_inc(y_ps, 1)
                    if c == 0:
                        pe.matmul(psY[:], b2[:], hotF[:, sl], start=False, stop=False)
                pe.wait_ge(y_out, r + 2)
                pe.wait_ge(added, r + 1)
                for k in range(BT):
                    ins = pe.transpose(psT[:, k * P:(k + 1) * P], yT[:, k * P:(k + 1) * P], ident[:])
                ins.then_inc(y_turned, 1)

        @block.scalar
        def _(act):
            with act.Fori(0, BLOCKS) as r:
                for c in range(NC):
                    act.wait_ge(h_ps, NC * r + c + 1)
                    act.wait_ge(hid_ready, NC * r + max(0, c - 2) + 1)
                    act.activation(g[:, c % 3, :], psH[:, c % 2, :], ACT.Gelu, bias=b1[:, c:c + 1]).then_inc(gelu_ready, 1)
                act.wait_ge(y_ps, NC * r + NC + 1)
                act.wait_ge(y_turned, r + 1)
                act.activation(yT[:], psY[:], ACT.Copy).then_inc(y_out, 1)

        @block.vector
        def _(dve):
            with dve.Fori(0, BLOCKS) as r:
                for c in range(NC):
                    dve.wait_ge(gelu_ready, NC * r + c + 2)
                    dve.wait_ge(y_ps, NC * r + max(0, c - 1) + 1)
                    dve.tensor_tensor(hid[:, c % 2, :], g[:, c % 3, :], psC[:, (c // 4) % 2, :], ALU.mult).then_inc(hid_ready, 1)
                dve.wait_ge(y_turned, r + 2)
                xt = x[:, bass.ds(BT * r, BT), :]
                dve.tensor_tensor(xt, xt, psT[:].rearrange("p (t e) -> p t e", e=E), ALU.add).then_inc(added, 1)


def four_layers(nc, a, out):
    with ExitStack() as ctx:
        sb = lambda n, s, d=F32: ctx.enter_context(nc.sbuf_tensor(n, s, d))
        x = sb("x", [P, TILES, E])
        xT = sb("xT", [P, NTOK])
        ident = sb("ident", [P, P])
        identb = sb("identb", [P, P], BF16)
        half = sb("half", [P, CT])
        vd = nc.dram_tensor("v_by_token", [NTOK + P, HEADS * 2 * HD], BF16).ap()
        od = nc.dram_tensor("heads_out", [NTOK, HEADS * HD], F32).ap()
        const_ready = ctx.enter_context(nc.semaphore("const_ready"))
        const_loaded = ctx.enter_context(nc.semaphore("const_loaded"))
        passed = ctx.enter_context(nc.semaphore("act_passed"))
        stored = ctx.enter_context(nc.semaphore("stored"))

        with nc.Block() as block:
            @block.sync
            def _(sp):
                sp.dma_start(ident[:], a["ident"]).then_inc(const_loaded, 16)
                sp.dma_start(identb[:], a["identb"]).then_inc(const_loaded, 16)
                sp.wait_ge(const_loaded, 32)

            @block.vector
            def _(dve):
                dve.memset(half[:], -0.5).then_inc(const_ready, 1)
                dve.wait_ge(const_ready, 1)

        def weights(c, names):
            held = {n: c.enter_context(nc.sbuf_tensor(f"w_{n}", list(a[n].shape), a[n].dtype))[:] for n in names}
            return held, [(held[n], a[n]) for n in names]

        def cut(c, w, names):
            parts = {n: [c.enter_context(nc.sbuf_tensor(f"w_{n}{k}", list(a[n].shape), BF16))[:] for k in "hl"] for n in names}
            return parts, [(w[n], *parts[n]) for n in names]

        with ExitStack() as c:
            w, loads = weights(c, ["wq", "wk", "wv", "mask_qk", "mask_kq", "row_mask", "wp", "bp"])
            p, splits = cut(c, w, ["wq", "wk", "wv"])
            xh, xl = (c.enter_context(nc.sbuf_tensor(n, [P, NTOK + 2 * P], BF16)) for n in ("xh", "xl"))
            layernorm_block(nc, "ln0", x, xT, half, ident, False, loads, xh, xl, splits, x_dram=a["L0_attn_x"])
            attention_block(nc, xh, xl, p["wq"], p["wk"], p["wv"], identb[:], w["mask_qk"], w["mask_kq"], w["row_mask"], vd, od)
            projection_block(nc, x, w["wp"], w["bp"], od, ident)
        with ExitStack() as c:
            names = ["wgate", "gbias", "lower4", "lower16", "wg", "wu", "wd", "sel"]
            w, loads = weights(c, names)
            layernorm_block(nc, "ln1", x, xT, half, ident, True, loads)
            moe0_block(nc, x, xT, *[w[n] for n in names], ident, identb[:])
        with ExitStack() as c:
            names = [n for n in MAMBA if n != "ident"]
            w, loads = weights(c, names + ["norm_w"])
            layernorm_block(nc, "ln2", x, xT, half, ident, True, loads, rms_w=w["norm_w"])
            mamba_block(nc, x, xT, *[w[n] for n in names], ident, passed)
        with ExitStack() as c:
            names = [n for n in MOE1 if n not in ("ident", "identb")]
            w, loads = weights(c, names)
            layernorm_block(nc, "ln3", x, xT, half, ident, False, loads)
            moe1_block(nc, x, xT, *[w[n] for n in names], ident, identb[:])

        with nc.Block() as block:
            @block.sync
            def _(sp):
                sp.dma_start(out.rearrange("(t p) e -> p t e", p=P), x[:]).then_inc(stored, 16)
                sp.wait_ge(stored, 16)


def host_constants():
    bf16 = np.dtype("bfloat16")
    c = {"ident": np.eye(P, dtype=np.float32), "identb": np.eye(P, dtype=np.float32).astype(bf16)}
    at = np.arange(P) % TT * HEADS + np.arange(P) // TT
    mask = np.where(at[None, :] <= at[:, None], 0.0, -1e30).astype(bf16)
    c["mask_qk"], c["mask_kq"] = mask, np.ascontiguousarray(mask.T)
    rows = np.zeros((MROWS, PT, P), np.float32)
    for r in range(MROWS):
        rows[r, r % PT] = 1
    c["row_mask"] = rows.astype(bf16)
    for n in (4, 8, 16):
        c[f"lower{n}"] = np.tile(np.arange(n - 1, -1, -1, dtype=np.float32), (P, 1))
    sel = np.zeros((3, 16, 8, P), np.float32)
    for e in range(16):
        sel[:, e, e // 2, (e % 2) * 64:(e % 2 + 1) * 64] = 1
    c["sel"] = sel.reshape(48, 8, P).astype(bf16)
    sel = np.zeros((8, 8, P), np.float32)
    for e in range(8):
        sel[e, e] = 1
    c["sel8"] = sel.astype(bf16)
    sel = np.zeros((3, 32, 32, P), np.float32)
    for e in range(32):
        sel[:, e, e] = 1
    c["sel32"] = sel.reshape(96, 32, P).astype(bf16)
    return c


def host_weights(d):
    ca = np.ascontiguousarray
    pair = lambda w: ca(np.stack([np.concatenate([w[j], w[j + PAIRS]], 1) for j in range(PAIRS)], 1))
    w = {"wq": pair(d["L0_attn_Wq"]), "wk": pair(d["L0_attn_Wk"]),
         "wv": ca(d["L0_attn_Wv"].transpose(1, 0, 2).reshape(E, HEADS * HD)),
         "wp": ca(d["L0_attn_proj_w"].T.reshape(8, P, E).transpose(1, 0, 2)),
         "bp": ca(np.broadcast_to(d["L0_attn_proj_b"], (P, E)))}
    w["wgate"] = ca(d["L0_ffn_gate_w"].T)
    w["gbias"] = ca(np.broadcast_to(d["L0_ffn_gate_bias"], (P, 16)))
    up = lambda we, ws: ca(np.concatenate([we.reshape(1024, E), ws]).reshape(9, P, E).transpose(2, 0, 1))
    w["wg"], w["wu"] = up(d["L0_ffn_Wg"], d["L0_ffn_Ws_g"]), up(d["L0_ffn_Wu"], d["L0_ffn_Ws_u"])
    w["wd"] = ca(np.concatenate([d["L0_ffn_Wd"].transpose(0, 2, 1).reshape(1024, E), d["L0_ffn_Ws_d"].T]).reshape(9, P, E).transpose(1, 0, 2))
    chan = lambda a: ca(a.reshape(2, P, -1).transpose(1, 0, 2))
    w["norm_w"] = ca(d["L1_attn_norm_w"].reshape(P, 1))
    w["skip_w"], w["in_w"] = ca(d["L1_attn_skip_w"].T), ca(d["L1_attn_in_w"].T)
    w["conv_w"], w["conv_b"] = chan(d["L1_attn_conv_w"]), chan(d["L1_attn_conv_b"])
    w["wdbc"] = chan(np.concatenate([d["L1_attn_wd1"], d["L1_attn_wb"], d["L1_attn_wc"]]).T)
    w["wd2"], w["wd2_b"] = ca(d["L1_attn_wd2"].T), chan(d["L1_attn_wd2_b"])
    w["a_log"], w["w_d"] = chan(d["L1_attn_A_log"]), chan(d["L1_attn_W_D"])
    w["out_w"] = chan(d["L1_attn_out_w"].T)
    w["wr"], w["br"] = ca(d["L1_ffn_wr"]), ca(np.broadcast_to(d["L1_ffn_br"], (P, 8)))
    w["w1"] = ca(d["L1_ffn_w1"].transpose(1, 0, 2).reshape(E, 4096))
    w["b1"] = ca(d["L1_ffn_b1"].reshape(32, P).T)
    w["w2"] = ca(d["L1_ffn_w2"].reshape(32, P, E).transpose(1, 0, 2))
    w["b2"] = ca(d["L1_ffn_b2"])
    return w


def kernel(**inputs):
    import concourse.bacc as bacc
    from concourse.bass_utils import run_bass_kernel_spmd

    data = {n: np.asarray(v) for n, v in inputs.items()}
    arrays = {**host_constants(), **host_weights(data)}
    arrays["L0_attn_x"] = np.ascontiguousarray(data["L0_attn_x"].reshape(NTOK, E))
    nc = bacc.Bacc("TRN2", target_bir_lowering=False, num_devices=1)
    arrays = {f"in_{n}": v for n, v in arrays.items()}
    aps = {n[3:]: nc.dram_tensor(n, v.shape, mybir.dt.from_np(v.dtype), kind="ExternalInput").ap() for n, v in arrays.items()}
    out = nc.dram_tensor("out_0", (NTOK, E), F32, kind="ExternalOutput").ap()
    four_layers(nc, aps, out)
    r = run_bass_kernel_spmd(nc, [arrays], core_ids=[0])
    return r.results[0]["out_0"].reshape(B, S, E)
```

```python
from contextlib import ExitStack

import numpy as np

import concourse.bass as bass
from concourse import mybir

ALU = mybir.AluOpType
ACT = mybir.ActivationFunctionType
AX = mybir.AxisListType
F32 = mybir.dt.float32
BF16 = mybir.dt.bfloat16
I32 = mybir.dt.int32

P = 128
B, S, E = 4, 1024, 128
NTOK = B * S
TILES = NTOK // P
EPS = 1e-5

HEADS, HD = 16, 64
GROUP_TOK = 64
POS = GROUP_TOK * HEADS
PT = POS // P
TT = GROUP_TOK // PT
PAIRS = HEADS // 2
PARTS = 3
MROWS = PARTS * PT
KAUG = HD + MROWS


class Chain:

    def __init__(self, eng, sem, base=0):
        self.eng, self.sem, self.base, self.n = eng, sem, base, 0

    def __call__(self, ins):
        ins.then_inc(self.sem, 1)
        self.n += 1
        self.eng.wait_ge(self.sem, self.base + self.n)


def bc(ap, n):
    return ap.unsqueeze(len(ap.shape)).broadcast_to([*ap.shape, n])


def start_at_one(sp, *sems):
    for s in sems:
        sp.sem_inc(s, 1)


LN_CHUNKS = 4
CT = TILES // LN_CHUNKS


def layernorm_block(nc, tag, x, xT, half, ident, keep_norm, loads, xh=None, xl=None, splits=(), x_dram=None, rms_w=None, rows=None):
    with ExitStack() as ctx:
        sb = lambda n, s, d=F32: ctx.enter_context(nc.sbuf_tensor(f"{tag}_{n}", s, d))
        sem = lambda n: ctx.enter_context(nc.semaphore(f"{tag}_{n}"))
        ring = 3 if rows is None else LN_CHUNKS
        xn = sb("xn", [P, ring, CT, E]) if rows is None else rows[:].rearrange("p (c t) e -> p c t e", c=LN_CHUNKS)
        sq = sb("sq", [P, CT, E])
        st = sb("st", [P, 4, TILES])
        ps = ctx.enter_context(nc.psum_tensor(f"{tag}_ps", [P, 4, 512], F32))
        steps, var_ready, rstd_ready, norm_ready = sem("steps"), sem("var_ready"), sem("rstd_ready"), sem("norm_ready")
        turned, evicted, weights_loaded = sem("turned"), sem("evicted"), sem("weights_loaded")
        if xh is not None:
            high_ready, low_ready = sem("high_ready"), sem("low_ready")
        if x_dram is not None:
            x_loaded = [sem(f"x_loaded{c}") for c in range(LN_CHUNKS)]
        block = ctx.enter_context(nc.Block())
        rounds = 2 if rms_w is not None else 1
        outs = (xT,) if xh is None else (xT, xh)
        variances = [(k - r, r) for k in range(LN_CHUNKS + rounds) for r in range(rounds) if 0 <= k - r < LN_CHUNKS]

        @block.sync
        def _(sp):
            if x_dram is not None:
                for c in range(LN_CHUNKS):
                    sl = slice(c * CT, (c + 1) * CT)
                    sp.dma_start(x[:, sl], x_dram.rearrange("(t p) e -> p t e", p=P)[:, sl]).then_inc(x_loaded[c], 16)
            for dst, src in loads:
                sp.dma_start(dst, src).then_inc(weights_loaded, 16)
            sp.wait_ge(weights_loaded, 16 * len(loads))

        @block.vector
        def _(dve):
            step = Chain(dve, steps)
            part = lambda k, c: st[:, k, c * CT:(c + 1) * CT]

            def moments(c, r):
                y = xn[:, c % ring]
                if r == 0:
                    if x_dram is not None:
                        dve.wait_ge(x_loaded[c], 16)
                    if c >= ring:
                        dve.wait_ge(turned, (c - ring + 1) * CT)
                    xc = x[:, c * CT:(c + 1) * CT, :]
                    step(dve.tensor_reduce(part(0, c), xc, AX.X, ALU.add))
                    step(dve.tensor_scalar(part(0, c), part(0, c), -1.0 / E, None, ALU.mult))
                    step(dve.tensor_tensor(y, xc, bc(part(0, c), E), ALU.add))
                step(dve.tensor_tensor(sq[:], y, y, ALU.mult))
                step(dve.tensor_reduce(part(1, c), sq[:], AX.X, ALU.add))
                dve.tensor_scalar(part(2, c), part(1, c), 1.0 / E, EPS, ALU.mult, ALU.add).then_inc(var_ready, 1)

            def scale(c, r):
                y = xn[:, c % ring]
                dve.wait_ge(rstd_ready, variances.index((c, r)) + 1)
                ins = dve.tensor_tensor(y, y, bc(part(3, c), E), ALU.mult)
                if r == rounds - 1:
                    ins.then_inc(norm_ready, 1)
                    dve.wait_ge(norm_ready, c + 1)
                else:
                    step(ins)
                if r == 0 and keep_norm:
                    xc = x[:, c * CT:(c + 1) * CT, :]
                    step(dve.tensor_tensor(xc, xc, y, ALU.add))

            for k in range(LN_CHUNKS + rounds):
                for r in range(rounds + 1):
                    if 0 <= k - r < LN_CHUNKS:
                        if r > 0:
                            scale(k - r, r - 1)
                        if r < rounds:
                            moments(k - r, r)
            for z in (xh, xl) if xh is not None else ():
                dve.memset(z[:, NTOK:], 0.0).then_inc(low_ready, 1)
            for i, (w, high, low) in enumerate(splits):
                dve.wait_ge(high_ready, i + 1)
                dve.tensor_tensor(low, w, high, ALU.subtract).then_inc(low_ready, 1)
            for q in range(TILES // 4 if xl is not None else 0):
                dve.wait_ge(evicted, 2 * q + 2)
                sl = slice(q * 512, (q + 1) * 512)
                dve.tensor_tensor(xl[:, sl], xT[:, sl], xh[:, sl], ALU.subtract).then_inc(low_ready, 1)

        @block.gpsimd
        def _(pool):
            for n, (c, r) in enumerate(variances):
                pool.wait_ge(var_ready, n + 1)
                sl = slice(c * CT, (c + 1) * CT)
                pool.tensor_tensor(st[:, 3, sl], st[:, 2, sl], half[:, 0:CT], ALU.pow).then_inc(rstd_ready, 1)

        @block.tensor
        def _(pe):
            for c in range(LN_CHUNKS):
                pe.wait_ge(norm_ready, c + 1)
                for k in range(CT):
                    n = c * CT + k
                    if k % 4 == 0 and n >= 16:
                        pe.wait_ge(evicted, len(outs) * (n // 4 - 3))
                    pe.transpose(ps[:, (n // 4) % 4, (k % 4) * P:(k % 4 + 1) * P], xn[:, c % ring, k, :], ident[:]).then_inc(turned, 1)

        @block.scalar
        def _(act):
            if rms_w is not None:
                act.wait_ge(weights_loaded, 16 * len(loads))
            for q in range(TILES // 4):
                act.wait_ge(turned, 4 * q + 4)
                scale = 1.0 if rms_w is None else rms_w[:, 0:1]
                func = ACT.Copy if rms_w is None else ACT.Identity
                for dst in outs:
                    act.activation(dst[:, q * 512:(q + 1) * 512], ps[:, q % 4, :], func, scale=scale).then_inc(evicted, 1)
            act.wait_ge(weights_loaded, 16 * len(loads))
            for w, high, low in splits:
                act.activation(high, w, ACT.Copy).then_inc(high_ready, 1)


def attention_block(nc, xh, xl, wq, wk, wv, identb, mask_qk, mask_kq, row_mask, vd, od):
    with ExitStack() as ctx:
        sb = lambda n, s, d=F32: ctx.enter_context(nc.sbuf_tensor(f"at_{n}", s, d))
        sem = lambda n: ctx.enter_context(nc.semaphore(f"at_{n}"))
        pst = lambda n, s, d=F32: ctx.enter_context(nc.psum_tensor(f"at_{n}", s, d))
        xs = [sb(f"xs{k}", [P, P], BF16) for k in range(2)]
        high = sb("high", [P, 2, 2 * PT, PAIRS, TT], BF16)
        low = sb("low", [P, 2, 2 * PT, PAIRS, TT], BF16)
        q1 = sb("q1", [P, 4, PT, P], BF16)
        q2 = sb("q2", [P, 4, PT, P], BF16)
        k1 = sb("k1", [P, 4, PT, P], BF16)
        k2 = sb("k2", [P, 4, PT, P], BF16)
        vs = sb("vs", [P, HEADS, 2 * HD], BF16)
        vp = sb("vp", [P, 4, PT, 2 * HD + 2], BF16)
        rpart = sb("rpart", [P, 2, PT])
        rmax = sb("rmax", [P, PT])
        rest = sb("rest", [P, PT])
        mparts = sb("mparts", [P, PARTS, PT], BF16)
        prob = sb("prob", [P, PBUFS, PT * P])
        prob_h = sb("prob_h", [P, PBUFS, PT * P], BF16)
        prob_l = sb("prob_l", [P, PBUFS, PT * P], BF16)
        rden = sb("rden", [P, 4])
        outs = sb("outs", [P, 2, PT, HD])
        psP = pst("psP", [P, 1024])
        psM = pst("psM", [P, 1024])
        psS = pst("psS", [P, 1024])
        psO = pst("psO", [P, 2, 512])

        setup = sem("setup")
        xs_ready = sem("xs_ready")
        q_ps, k_ps, v_ps = sem("q_ps"), sem("k_ps"), sem("v_ps")
        q_high, k_high, v_out = sem("q_high"), sem("k_high"), sem("v_out")
        q_low, k_low = sem("q_low"), sem("k_low")
        packed = sem("packed")
        max_ps, reduced = sem("max_ps"), sem("reduced")
        max_split = sem("max_split")
        max_turned, max_rows = sem("max_turned"), sem("max_rows")
        score_ps, probs = sem("score_ps"), sem("probs")
        high_probs, low_probs, v_low = sem("high_probs"), sem("low_probs"), sem("v_low")
        pv_done = sem("pv_done")
        recip, out_ready = sem("recip"), sem("out_ready")
        o_stored = [[sem(f"o_stored{a}{b}") for b in range(2)] for a in range(2)]
        v_stored = sem("v_stored")
        v_loaded = [sem(f"v_loaded{a}") for a in range(2)]
        block = ctx.enter_context(nc.Block())

        SCORE_ORDER = [7, 6, 5, 4, 3, 2, 1, 0]
        MAX_ORDER = [7, 6, 5, 4, 0, 3, 2, 1]

        def pieces(order):
            cut = [(t, lo, min(t + 1, lo + 4)) for t in order for lo in range(0, t + 1, 4)]
            return {t: [(n, lo, hi) for n, (u, lo, hi) in enumerate(cut) if u == t] for t in order}

        SCORE_PIECES, MAX_PIECES = pieces(SCORE_ORDER), pieces(MAX_ORDER)
        PIECES = sum(len(v) for v in SCORE_PIECES.values())
        MAX_STEPS = {0: [3, 2], 1: [1], 4: [7], 5: [6], 6: [5], 7: [4, 0]}
        ROUNDS = TILES // 2

        PARTS_OF = ((0, 0), (0, 1), (1, 0))

        def project(pe, what, tile, rows=None):
            if what == "q":
                pe.wait_ge(xs_ready, 2 * tile + 2)
                if rows is not None:
                    pe.wait_ge(max_rows, rows)
                elif tile:
                    pe.wait_ge(v_low, tile)
            elif what == "k":
                pe.wait_ge(q_low, tile + 1)
            elif rows is not None:
                pe.wait_ge(max_rows, rows)
            else:
                pe.wait_ge(k_low, tile + 1)
            if what == "v":
                for h in range(2):
                    for a, b in PARTS_OF:
                        ins = pe.matmul(psP[:, h * 512:(h + 1) * 512], xs[a][:], wv[b][:, h * 512:(h + 1) * 512],
                                        start=a + b == 0, stop=a == 1)
            else:
                w = wq if what == "q" else wk
                for j in range(PAIRS):
                    for a, b in PARTS_OF:
                        ins = pe.matmul(psP[:, j * P:(j + 1) * P], w[a][:, j, :], xs[b][:], start=j % 4 == 0 and a + b == 0,
                                        stop=j % 4 == 3 and a == 1, skip_group_check=True)
            ins.then_inc({"q": q_ps, "k": k_ps, "v": v_ps}[what], 1)

        def max_pass(pe, slot, g, t):
            for n, lo, hi in MAX_PIECES[t]:
                pe.wait_ge(reduced, PIECES * g + n + 1)
                out = psM[:, n % 2 * 512:n % 2 * 512 + (hi - lo) * P]
                diag = hi == t + 1
                pe.matmul(out, q1[:, slot, t, :], k1[:, slot, lo:hi, :], start=True, stop=False, skip_group_check=True)
                ins = pe.matmul(out, q1[0:HD, slot, t, :], k2[0:HD, slot, lo:hi, :], start=False, stop=not diag,
                                skip_group_check=True)
                if diag:
                    ins = pe.matmul(out[:, (t - lo) * P:], identb, mask_qk, start=False, stop=True, skip_group_check=True)
                ins.then_inc(max_ps, 1)

        def turn_max(pe, g):
            pe.wait_ge(max_split, 5 * g + 5)
            pe.transpose(psP[0:MROWS, 0:P // 2].bitcast(BF16), mparts[:].rearrange("p a b -> p (a b)"),
                         identb).then_inc(max_turned, 1)

        def score_pass(pe, slot, g, i):
            t = SCORE_ORDER[i]
            if i == 0:
                pe.wait_ge(max_rows, g + 1)
            for n, lo, hi in SCORE_PIECES[t]:
                pe.wait_ge(probs, PIECES * g + n + 1)
                for j in range(lo, hi):
                    out = psS[:, n % 2 * 512 + (j - lo) * P:n % 2 * 512 + (j - lo + 1) * P]
                    pe.matmul(out, k1[:, slot, j, :], q1[:, slot, t, :], start=j == lo, stop=False, skip_group_check=True)
                    ins = pe.matmul(out, k2[0:KAUG, slot, j, :], q2[0:KAUG, slot, t, :], start=False, stop=j < t,
                                    skip_group_check=True)
                if hi == t + 1:
                    ins = pe.matmul(out, identb, mask_kq, start=False, stop=True, skip_group_check=True)
                ins.then_inc(score_ps, 1)

        def pv_pass(pe, slot, g, loads, i):
            t = PT - 1 - i
            pe.wait_ge(low_probs, PT * g + i + 1)
            if i == 0:
                pe.wait_ge(v_loaded[slot // 2], loads)
            if i % 4 == 0:
                pe.wait_ge(out_ready, 2 * g + i // 4 + 1)
            c = (t % 4) * (HD + 1)
            both, low = psO[:, t // 4, c:c + HD + 1], psO[:, t // 4, c:c + HD]
            for j in range(t + 1):
                ph, pl = (z[:, i % PBUFS, j * P:(j + 1) * P] for z in (prob_h, prob_l))
                v1, vl = vp[:, slot, j, HD:2 * HD + 1], vp[:, slot, j, 0:HD]
                pe.matmul(both, ph, v1, start=j == 0 and i % 4 == 0, stop=False, skip_group_check=True)
                pe.matmul(low, ph, vl, start=False, stop=False, skip_group_check=True)
                ins = pe.matmul(both, pl, v1, start=False, stop=j == t, skip_group_check=True)
            ins.then_inc(pv_done, 1)

        @block.tensor
        def _(pe):
            pe.wait_ge(setup, 3)
            for what in "qkv":
                project(pe, what, 0)
            for what in "qk":
                project(pe, what, 1)
            pe.wait_ge(packed, 2)
            for t in MAX_ORDER:
                max_pass(pe, 0, 0, t)
            pe.wait_ge(k_low, 2)
            turn_max(pe, 0)
            for i in range(4, PT):
                if i + LAG >= PT:
                    score_pass(pe, 0, 0, i + LAG - PT)
                for t in MAX_STEPS[i]:
                    max_pass(pe, 1, 1, t)
            with pe.Fori(0, ROUNDS) as r:
                for s in range(4):
                    g, tile = 4 * r + s, 2 * r + (s // 2 + 1)
                    for i in range(PT):
                        ahead = int(i + LAG >= PT)
                        score_pass(pe, (s + ahead) % 4, g + ahead, (i + LAG) % PT)
                        if i == 2:
                            pe.wait_ge((k_low, v_low)[s % 2], tile + 1)
                            turn_max(pe, g + 1)
                        if i == 4:
                            pe.wait_ge(packed, g + 3)
                        ahead = 1 + (i >= 4)
                        for t in MAX_STEPS.get(i, ()):
                            max_pass(pe, (s + ahead) % 4, g + ahead, t)
                        pv_pass(pe, s, g, V_LOADS * (r + 1), i)
                        if s % 2 == 0 and i == 3:
                            project(pe, "v", tile, g + 2)
                        if s % 2 and i == 3:
                            project(pe, "q", tile + 1, g + 2)
                        if s % 2 and i == 5:
                            project(pe, "k", tile + 1)

        def lower_part(dve, which, tile):
            dve.wait_ge((q_high, k_high)[which], tile + 1)
            src = psP[:].rearrange("p (j g x) -> p g j x", j=PAIRS, x=TT)
            dve.tensor_tensor(low[:, which], src, high[:, which], ALU.subtract).then_inc((q_low, k_low)[which], 1)

        def pack_half(slot):
            return slice((slot % 2) * PT, (slot % 2 + 1) * PT)

        def pack_q(dve, slot, *sides):
            for side in sides:
                for dst, rows, part in ((q1, 0, high), (q1, HD, low), (q2, 0, high)):
                    dve.tensor_copy(dst[rows:rows + HD, slot, :, side * HD:(side + 1) * HD],
                                    part[side * HD:(side + 1) * HD, 0, pack_half(slot)].rearrange("p g j x -> p g (j x)"))

        def pack_k(dve, slot):
            for dst, rows, part in ((k1, 0, high), (k1, HD, high), (k2, 0, low)):
                for side in range(2):
                    ins = dve.tensor_copy(dst[rows:rows + HD, slot, :, side * HD:(side + 1) * HD],
                                          part[side * HD:(side + 1) * HD, 1, pack_half(slot)].rearrange("p g j x -> p g (j x)"))
            ins.then_inc(packed, 1)

        def reduce_tile(dve, g, t):
            for n, lo, hi in MAX_PIECES[t]:
                dve.wait_ge(max_ps, PIECES * g + n + 1)
                dve.tensor_reduce(rpart[:, lo // 4, t:t + 1], psM[:, n % 2 * 512:n % 2 * 512 + (hi - lo) * P], AX.X,
                                  ALU.max).then_inc(reduced, 1)

        def split_max(dve, g):
            dve.wait_ge(reduced, PIECES * g + PIECES + 2)
            dve.tensor_tensor(rmax[:], rpart[:, 0, :], rpart[:, 1, :], ALU.max).then_inc(max_split, 1)
            dve.wait_ge(max_split, 5 * g + 1)
            if not isinstance(g, int):
                dve.wait_ge(max_turned, g)
            h, m, l = (mparts[:, k, :] for k in range(PARTS))
            dve.tensor_scalar(h, rmax[:], -1.0, None, ALU.mult).then_inc(max_split, 1)
            dve.wait_ge(max_split, 5 * g + 2)
            dve.scalar_tensor_tensor(rest[:], rmax[:], -1.0, h, ALU.mult, ALU.subtract).then_inc(max_split, 1)
            dve.wait_ge(max_split, 5 * g + 3)
            dve.tensor_copy(m, rest[:]).then_inc(max_split, 1)
            dve.wait_ge(max_split, 5 * g + 4)
            dve.tensor_tensor(l, rest[:], m, ALU.subtract).then_inc(max_split, 1)

        def place_max(dve, slot, g):
            dve.wait_ge(max_turned, g + 1)
            src = psP[0:MROWS, 0:P // 2].bitcast(BF16).unsqueeze(1).broadcast_to([MROWS, PT, P])
            dve.tensor_tensor(q2[HD:KAUG, slot], src, row_mask, ALU.mult).then_inc(max_rows, 1)

        def low_v(dve, tile):
            dve.wait_ge(v_out, tile + 1)
            dve.tensor_tensor(vs[:, :, 0:HD], psP[:].rearrange("p (i d) -> p i d", d=HD), vs[:, :, HD:2 * HD],
                              ALU.subtract).then_inc(v_low, 1)

        def normalise(dve, s, g, uses, n):
            h = 1 - n
            dve.wait_ge(pv_done, PT * g + 4 * n + 4 + PBUFS)
            dve.wait_ge(o_stored[s % 2][h], 64 * uses + 1)
            acc = psO[:, h, 0:4 * (HD + 1)].rearrange("p (t c) -> p t c", t=4)
            dve.reciprocal(rden[:], acc[:, :, HD]).then_inc(recip, 1)
            dve.wait_ge(recip, 2 * g + n + 1)
            dve.tensor_tensor(outs[:, s % 2, 4 * h:4 * h + 4, :], acc[:, :, 0:HD], bc(rden[:], HD), ALU.mult).then_inc(out_ready, 1)
            dve.wait_ge(out_ready, 2 * g + n + 3)

        @block.vector
        def _(dve):
            dve.wait_ge(setup, 3)
            lower_part(dve, 0, 0)
            lower_part(dve, 1, 0)
            dve.wait_ge(k_low, 1)
            for slot in range(2):
                pack_q(dve, slot, 0, 1)
                pack_k(dve, slot)
            low_v(dve, 0)
            lower_part(dve, 0, 1)
            dve.wait_ge(q_low, 2)
            pack_q(dve, 2, 0, 1)
            lower_part(dve, 1, 1)
            for t in MAX_ORDER:
                reduce_tile(dve, 0, t)
            split_max(dve, 0)
            place_max(dve, 0, 0)
            for i in range(4, PT):
                for t in MAX_STEPS[i]:
                    reduce_tile(dve, 1, t)
            with dve.Fori(0, ROUNDS) as r:
                for s in range(4):
                    g, tile = 4 * r + s, 2 * r + (s // 2 + 1)
                    for i in range(4):
                        for t in MAX_STEPS.get(i, ()):
                            reduce_tile(dve, g + 1, t)
                    split_max(dve, g + 1)
                    place_max(dve, (s + 1) % 4, g + 1)
                    dve.wait_ge(k_low, tile + 1)
                    pack_k(dve, (s + 2) % 4)
                    for i in range(4, PT):
                        for t in MAX_STEPS[i]:
                            reduce_tile(dve, g + 2, t)
                        if i == 4:
                            normalise(dve, s, g, 2 * r + s // 2, 0)
                            if s % 2:
                                lower_part(dve, 0, tile + 1)
                                dve.wait_ge(q_low, tile + 2)
                        if i in (5, 6):
                            pack_q(dve, (s + 3) % 4, i - 5)
                        if i == 7 and s % 2:
                            lower_part(dve, 1, tile + 1)
                        if i == 7 and s % 2 == 0:
                            low_v(dve, tile)
                    normalise(dve, s, g, 2 * r + s // 2, 1)

        def exp_tile(act, g, i):
            t = SCORE_ORDER[i]
            act.wait_ge(pv_done, PT * g + i + 1)
            for n, lo, hi in SCORE_PIECES[t]:
                act.wait_ge(score_ps, PIECES * g + n + 1)
                act.activation(prob[:, i % PBUFS, lo * P:hi * P], psS[:, n % 2 * 512:n % 2 * 512 + (hi - lo) * P], ACT.Exp,
                               scale=HD ** -0.5).then_inc(probs, 1)

        def high_prob(act, g, i):
            t = SCORE_ORDER[i]
            act.wait_ge(probs, PIECES * g + SCORE_PIECES[t][-1][0] + 3)
            act.activation(prob_h[:, i % PBUFS, 0:(t + 1) * P], prob[:, i % PBUFS, 0:(t + 1) * P], ACT.Copy).then_inc(high_probs, 1)

        def upper_part(act, which, tile, before=None):
            act.wait_ge((q_ps, k_ps)[which], tile + 1)
            if which == 0 and before is not None:
                act.wait_ge(packed, before)
            src = psP[:].rearrange("p (j g x) -> p g j x", j=PAIRS, x=TT)
            act.activation(high[:, which], src, ACT.Copy).then_inc((q_high, k_high)[which], 1)

        def v_to_sbuf(act, tile):
            act.wait_ge(v_ps, tile + 1)
            act.wait_ge(v_stored, 16 * tile)
            act.activation(vs[:, :, HD:2 * HD], psP[:].rearrange("p (i d) -> p i d", d=HD), ACT.Copy).then_inc(v_out, 1)
            for k in range(2):
                act.activation(xs[k][:], (xh, xl)[k][:, bass.ds((tile + 1) * P, P)], ACT.Copy).then_inc(xs_ready, 1)

        @block.scalar
        def _(act):
            for k in range(2):
                act.activation(xs[k][:], (xh, xl)[k][:, 0:P], ACT.Copy).then_inc(xs_ready, 1)
            upper_part(act, 0, 0)
            upper_part(act, 1, 0)
            v_to_sbuf(act, 0)
            upper_part(act, 0, 1, 2)
            upper_part(act, 1, 1)
            for i in range(LAG):
                exp_tile(act, 0, i)
                if i:
                    high_prob(act, 0, i - 1)
            with act.Fori(0, ROUNDS) as r:
                for s in range(4):
                    g, tile = 4 * r + s, 2 * r + (s // 2 + 1)
                    for i in range(PT):
                        ahead, ahead_high = int(i + LAG >= PT), int(i + LAG > PT)
                        exp_tile(act, g + ahead, (i + LAG) % PT)
                        high_prob(act, g + ahead_high, (i + LAG - 1) % PT)
                        if s % 2 and i in (4, 6):
                            upper_part(act, i // 6, tile + 1, g + 3)
                        if s % 2 == 0 and i == 4:
                            v_to_sbuf(act, tile)

        def turn_v(sp, slot, tile):
            sp.wait_ge(v_low, tile + 1)
            rows = vd[bass.ds(tile * P, P), :]
            sp.dma_start(rows, vs[:].rearrange("p i c -> p (i c)")).then_inc(v_stored, 16)
            sp.wait_ge(v_stored, 16 * tile + 16)
            for h in range(2):
                for t in range(PT):
                    src = vd[bass.ds(tile * P + (h * GROUP_TOK + t * TT), TT), :].rearrange("x (i d) -> i x d", i=HEADS)
                    sp.dma_start(vp[:, slot + h, t, 0:2 * HD], src).then_inc(v_loaded[slot // 2], 16)

        def store_outs(sp, s, g, n):
            h = 1 - n
            sp.wait_ge(out_ready, 2 * g + n + 3)
            for t in range(4 * h, 4 * h + 4):
                dst = od[bass.ds(g * GROUP_TOK + t * TT, TT), :].rearrange("x (i d) -> i x d", i=HEADS)
                sp.dma_start(dst, outs[:, s % 2, t, :]).then_inc(o_stored[s % 2][h], 16)

        @block.sync
        def _(sp):
            start_at_one(sp, *o_stored[0], *o_stored[1])
            sp.wait_ge(setup, 3)
            turn_v(sp, 0, 0)
            with sp.Fori(0, ROUNDS) as r:
                for s in range(4):
                    g, tile = 4 * r + s, 2 * r + (s // 2 + 1)
                    store_outs(sp, s, g, 0)
                    if s % 2 == 0:
                        turn_v(sp, (s + 2) % 4, tile)
                    store_outs(sp, s, g, 1)
            for a in range(2):
                for b in range(2):
                    sp.wait_ge(o_stored[a][b], 64 * 2 * ROUNDS + 1)
            for a in range(2):
                sp.wait_ge(v_loaded[a], V_LOADS * (ROUNDS + (a == 0)))

        @block.gpsimd
        def _(pool):
            pool.memset(k2[HD:KAUG], 1.0).then_inc(setup, 1)
            pool.wait_ge(setup, 1)
            pool.memset(vp[:, :, :, 2 * HD:2 * HD + 1], 1.0).then_inc(setup, 1)
            pool.wait_ge(setup, 2)
            pool.memset(rpart[:, 1, :], -3e38).then_inc(setup, 1)
            pool.sem_inc(reduced, 2)
            pool.sem_inc(probs, 2)
            pool.sem_inc(pv_done, PBUFS)
            pool.sem_inc(out_ready, 2)
            with pool.Fori(0, ROUNDS) as r:
                for s in range(4):
                    for i in range(PT):
                        n = (PT - i) * P
                        pool.wait_ge(high_probs, PT * (4 * r + s) + i + 1)
                        pool.tensor_tensor(prob_l[:, i % PBUFS, 0:n], prob[:, i % PBUFS, 0:n], prob_h[:, i % PBUFS, 0:n],
                                           ALU.subtract).then_inc(low_probs, 1)


PBUFS = 4
LAG = 3
V_LOADS = 2 * PT * 16


def projection_block(nc, x, wp, bias, od, ident):
    with ExitStack() as ctx:
        sb = lambda n, s, d=F32: ctx.enter_context(nc.sbuf_tensor(f"pr_{n}", s, d))
        sem = lambda n: ctx.enter_context(nc.semaphore(f"pr_{n}"))
        KC = HEADS * HD // P
        o = sb("o", [P, 4, KC, P])
        oT = sb("oT", [P, 2, KC, P])
        psT = ctx.enter_context(nc.psum_tensor("pr_psT", [P, 2, KC * P], F32))
        psY = ctx.enter_context(nc.psum_tensor("pr_psY", [P, 2, 512], F32))
        loaded = [sem(f"loaded{s}") for s in range(4)]
        turned, o_turned, y_ps, added = sem("turned"), sem("o_turned"), sem("y_ps"), sem("added")
        block = ctx.enter_context(nc.Block())
        ROUNDS = TILES // 4

        @block.sync
        def _(sp):
            sp.sem_inc(turned, 4)
            start_at_one(sp, y_ps)
            with sp.Fori(0, ROUNDS) as r:
                for s in range(4):
                    sp.wait_ge(turned, 4 * r + s + 1)
                    sp.dma_start(o[:, s], od[bass.ds((4 * r + s) * P, P), :].rearrange("p (k c) -> p k c", c=P)).then_inc(loaded[s], 16)
            for s in range(4):
                sp.wait_ge(loaded[s], 16 * ROUNDS)

        @block.tensor
        def _(pe):
            with pe.Fori(0, ROUNDS) as r:
                for pair in (0, 2):
                    for s in range(pair, pair + 2):
                        pe.wait_ge(loaded[s], 16 * r + 16)
                        for k in range(KC):
                            ins = pe.transpose(psT[:, s % 2, k * P:(k + 1) * P], o[:, s, k, :], ident[:])
                        ins.then_inc(turned, 1)
                    for s in range(pair, pair + 2):
                        pe.wait_ge(o_turned, 4 * r + s + 1)
                        pe.wait_ge(added, 4 * r + pair + 1)
                        for k in range(KC):
                            ins = pe.matmul(psY[:, s % 2, 0:E], oT[:, s % 2, k, :], wp[:, k, :], start=k == 0, stop=k == KC - 1)
                        ins.then_inc(y_ps, 1)

        @block.scalar
        def _(act):
            with act.Fori(0, ROUNDS) as r:
                for s in range(4):
                    act.wait_ge(turned, 4 * r + s + 5)
                    act.wait_ge(y_ps, 4 * r + s // 2 * 2 + 1)
                    act.activation(oT[:, s % 2], psT[:, s % 2, :], ACT.Copy).then_inc(o_turned, 1)

        @block.vector
        def _(dve):
            dve.tensor_tensor(x[:], x[:], bias.unsqueeze(1).broadcast_to([P, TILES, E]), ALU.add).then_inc(added, 1)
            dve.wait_ge(added, 1)
            with dve.Fori(0, ROUNDS) as r:
                for s in range(4):
                    dve.wait_ge(y_ps, 4 * r + s + 2)
                    xt = x[:, bass.ds(4 * r + s, 1), :]
                    dve.tensor_tensor(xt, xt, psY[:, s % 2:s % 2 + 1, 0:E], ALU.add).then_inc(added, 1)


def rank_steps(step, dve, cnt, t, v, n, lower):
    sh = list(v.shape)[:-1]
    step(dve.tensor_copy(cnt, lower.unsqueeze(1).broadcast_to([*sh, n])))
    for d in range(1, n):
        ge = t[..., 0:n - d]
        step(dve.tensor_tensor(ge, v[..., 0:n - d], v[..., d:n], ALU.is_ge))
        step(dve.tensor_tensor(cnt[..., d:n], cnt[..., d:n], ge, ALU.add))
        step(dve.tensor_tensor(cnt[..., 0:n - d], cnt[..., 0:n - d], ge, ALU.subtract))


def split_parts(step, dve, parts, v, rest):
    step(dve.tensor_copy(parts[0], v))
    step(dve.tensor_tensor(rest, v, parts[0], ALU.subtract))
    step(dve.tensor_copy(parts[1], rest))
    step(dve.tensor_tensor(parts[2], rest, parts[1], ALU.subtract))


TB = 512
BLOCKS = NTOK // TB
BT = TB // P


def moe0_block(nc, x, xT, wgate, gbias, lower4, lower16, wg, wu, wd, sel, ident, identb):
    NE, TOPK, SCALE = 16, 4, 2.5
    NP_ = NE // 2
    NC = NP_ + 1
    with ExitStack() as ctx:
        sb = lambda n, s, d=F32: ctx.enter_context(nc.sbuf_tensor(f"m0_{n}", s, d))
        sem = lambda n: ctx.enter_context(nc.semaphore(f"m0_{n}"))
        cwT = sb("cwT", [PARTS * NE, NTOK], BF16)
        with ExitStack() as rc:
            rb = lambda n, s, d=F32: rc.enter_context(nc.sbuf_tensor(f"r0_{n}", s, d))
            scores, v, cnt, t = (rb(n, [P, TILES, NE]) for n in ("scores", "v", "cnt", "t"))
            pa, pb, pc, pd, gs, gcnt, gt = (rb(n, [P, TILES, 4]) for n in ("pa", "pb", "pc", "pd", "gs", "gcnt", "gt"))
            den = rb("den", [P, TILES])
            parts = rb("parts", [P, TILES, PARTS, NE], BF16)
            psL = rc.enter_context(nc.psum_tensor("r0_psL", [P, TILES, NE], F32))
            psW = rc.enter_context(nc.psum_tensor("r0_psW", [P, 4, 512], F32))
            logits, scored, steps, turned, evicted, parts_ready = (rc.enter_context(nc.semaphore(f"r0_{n}")) for n in (
                "logits", "scored", "steps", "turned", "evicted", "parts_ready"))
            block = rc.enter_context(nc.Block())

            @block.tensor
            def _(pe):
                for k in range(TILES):
                    ins = pe.matmul(psL[:, k, :], xT[:, k * P:(k + 1) * P], wgate[:], start=k == 0, stop=k == TILES - 1, skip_group_check=True)
                ins.then_inc(logits, 1)
                pe.wait_ge(parts_ready, 1)
                for k in range(TILES):
                    if k % 8 == 0 and k >= 32:
                        pe.wait_ge(evicted, k // 8 - 3)
                    out = psW[0:PARTS * NE, k // 8, :].bitcast(BF16)[:, (k % 8) * P:(k % 8 + 1) * P]
                    pe.transpose(out, parts[:, k].rearrange("p a b -> p (a b)"), identb).then_inc(turned, 1)

            @block.scalar
            def _(act):
                act.wait_ge(logits, 1)
                act.activation(scores[:], psL[:], ACT.Sigmoid).then_inc(scored, 1)
                for q in range(TILES // 8):
                    act.wait_ge(turned, 8 * q + 8)
                    act.activation(cwT[:, q * 1024:(q + 1) * 1024], psW[0:PARTS * NE, q, :].bitcast(BF16), ACT.Copy).then_inc(evicted, 1)

            @block.vector
            def _(dve):
                step = Chain(dve, steps)
                dve.wait_ge(scored, 1)
                step(dve.tensor_tensor(v[:], scores[:], gbias.unsqueeze(1).broadcast_to([P, TILES, NE]), ALU.add))
                v4 = v[:].rearrange("p t (g k) -> p t g k", k=4)
                step(dve.tensor_tensor(pa[:], v4[..., 0], v4[..., 1], ALU.max))
                step(dve.tensor_tensor(pb[:], v4[..., 0], v4[..., 1], ALU.min))
                step(dve.tensor_tensor(pc[:], v4[..., 2], v4[..., 3], ALU.max))
                step(dve.tensor_tensor(pd[:], v4[..., 2], v4[..., 3], ALU.min))
                step(dve.tensor_tensor(gs[:], pa[:], pc[:], ALU.add))
                step(dve.tensor_tensor(pb[:], pa[:], pb[:], ALU.add))
                step(dve.tensor_tensor(pd[:], pc[:], pd[:], ALU.add))
                step(dve.tensor_tensor(gs[:], gs[:], pb[:], ALU.max))
                step(dve.tensor_tensor(gs[:], gs[:], pd[:], ALU.max))
                rank_steps(step, dve, gcnt[:], gt[:], gs[:], 4, lower4)
                step(dve.tensor_scalar(gt[:], gcnt[:], 1.5, None, ALU.is_lt))
                step(dve.tensor_scalar(gt[:], gt[:], 1e30, -1e30, ALU.mult, ALU.add))
                step(dve.tensor_tensor(v4.rearrange("p t g k -> p (t g) k"), v4.rearrange("p t g k -> p (t g) k"),
                                       bc(gt[:].rearrange("p t g -> p (t g)"), 4), ALU.add))
                rank_steps(step, dve, cnt[:], t[:], v[:], NE, lower16)
                step(dve.tensor_scalar(cnt[:], cnt[:], TOPK - 0.5, None, ALU.is_lt))
                step(dve.tensor_tensor(v[:], scores[:], cnt[:], ALU.mult))
                step(dve.tensor_reduce(den[:], v[:], AX.X, ALU.add))
                step(dve.tensor_scalar(den[:], den[:], 1e-20, None, ALU.add))
                step(dve.reciprocal(den[:], den[:]))
                step(dve.tensor_scalar(den[:], den[:], SCALE, None, ALU.mult))
                step(dve.tensor_tensor(v[:], v[:], bc(den[:], NE), ALU.mult))
                split_parts(step, dve, [parts[:, :, k, :] for k in range(PARTS)], v[:], t[:])
                dve.sem_inc(parts_ready, 1)

        act_s = sb("silu", [P, 2, TB])
        prod = sb("prod", [P, TB])
        hid = sb("hid", [P, 2, TB])
        yT = sb("yT", [P, TB])
        psG, psU, psC = (ctx.enter_context(nc.psum_tensor(f"m0_{n}", [P, 2, TB], F32)) for n in ("psG", "psU", "psC"))
        psY = ctx.enter_context(nc.psum_tensor("m0_psY", [P, TB], F32))
        psT = ctx.enter_context(nc.psum_tensor("m0_psT", [P, TB], F32))
        up_ps, silu_ready, prod_ready, hid_ready, y_ps, y_out, y_turned, added = (sem(n) for n in (
            "up_ps", "silu_ready", "prod_ready", "hid_ready", "y_ps", "y_out", "y_turned", "added"))
        block = ctx.enter_context(nc.Block())

        @block.sync
        def _(sp):
            start_at_one(sp, added, hid_ready, prod_ready, y_out, y_ps, y_turned)

        @block.tensor
        def _(pe):
            def up(r, c):
                pe.wait_ge(hid_ready, NC * r + max(c, 1))
                tok = bass.ds(r * TB, TB)
                pe.matmul(psG[:, c % 2, :], wg[:, c, :], xT[:, tok], start=True, stop=True)
                ins = pe.matmul(psU[:, c % 2, :], wu[:, c, :], xT[:, tok], start=True, stop=True)
                if c < NP_:
                    ins = pe.matmul(psC[:, c % 2, :], sel[:, c, :], cwT[:, tok], start=True, stop=True)
                ins.then_inc(up_ps, 1)

            def round_of(r, last):
                for c in range(NC):
                    if c + 1 < NC:
                        up(r, c + 1)
                    if c == 0:
                        pe.wait_ge(y_out, r + 1)
                    pe.wait_ge(hid_ready, NC * r + c + 2)
                    pe.matmul(psY[:], wd[:, c, :], hid[:, c % 2, :], start=c == 0, stop=c == NC - 1).then_inc(y_ps, 1)
                if not last:
                    up(r + 1, 0)
                pe.wait_ge(y_out, r + 2)
                pe.wait_ge(added, r + 1)
                for k in range(BT):
                    ins = pe.transpose(psT[:, k * P:(k + 1) * P], yT[:, k * P:(k + 1) * P], ident[:])
                ins.then_inc(y_turned, 1)

            up(0, 0)
            with pe.Fori(0, BLOCKS - 1) as r:
                round_of(r, False)
            round_of(BLOCKS - 1, True)

        @block.scalar
        def _(act):
            with act.Fori(0, BLOCKS) as r:
                for c in range(NC):
                    act.wait_ge(up_ps, NC * r + c + 1)
                    act.wait_ge(prod_ready, NC * r + c) if c else act.wait_ge(prod_ready, NC * r + 1)
                    act.activation(act_s[:, c % 2, :], psG[:, c % 2, :], ACT.Silu).then_inc(silu_ready, 1)
                act.wait_ge(y_ps, NC * r + NC + 1)
                act.wait_ge(y_turned, r + 1)
                act.activation(yT[:], psY[:], ACT.Copy).then_inc(y_out, 1)

        @block.vector
        def _(dve):
            with dve.Fori(0, BLOCKS) as r:
                for c in range(NC):
                    n = NC * r + c
                    dve.wait_ge(silu_ready, n + 1)
                    if c < NP_:
                        dve.wait_ge(hid_ready, n + 1)
                        dve.tensor_tensor(prod[:], act_s[:, c % 2, :], psU[:, c % 2, :], ALU.mult).then_inc(prod_ready, 1)
                        dve.wait_ge(prod_ready, n + 2)
                        dve.wait_ge(y_ps, n) if c else dve.wait_ge(y_ps, n + 1)
                        dve.tensor_tensor(hid[:, c % 2, :], prod[:], psC[:, c % 2, :], ALU.mult).then_inc(hid_ready, 1)
                    else:
                        dve.wait_ge(y_ps, n)
                        dve.tensor_tensor(hid[:, c % 2, :], act_s[:, c % 2, :], psU[:, c % 2, :], ALU.mult).then_inc(hid_ready, 1)
                        dve.wait_ge(hid_ready, n + 2)
                        dve.sem_inc(prod_ready, 1)
                dve.wait_ge(y_turned, r + 2)
                xt = x[:, bass.ds(BT * r, BT), :]
                dve.tensor_tensor(xt, xt, psT[:].rearrange("p (t e) -> p t e", e=E), ALU.add).then_inc(added, 1)


MAMBA = ["skip_w", "in_w", "conv_w", "conv_b", "wdbc", "wd2", "wd2_b", "a_log", "w_d", "out_w", "sel32", "ident"]


def mamba_block(nc, x, xT, skip_w, in_w, conv_w, conv_b, wdbc, wd2, wd2_b, a_log, w_d, out_w, sel32, ident, passed):
    CH, NS, KW, RANK = 2, 16, 4, 64
    PAD = KW - 1
    with ExitStack() as ctx:
        sb = lambda n, s, d=F32: ctx.enter_context(nc.sbuf_tensor(f"mb_{n}", s, d))
        u = sb("u", [P, CH, NTOK])
        gate = sb("gate", [P, CH, NTOK])
        delta = sb("delta", [P, CH, NTOK])
        bcT = sb("bcT", [PARTS * 2 * NS, NTOK], BF16)
        aneg = sb("aneg", [P, CH, NS])

        with ExitStack() as c1:
            sb1 = lambda n, s, d=F32: c1.enter_context(nc.sbuf_tensor(f"mc_{n}", s, d))
            sem = lambda n: c1.enter_context(nc.semaphore(f"mc_{n}"))
            xin = sb1("xin", [P, CH, PAD + S])
            conv = sb1("conv", [P, 2, S])
            ps = c1.enter_context(nc.psum_tensor("mc_ps", [P, 2, CH, TB], F32))
            psi = c1.enter_context(nc.psum_tensor("mc_psi", [P, 2, CH, TB], F32))
            setup, skip_ps, gate_ready, in_ps, in_ready, taps, conv_ready, u_ready = (sem(n) for n in (
                "setup", "skip_ps", "gate_ready", "in_ps", "in_ready", "taps", "conv_ready", "u_ready"))
            block = c1.enter_context(nc.Block())

            @block.sync
            def _(sp):
                start_at_one(sp, conv_ready, gate_ready, in_ready, u_ready)

            @block.tensor
            def _(pe):
                with pe.Fori(0, B) as b:
                    for h in range(2):
                        tok = xT[:, bass.ds(b * S + h * TB, TB)]
                        pe.wait_ge(in_ready, 2 * b + 1)
                        for c in range(CH):
                            ins = pe.matmul(psi[:, h, c, :], in_w[:, c * P:(c + 1) * P], tok, start=True, stop=True)
                        ins.then_inc(in_ps, 1)
                    for h in range(2):
                        tok = xT[:, bass.ds(b * S + h * TB, TB)]
                        pe.wait_ge(gate_ready, 2 * b + 1)
                        for c in range(CH):
                            ins = pe.matmul(ps[:, h, c, :], skip_w[:, c * P:(c + 1) * P], tok, start=True, stop=True)
                        ins.then_inc(skip_ps, 1)

            @block.scalar
            def _(act):
                act.wait_ge(setup, 1)
                with act.Fori(0, B) as b:
                    for h in range(2):
                        act.wait_ge(in_ps, 2 * b + h + 1)
                        act.wait_ge(conv_ready, 2 * b + 1)
                        act.activation(xin[:, :, PAD + h * TB:PAD + (h + 1) * TB], psi[:, h], ACT.Copy).then_inc(in_ready, 1)
                    for h in range(2):
                        act.wait_ge(skip_ps, 2 * b + h + 1)
                        act.sem_inc(passed, 1)
                        act.activation(gate[:, :, bass.ds(b * S + h * TB, TB)], ps[:, h], ACT.Silu).then_inc(gate_ready, 1)
                    for c in range(CH):
                        act.wait_ge(conv_ready, 2 * b + c + 2)
                        act.sem_inc(passed, 1)
                        act.activation(u[:, c, bass.ds(b * S, S)], conv[:, c, :], ACT.Silu, bias=conv_b[:, c, 0:1]).then_inc(u_ready, 1)
                act.activation(aneg[:], a_log, ACT.Exp).then_inc(setup, 1)

            @block.vector
            def _(dve):
                dve.memset(xin[:, :, 0:PAD], 0.0).then_inc(setup, 1)
                with dve.Fori(0, B) as b:
                    dve.wait_ge(in_ready, 2 * b + 3)
                    dve.wait_ge(u_ready, 2 * b + 1)
                    for k in range(KW):
                        for c in range(CH):
                            src, w, out = xin[:, c, k:k + S], conv_w[:, c, k:k + 1], conv[:, c, :]
                            if k == 0:
                                ins = dve.tensor_scalar(out, src, w, None, ALU.mult)
                            else:
                                dve.wait_ge(taps, 6 * b + 2 * (k - 1) + c + 1)
                                ins = dve.scalar_tensor_tensor(out, src, w, out, ALU.mult, ALU.add)
                            ins.then_inc(conv_ready if k == KW - 1 else taps, 1)
                dve.wait_ge(setup, 2)
                dve.tensor_scalar(aneg[:], aneg[:], -1.0, None, ALU.mult).then_inc(setup, 1)
                dve.wait_ge(setup, 3)

        with ExitStack() as c2:
            sb2 = lambda n, s, d=F32: c2.enter_context(nc.sbuf_tensor(f"md_{n}", s, d))
            sem = lambda n: c2.enter_context(nc.semaphore(f"md_{n}"))
            z1 = sb2("z1", [RANK, 2, TB])
            pos = sb2("pos", [P, CH, NTOK])
            middle, rest = sb2("middle", [2 * NS, TB], BF16), sb2("rest", [2 * NS, TB])
            psA = c2.enter_context(nc.psum_tensor("md_psA", [P, 2, TB], F32))
            psZ = c2.enter_context(nc.psum_tensor("md_psZ", [P, 2, CH, TB], F32))
            z1_ps, z1_ready, bc_steps, z2_ps, abs_ready, pos_ready, exp_ready, log_ready, delta_ready = (sem(n) for n in (
                "z1_ps", "z1_ready", "bc_steps", "z2_ps", "abs_ready", "pos_ready", "exp_ready", "log_ready", "delta_ready"))
            block = c2.enter_context(nc.Block())

            @block.sync
            def _(sp):
                start_at_one(sp, bc_steps, pos_ready, z1_ready, z2_ps, abs_ready)

            @block.tensor
            def _(pe):
                with pe.Fori(0, BLOCKS // 2) as r:
                    for s in range(2):
                        pe.wait_ge(z1_ready, 2 * r + 1)
                        pe.wait_ge(bc_steps, 8 * r + 1)
                        for c in range(CH):
                            ins = pe.matmul(psA[0:RANK + 2 * NS, s, :], wdbc[:, c, :], u[:, c, bass.ds((2 * r + s) * TB, TB)],
                                            start=c == 0, stop=c == CH - 1)
                        ins.then_inc(z1_ps, 1)
                    for s in range(2):
                        pe.wait_ge(z1_ready, 2 * r + s + 2)
                        pe.wait_ge(pos_ready, 2 * r + 1)
                        pe.wait_ge(abs_ready, 2 * r + 1)
                        for c in range(CH):
                            ins = pe.matmul(psZ[:, s, c, :], wd2[:, c * P:(c + 1) * P], z1[:, s, :], start=True, stop=True)
                        ins.then_inc(z2_ps, 1)

            @block.scalar
            def _(act):
                with act.Fori(0, BLOCKS // 2) as r:
                    for s in range(2):
                        act.wait_ge(z1_ps, 2 * r + s + 1)
                        act.wait_ge(z2_ps, 2 * r + 1)
                        act.activation(z1[:, s, :], psA[0:RANK, s, :], ACT.Copy).then_inc(z1_ready, 1)
                    for s in range(2):
                        act.wait_ge(z2_ps, 2 * r + s + 2)
                        act.sem_inc(passed, 1)
                        for c in range(CH):
                            ins = act.activation(delta[:, c, bass.ds((2 * r + s) * TB, TB)], psZ[:, s, c, :], ACT.Abs, bias=wd2_b[:, c, 0:1])
                        ins.then_inc(abs_ready, 1)
                    act.wait_ge(abs_ready, 2 * r + 3)
                    act.sem_inc(passed, 1)
                    both = delta[:, :, bass.ds(2 * r * TB, 2 * TB)]
                    act.activation(both, both, ACT.Exp, scale=-1.0).then_inc(exp_ready, 1)
                act.wait_ge(exp_ready, BLOCKS // 2)
                with act.Fori(0, B) as b:
                    seq = delta[:, :, bass.ds(b * S, S)]
                    act.activation(seq, seq, ACT.Ln, bias=1.0).then_inc(log_ready, 1)

            @block.vector
            def _(dve):
                with dve.Fori(0, BLOCKS // 2) as r:
                    for s in range(2):
                        n = 2 * r + s
                        bc_ps = psA[RANK:RANK + 2 * NS, s, :]
                        dve.wait_ge(z1_ps, n + 1)
                        part = [bcT[k * 2 * NS:(k + 1) * 2 * NS, bass.ds(n * TB, TB)] for k in range(PARTS)]
                        dve.tensor_copy(part[0], bc_ps).then_inc(bc_steps, 1)
                        dve.wait_ge(bc_steps, 4 * n + 2)
                        dve.tensor_tensor(rest[:], bc_ps, part[0], ALU.subtract).then_inc(bc_steps, 1)
                        dve.wait_ge(bc_steps, 4 * n + 3)
                        dve.tensor_copy(middle[:], rest[:]).then_inc(bc_steps, 1)
                        dve.wait_ge(bc_steps, 4 * n + 4)
                        dve.tensor_copy(part[1], middle[:])
                        dve.tensor_tensor(part[2], rest[:], middle[:], ALU.subtract).then_inc(bc_steps, 1)
                        dve.wait_ge(bc_steps, 4 * n + 5)
                    for s in range(2):
                        dve.wait_ge(abs_ready, 2 * r + s + 2)
                        for c in range(CH):
                            ins = dve.tensor_scalar(pos[:, c, bass.ds((2 * r + s) * TB, TB)], psZ[:, s, c, :], wd2_b[:, c, 0:1], 0.0, ALU.add, ALU.max)
                        ins.then_inc(pos_ready, 1)
                dve.wait_ge(pos_ready, BLOCKS + 1)
                with dve.Fori(0, B) as b:
                    seq = bass.ds(b * S, S)
                    dve.wait_ge(log_ready, b + 1)
                    dve.tensor_tensor(delta[:, :, seq], pos[:, :, seq], delta[:, :, seq], ALU.add).then_inc(delta_ready, 1)


        with ExitStack() as c3:
            sb3 = lambda n, s, d=F32: c3.enter_context(nc.sbuf_tensor(f"ms_{n}", s, d))
            sem = lambda n: c3.enter_context(nc.semaphore(f"ms_{n}"))
            du = sb3("du", [P, CH, S])
            decay, inject, part_y, b_all, c_all = (sb3(n, [P, 2, S]) for n in ("decay", "inject", "part_y", "b_all", "c_all"))
            state = xT[:, 0:3 * S].rearrange("p (k t) -> p k t", k=3)
            y = part_y
            psBC = c3.enter_context(nc.psum_tensor("ms_psBC", [P, 2, S], F32))
            psY = c3.enter_context(nc.psum_tensor("ms_psY", [P, CH, S], F32))
            bc_ps, du_ready, decay_ready = sem("bc_ps"), sem("du_ready"), sem("decay_ready")
            inject_ready, state_ready, read_out, summed = four = [sem(n) for n in ("inject_ready", "state_ready", "read_out", "summed")]
            bc_out, ends = sem("bc_out"), sem("ends")
            block = c3.enter_context(nc.Block())
            UNITS = CH * NS

            @block.sync
            def _(sp):
                for z in four:
                    sp.sem_inc(z, 4)
                sp.sem_inc(bc_out, 2)
                start_at_one(sp, ends)

            @block.tensor
            def _(pe):
                def spread(b, n, k):
                    pe.wait_ge(bc_out, 2 * (NS * b + n) + k + 1)
                    for h in range(2):
                        ins = pe.matmul(psBC[:, k, h * TB:(h + 1) * TB], sel32[:, k * NS + n, :],
                                        bcT[:, bass.ds(b * S + h * TB, TB)], start=True, stop=True)
                    ins.then_inc(bc_ps, 1)

                with pe.Fori(0, B) as b:
                    for n, k in ((0, 0), (0, 1), (1, 0), (1, 1), (2, 0)):
                        spread(b, n, k)
                    pe.wait_ge(ends, 3 * b + 1)
                    for w in range(UNITS):
                        n, c = w // CH, w % CH
                        if n + 2 + c < NS:
                            spread(b, n + 2 + c, 1 - c)
                        pe.wait_ge(read_out, UNITS * b + w + 5)
                        for h in range(2):
                            ins = pe.matmul(psY[:, c, h * TB:(h + 1) * TB], ident[:], part_y[:, w % 2, h * TB:(h + 1) * TB],
                                            start=n == 0, stop=n == NS - 1, skip_group_check=True)
                        ins.then_inc(summed, 1)

            @block.scalar
            def _(act):
                def take_bc(b, n, k):
                    dst, used = ((b_all, inject_ready), (c_all, read_out))[k]
                    act.wait_ge(bc_ps, 2 * (NS * b + n) + k + 1)
                    act.wait_ge(used, UNITS * b + CH * n + 2)
                    act.activation(dst[:, n % 2, :], psBC[:, k, :], ACT.Copy).then_inc(bc_out, 1)

                with act.Fori(0, B) as b:
                    take_bc(b, 0, 0)
                    take_bc(b, 0, 1)
                    for w in range(UNITS):
                        n, c = w // CH, w % CH
                        act.wait_ge(state_ready, UNITS * b + w + 3)
                        act.sem_inc(passed, 1)
                        act.activation(decay[:, w % 2, :], delta[:, c, bass.ds(b * S, S)], ACT.Exp,
                                       scale=aneg[:, c, n:n + 1]).then_inc(decay_ready, 1)
                        if n + 1 < NS:
                            take_bc(b, n + 1, c)

            @block.gpsimd
            def _(pool):
                with pool.Fori(0, B) as b:
                    pool.wait_ge(du_ready, b + 1)
                    for w in range(UNITS):
                        n, c = w // CH, w % CH
                        if c == 0:
                            pool.wait_ge(bc_out, 2 * (NS * b + n) + 3)
                        pool.wait_ge(state_ready, UNITS * b + w + 3)
                        pool.tensor_tensor(inject[:, w % 2, :], du[:, c, :], b_all[:, n % 2, :], ALU.mult).then_inc(inject_ready, 1)

            @block.vector
            def _(dve):
                def take_du(b):
                    seq = bass.ds(b * S, S)
                    dve.tensor_tensor(du[:], delta[:, :, seq], u[:, :, seq], ALU.mult).then_inc(du_ready, 1)

                def sequence(b, last):
                    seq = bass.ds(b * S, S)
                    base = UNITS * b
                    for i in range(UNITS + 1):
                        w = i
                        if w < UNITS:
                            dve.wait_ge(inject_ready, base + w + 5)
                            dve.wait_ge(decay_ready, base + w + 1)
                            dve.wait_ge(read_out, base + w + 2)
                            dve.tensor_tensor_scan(state[:, w % 3, :], decay[:, w % 2, :], inject[:, w % 2, :], 0.0,
                                                   ALU.mult, ALU.add).then_inc(state_ready, 1)
                        w = i - 1
                        if w >= 0:
                            n, c = w // CH, w % CH
                            if c == 0:
                                dve.wait_ge(bc_out, 2 * (NS * b + n) + 4)
                            dve.wait_ge(state_ready, base + w + 5)
                            dve.wait_ge(summed, base + w + 3)
                            dve.tensor_tensor(part_y[:, w % 2, :], state[:, w % 3, :], c_all[:, n % 2, :], ALU.mult).then_inc(read_out, 1)
                    if not last:
                        take_du(b + 1)
                    dve.wait_ge(summed, base + UNITS + 4)
                    for c in range(CH):
                        dve.scalar_tensor_tensor(y[:, c, :], u[:, c, seq], w_d[:, c, 0:1], psY[:, c, :], ALU.mult, ALU.add).then_inc(ends, 1)
                    dve.wait_ge(ends, 3 * b + 3)
                    dve.tensor_tensor(u[:, :, seq], y[:], gate[:, :, seq], ALU.mult).then_inc(ends, 1)
                    dve.wait_ge(ends, 3 * b + 4)

                take_du(0)
                with dve.Fori(0, B - 1) as b:
                    sequence(b, False)
                sequence(B - 1, True)

        with ExitStack() as c4:
            sem = lambda n: c4.enter_context(nc.semaphore(f"mo_{n}"))
            yT = c4.enter_context(nc.sbuf_tensor("mo_yT", [P, 2, TB], F32))
            psY = c4.enter_context(nc.psum_tensor("mo_psY", [P, 2, TB], F32))
            psT = c4.enter_context(nc.psum_tensor("mo_psT", [P, 2, TB], F32))
            y_ps, y_out, y_turned, added = (sem(n) for n in ("y_ps", "y_out", "y_turned", "added"))
            block = c4.enter_context(nc.Block())

            @block.sync
            def _(sp):
                start_at_one(sp, added, y_out, y_turned)

            @block.tensor
            def _(pe):
                with pe.Fori(0, BLOCKS // 2) as r:
                    for s in range(2):
                        pe.wait_ge(y_out, 2 * r + 1)
                        for c in range(CH):
                            ins = pe.matmul(psY[:, s, :], out_w[:, c, :], u[:, c, bass.ds((2 * r + s) * TB, TB)], start=c == 0, stop=c == CH - 1)
                        ins.then_inc(y_ps, 1)
                    for s in range(2):
                        pe.wait_ge(y_out, 2 * r + s + 2)
                        pe.wait_ge(added, 2 * r + 1)
                        for k in range(BT):
                            ins = pe.transpose(psT[:, s, k * P:(k + 1) * P], yT[:, s, k * P:(k + 1) * P], ident[:])
                        ins.then_inc(y_turned, 1)

            @block.scalar
            def _(act):
                with act.Fori(0, BLOCKS // 2) as r:
                    for s in range(2):
                        act.wait_ge(y_ps, 2 * r + s + 1)
                        act.wait_ge(y_turned, 2 * r + 1)
                        act.activation(yT[:, s, :], psY[:, s, :], ACT.Copy).then_inc(y_out, 1)

            @block.vector
            def _(dve):
                with dve.Fori(0, BLOCKS // 2) as r:
                    for s in range(2):
                        dve.wait_ge(y_turned, 2 * r + s + 2)
                        xt = x[:, bass.ds(BT * (2 * r + s), BT), :]
                        dve.tensor_tensor(xt, xt, psT[:, s, :].rearrange("p (t e) -> p t e", e=E), ALU.add).then_inc(added, 1)


MOE1 = ["wr", "br", "lower8", "upper", "ones", "numbers", "b2"]
NUMBERS = [(0, 256), (256, 288), (288, 336), (336, 337)]


SORTED = 40
LOOKAHEAD = 8
ROW1 = 1028


def moe1_block(nc, x, xT, rows, wr, br, lower8, upper, ones, numbers, b2, ident, w_rows, xs_d, ys_d, passed, out):
    NE, HC = 8, 4
    with ExitStack() as ctx:
        sb = lambda n, s, d=F32: ctx.enter_context(nc.sbuf_tensor(f"m1_{n}", s, d))
        sem = lambda n: ctx.enter_context(nc.semaphore(f"m1_{n}"))
        slot = sb("slot", [P, TILES], I32)
        w_row = sb("w_row", [P, SORTED + LOOKAHEAD], I32)
        with ExitStack() as rc:
            rb = lambda n, s, d=F32: rc.enter_context(nc.sbuf_tensor(f"r1_{n}", s, d))
            v, cnt, t = (rb(n, [P, TILES, NE]) for n in ("v", "cnt", "t"))
            hot = rb("hot", [P, TILES, NE], BF16)
            hotT = rb("hotT", [NE, NTOK])
            total, before = (rb(n, [P, NE, TILES]) for n in ("total", "before"))
            tiles, ends, starts = (rb(n, [P, NE]) for n in ("tiles", "ends", "starts"))
            place, expert = rb("place", [P, TILES]), rb("expert", [P, SORTED + LOOKAHEAD])
            passed_ends = rb("passed_ends", [P, SORTED + LOOKAHEAD, NE])
            blank = rb("blank", [P, 8, E])
            psL = rc.enter_context(nc.psum_tensor("r1_psL", [P, TILES, NE], F32))
            psR = rc.enter_context(nc.psum_tensor("r1_psR", [P, 2, TILES, NE], F32))
            psW = rc.enter_context(nc.psum_tensor("r1_psW", [P, 2, 512], F32))
            psB = rc.enter_context(nc.psum_tensor("r1_psB", [P, 2, 512], F32))
            (logits, steps, turned, evicted, hot_ready, counted, b2_ps, b2_added, blank_ready, blanked,
             sorted_) = (rc.enter_context(nc.semaphore(f"r1_{n}")) for n in (
                "logits", "steps", "turned", "evicted", "hot_ready", "counted", "b2_ps", "b2_added", "blank_ready",
                "blanked", "sorted"))
            block = rc.enter_context(nc.Block())

            @block.sync
            def _(sp):
                sp.wait_ge(blank_ready, 1)
                for k in range(SORTED // 8):
                    sp.dma_start(xs_d[k * 8 * P:(k + 1) * 8 * P].rearrange("(t p) e -> p t e", p=P), blank[:]).then_inc(blanked, 16)
                sp.wait_ge(blanked, 16 * (SORTED // 8))

            @block.tensor
            def _(pe):
                for k in range(TILES):
                    ins = pe.matmul(psL[:, k, :], xT[:, k * P:(k + 1) * P], wr[:], start=k == 0, stop=k == TILES - 1, skip_group_check=True)
                ins.then_inc(logits, 1)
                pe.wait_ge(hot_ready, 2)
                for k, m in enumerate((upper, ones)):
                    ins = pe.matmul(psR[:, k].rearrange("p t e -> p (t e)"), m, hot[:].rearrange("p t e -> p (t e)"),
                                    start=k == 0, stop=k == 1, skip_group_check=True)
                ins.then_inc(counted, 1)
                for q in range(TILES // 4 + 1):
                    if q < TILES // 4:
                        if q >= 2:
                            pe.wait_ge(evicted, q - 1)
                        for k in range(4):
                            ins = pe.transpose(psW[0:NE, q % 2, k * P:(k + 1) * P], v[:, 4 * q + k, :], ident[:])
                        ins.then_inc(turned, 1)
                    if q >= 1:
                        pe.wait_ge(evicted, q)
                        if q >= 3:
                            pe.wait_ge(b2_added, q - 2)
                        for k in range(4):
                            ins = pe.matmul(psB[:, (q - 1) % 2, k * P:(k + 1) * P], hotT[:, (4 * q - 4 + k) * P:(4 * q - 3 + k) * P], b2[:],
                                            start=k == 0, stop=k == 3, skip_group_check=True)
                        ins.then_inc(b2_ps, 1)

            @block.scalar
            def _(act):
                for q in range(TILES // 4):
                    act.wait_ge(turned, q + 1)
                    act.activation(hotT[:, q * 512:(q + 1) * 512], psW[0:NE, q % 2, :], ACT.Copy).then_inc(evicted, 1)

            @block.vector
            def _(dve):
                step = Chain(dve, steps)
                dve.memset(blank[:], 0.0).then_inc(blank_ready, 1)
                dve.wait_ge(logits, 1)
                step(dve.tensor_tensor(v[:], psL[:], br.unsqueeze(1).broadcast_to([P, TILES, NE]), ALU.add))
                rank_steps(step, dve, cnt[:], t[:], v[:], NE, lower8)
                step(dve.tensor_scalar(v[:], cnt[:], 0.5, None, ALU.is_lt))
                dve.sem_inc(hot_ready, 1)
                step(dve.tensor_copy(hot[:], v[:]))
                dve.sem_inc(hot_ready, 1)
                dve.wait_ge(counted, 1)
                restart, limits, tile_no, part_no = (numbers[:, a:b] for a, b in NUMBERS)
                step(dve.tensor_copy(total[:], psR[:, 1].rearrange("p t e -> p e t")))
                step(dve.tensor_tensor_scan(before[:].rearrange("p e t -> p (e t)"), restart, total[:].rearrange("p e t -> p (e t)"), 0.0,
                                            ALU.mult, ALU.add))
                step(dve.tensor_tensor(t[:].rearrange("p t e -> p (t e)").rearrange("p (e t) -> p e t", e=NE), bc(before[:, :, TILES - 1], TILES),
                                       limits.unsqueeze(1).broadcast_to([P, NE, TILES]), ALU.is_gt))
                step(dve.tensor_reduce(tiles[:], t[:].rearrange("p t e -> p (t e)").rearrange("p (e t) -> p e t", e=NE), AX.X, ALU.add))
                step(dve.tensor_tensor(before[:], before[:], total[:], ALU.subtract))
                step(dve.tensor_tensor_scan(ends[:], restart[:, 1:1 + NE], tiles[:], 0.0, ALU.mult, ALU.add))
                step(dve.tensor_tensor(starts[:], ends[:], tiles[:], ALU.subtract))
                step(dve.tensor_scalar(starts[:], starts[:], float(P), None, ALU.mult))
                step(dve.tensor_tensor(before[:], before[:], bc(starts[:], TILES), ALU.add))
                step(dve.tensor_tensor(t[:], psR[:, 0], before[:].rearrange("p e t -> p t e"), ALU.add))
                step(dve.tensor_tensor(t[:], t[:], v[:], ALU.mult))
                step(dve.tensor_reduce(place[:], t[:], AX.X, ALU.add))
                step(dve.tensor_copy(slot[:], place[:]))
                dve.sem_inc(hot_ready, 1)
                step(dve.tensor_tensor(passed_ends[:], ends[:].unsqueeze(1).broadcast_to([P, SORTED + LOOKAHEAD, NE]), bc(tile_no, NE), ALU.is_le))
                step(dve.tensor_reduce(expert[:], passed_ends[:], AX.X, ALU.add))
                step(dve.tensor_scalar(expert[:], expert[:], NE - 1.0, float(P), ALU.min, ALU.mult))
                step(dve.tensor_scalar(w_row[:], expert[:], part_no, None, ALU.add))
                for q in range(TILES // 4):
                    dve.wait_ge(b2_ps, q + 1)
                    xt = x[:, 4 * q:4 * q + 4, :]
                    dve.tensor_tensor(xt, xt, psB[:, q % 2, :].rearrange("p (t e) -> p t e", e=E), ALU.add).then_inc(b2_added, 1)

            @block.gpsimd
            def _(pool):
                pool.wait_ge(hot_ready, 3)
                pool.wait_ge(blanked, 16 * (SORTED // 8))
                for k in range(TILES):
                    pool.indirect_dma_start(xs_d[:], bass.IndirectOffsetOnAxis(ap=slot[:, k:k + 1], axis=0), rows[:, k, :],
                                            None).then_inc(sorted_, 16)
                pool.wait_ge(sorted_, 16 * TILES)

        TR = 8
        ROUNDS = SORTED // TR
        w = sb("w", [P, TR, ROW1])
        row_now = sb("row_now", [P, 2, 4], I32)
        xin = sb("xin", [P, 2, 4, E])
        xsT = sb("xsT", [P, 2, P])
        hid = sb("hid", [P, 2, HC, P])
        yo = sb("yo", [P, 2, 4, E])
        psX, psH, psY = (ctx.enter_context(nc.psum_tensor(f"m1_{n}", [P, 2, 512], F32)) for n in ("psX", "psH", "psY"))
        x_loaded, y_stored = ([sem(f"{n}{h}") for h in range(2)] for n in ("x_loaded", "y_stored"))
        w_loaded = [sem(f"w_loaded{k}") for k in range(TR)]
        xsT_ready, h_ps, hid_ready, y_out = two = [sem(n) for n in ("xsT_ready", "h_ps", "hid_ready", "y_out")]
        y_ps, x_ps, row_ready = sem("y_ps"), sem("x_ps"), sem("row_ready")
        experts = ctx.enter_context(ExitStack())
        block = experts.enter_context(nc.Block())

        @block.sync
        def _(sp):
            start_at_one(sp, *y_stored)
            for z in two:
                sp.sem_inc(z, 2)
            for z in (y_ps, x_ps):
                sp.sem_inc(z, TR)
            with sp.Fori(0, ROUNDS) as r:
                for h in range(2):
                    sp.wait_ge(x_ps, TR * r + 4 * h + 4)
                    sp.dma_start(xin[:, h], xs_d[bass.ds((TR * r + 4 * h) * P, 4 * P), :].rearrange("(t p) e -> p t e", p=P)).then_inc(x_loaded[h], 16)
            for h in range(2):
                sp.wait_ge(x_loaded[h], 16 * ROUNDS)

        @block.gpsimd
        def _(pool):
            with pool.Fori(0, ROUNDS) as r:
                for s in range(TR):
                    j = TR * r + s
                    pool.wait_ge(row_ready, 2 * r + s // 4 + 1)
                    pool.wait_ge(y_ps, j + 1)
                    pool.sem_inc(passed, 1)
                    pool.indirect_dma_start(w[:, s, :], None, w_rows[:], bass.IndirectOffsetOnAxis(ap=row_now[:, s // 4, s % 4:s % 4 + 1], axis=0)
                                            ).then_inc(w_loaded[s], 16)

        @block.tensor
        def _(pe):
            def turn(r, s):
                pe.wait_ge(x_loaded[s // 4], 16 * r + 16)
                pe.wait_ge(xsT_ready, TR * r + s + 1)
                pe.transpose(psX[:, s % 2, 0:P], xin[:, s // 4, s % 4, :], ident[:]).then_inc(x_ps, 1)

            def down(r, s):
                pe.wait_ge(hid_ready, TR * r + s + 3)
                pe.wait_ge(y_out, TR * r + s + 1)
                for c in range(HC):
                    ins = pe.matmul(psY[:, s % 2, 0:E], hid[:, s % 2, c, :], w[:, s, 512 + c * E:512 + (c + 1) * E], start=c == 0, stop=c == HC - 1)
                ins.then_inc(y_ps, 1)

            with pe.Fori(0, ROUNDS) as r:
                turn(r, 0)
                for s in range(TR):
                    if s + 1 < TR:
                        turn(r, s + 1)
                    pe.wait_ge(w_loaded[s], 16 * r + 16)
                    pe.wait_ge(xsT_ready, TR * r + s + 3)
                    pe.wait_ge(hid_ready, TR * r + s + 1)
                    for c in range(HC):
                        ins = pe.matmul(psH[:, s % 2, c * P:(c + 1) * P], w[:, s, c * P:(c + 1) * P], xsT[:, s % 2, :], start=c == 0,
                                        stop=c == HC - 1, skip_group_check=True)
                    ins.then_inc(h_ps, 1)
                    if s:
                        down(r, s - 1)
                down(r, TR - 1)

        @block.scalar
        def _(act):
            def store(r, h):
                act.wait_ge(y_out, TR * r + 4 * h + 6)
                act.dma_start(ys_d[bass.ds((TR * r + 4 * h) * P, 4 * P), :].rearrange("(t p) e -> p t e", p=P), yo[:, h]).then_inc(y_stored[h], 16)

            with act.Fori(0, ROUNDS) as r:
                for s in range(TR):
                    act.wait_ge(h_ps, TR * r + s + 3)
                    act.wait_ge(y_ps, TR * r + s + 7)
                    for c in range(HC):
                        ins = act.activation(hid[:, s % 2, c, :], psH[:, s % 2, c * P:(c + 1) * P], ACT.Gelu, bias=w[:, s, 1024 + c:1025 + c])
                    ins.then_inc(hid_ready, 1)
                    if s == 5:
                        store(r, 0)
                store(r, 1)
            for h in range(2):
                act.wait_ge(y_stored[h], 16 * ROUNDS + 1)

        @block.vector
        def _(dve):
            def take_x(r, s):
                dve.wait_ge(x_ps, TR * r + s + 1 + TR)
                dve.wait_ge(h_ps, TR * r + s + 1)
                dve.tensor_copy(xsT[:, s % 2, :], psX[:, s % 2, 0:P]).then_inc(xsT_ready, 1)

            def take_y(r, s):
                dve.wait_ge(y_ps, TR * r + s + 9)
                if s % 4 == 0:
                    dve.wait_ge(y_stored[s // 4], 16 * r + 1)
                dve.tensor_copy(yo[:, s // 4, s % 4, :], psY[:, s % 2, 0:E]).then_inc(y_out, 1)

            def set_rows(h, first):
                dve.tensor_copy(row_now[:, h, :], w_row[:, first]).then_inc(row_ready, 1)

            for h in range(2):
                set_rows(h, slice(4 * h, 4 * h + 4))
            with dve.Fori(0, ROUNDS) as r:
                take_x(r, 0)
                for s in range(TR):
                    if s + 1 < TR:
                        take_x(r, s + 1)
                    if s:
                        take_y(r, s - 1)
                    if s == 5:
                        set_rows(0, bass.ds(TR * r + TR, 4))
                take_y(r, TR - 1)
                set_rows(1, bass.ds(TR * r + TR + 4, 4))

        experts.close()
        with ExitStack() as fc:
            fetched = [fc.enter_context(nc.semaphore(f"f1_fetched{q}")) for q in range(2)]
            added, stored = (fc.enter_context(nc.semaphore(f"f1_{n}")) for n in ("added", "stored"))
            block = fc.enter_context(nc.Block())

            @block.gpsimd
            def _(pool):
                for k in range(TILES):
                    pool.indirect_dma_start(rows[:, k, :], None, ys_d[:], bass.IndirectOffsetOnAxis(ap=slot[:, k:k + 1], axis=0)
                                            ).then_inc(fetched[k // 16], 16)

            @block.vector
            def _(dve):
                for q in range(2):
                    dve.wait_ge(fetched[q], 256)
                    xt = x[:, 16 * q:16 * q + 16, :]
                    dve.tensor_tensor(xt, xt, rows[:, 16 * q:16 * q + 16, :], ALU.add).then_inc(added, 1)

            @block.sync
            def _(sp):
                for q in range(2):
                    sp.wait_ge(added, q + 1)
                    sp.dma_start(out[16 * q * P:(16 * q + 16) * P].rearrange("(t p) e -> p t e", p=P), x[:, 16 * q:16 * q + 16, :]).then_inc(stored, 16)
                sp.wait_ge(stored, 32)


def four_layers(nc, a, out):
    with ExitStack() as ctx:
        sb = lambda n, s, d=F32: ctx.enter_context(nc.sbuf_tensor(n, s, d))
        x = sb("x", [P, TILES, E])
        xT = sb("xT", [P, NTOK])
        ident = sb("ident", [P, P])
        identb = sb("identb", [P, P], BF16)
        half = sb("half", [P, CT])
        vd = nc.dram_tensor("v_by_token", [NTOK + P, HEADS * 2 * HD], BF16).ap()
        od = nc.dram_tensor("heads_out", [NTOK, HEADS * HD], F32).ap()
        xs_d, ys_d = (nc.dram_tensor(n, [SORTED * P, E], F32).ap() for n in ("sorted_in", "sorted_out"))
        const_ready = ctx.enter_context(nc.semaphore("const_ready"))
        const_loaded = ctx.enter_context(nc.semaphore("const_loaded"))
        passed = ctx.enter_context(nc.semaphore("passed"))

        with nc.Block() as block:
            @block.sync
            def _(sp):
                sp.dma_start(ident[:], a["ident"]).then_inc(const_loaded, 16)
                sp.dma_start(identb[:], a["identb"]).then_inc(const_loaded, 16)
                sp.wait_ge(const_loaded, 32)

            @block.vector
            def _(dve):
                dve.memset(half[:], -0.5).then_inc(const_ready, 1)
                dve.wait_ge(const_ready, 1)

        def weights(c, names):
            held = {n: c.enter_context(nc.sbuf_tensor(f"w_{n}", list(a[n].shape), a[n].dtype))[:] for n in names}
            return held, [(held[n], a[n]) for n in names]

        def cut(c, w, names):
            parts = {n: [c.enter_context(nc.sbuf_tensor(f"w_{n}{k}", list(a[n].shape), BF16))[:] for k in "hl"] for n in names}
            return parts, [(w[n], *parts[n]) for n in names]

        with ExitStack() as c:
            w, loads = weights(c, ["wq", "wk", "wv", "mask_qk", "mask_kq", "row_mask", "wp", "bp"])
            p, splits = cut(c, w, ["wq", "wk", "wv"])
            xh, xl = (c.enter_context(nc.sbuf_tensor(n, [P, NTOK + 2 * P], BF16)) for n in ("xh", "xl"))
            layernorm_block(nc, "ln0", x, xT, half, ident, False, loads, xh, xl, splits, x_dram=a["L0_attn_x"])
            attention_block(nc, xh, xl, p["wq"], p["wk"], p["wv"], identb[:], w["mask_qk"], w["mask_kq"], w["row_mask"], vd, od)
            projection_block(nc, x, w["wp"], w["bp"], od, ident)
        with ExitStack() as c:
            names = ["wgate", "gbias", "lower4", "lower16", "wg", "wu", "wd", "sel"]
            w, loads = weights(c, names)
            layernorm_block(nc, "ln1", x, xT, half, ident, True, loads)
            moe0_block(nc, x, xT, *[w[n] for n in names], ident, identb[:])
        with ExitStack() as c:
            names = [n for n in MAMBA if n != "ident"]
            w, loads = weights(c, names + ["norm_w"])
            layernorm_block(nc, "ln2", x, xT, half, ident, True, loads, rms_w=w["norm_w"])
            mamba_block(nc, x, xT, *[w[n] for n in names], ident, passed)
        with ExitStack() as c:
            w, loads = weights(c, MOE1)
            rows = c.enter_context(nc.sbuf_tensor("rows", [P, TILES, E], F32))
            layernorm_block(nc, "ln3", x, xT, half, ident, False, loads, rows=rows)
            moe1_block(nc, x, xT, rows, *[w[n] for n in MOE1], ident, a["w_rows"], xs_d, ys_d, passed, out)


def host_constants():
    bf16 = np.dtype("bfloat16")
    c = {"ident": np.eye(P, dtype=np.float32), "identb": np.eye(P, dtype=np.float32).astype(bf16)}
    at = np.arange(P) % TT * HEADS + np.arange(P) // TT
    mask = np.where(at[None, :] <= at[:, None], 0.0, -1e30).astype(bf16)
    c["mask_qk"], c["mask_kq"] = mask, np.ascontiguousarray(mask.T)
    rows = np.zeros((MROWS, PT, P), np.float32)
    for r in range(MROWS):
        rows[r, r % PT] = 1
    c["row_mask"] = rows.astype(bf16)
    for n in (4, 8, 16):
        c[f"lower{n}"] = np.tile(np.arange(n - 1, -1, -1, dtype=np.float32), (P, 1))
    sel = np.zeros((3, 16, 8, P), np.float32)
    for e in range(16):
        sel[:, e, e // 2, (e % 2) * 64:(e % 2 + 1) * 64] = 1
    c["sel"] = sel.reshape(48, 8, P).astype(bf16)
    c["upper"] = np.triu(np.ones((P, P), np.float32), 1).astype(bf16)
    c["ones"] = np.ones((P, P), np.float32).astype(bf16)
    restart = np.tile(np.arange(TILES) > 0, 8)
    row = np.concatenate([restart, np.arange(TILES) * P, np.arange(SORTED + LOOKAHEAD)])
    c["numbers"] = np.concatenate([np.tile(row, (P, 1)), np.arange(P)[:, None]], 1).astype(np.float32)
    sel = np.zeros((3, 32, 32, P), np.float32)
    for e in range(32):
        sel[:, e, e] = 1
    c["sel32"] = sel.reshape(96, 32, P).astype(bf16)
    return c


def host_weights(d):
    ca = np.ascontiguousarray
    pair = lambda w: ca(np.stack([np.concatenate([w[j], w[j + PAIRS]], 1) for j in range(PAIRS)], 1))
    w = {"wq": pair(d["L0_attn_Wq"]), "wk": pair(d["L0_attn_Wk"]),
         "wv": ca(d["L0_attn_Wv"].transpose(1, 0, 2).reshape(E, HEADS * HD)),
         "wp": ca(d["L0_attn_proj_w"].T.reshape(8, P, E).transpose(1, 0, 2)),
         "bp": ca(np.broadcast_to(d["L0_attn_proj_b"], (P, E)))}
    w["wgate"] = ca(d["L0_ffn_gate_w"].T)
    w["gbias"] = ca(np.broadcast_to(d["L0_ffn_gate_bias"], (P, 16)))
    up = lambda we, ws: ca(np.concatenate([we.reshape(1024, E), ws]).reshape(9, P, E).transpose(2, 0, 1))
    w["wg"], w["wu"] = up(d["L0_ffn_Wg"], d["L0_ffn_Ws_g"]), up(d["L0_ffn_Wu"], d["L0_ffn_Ws_u"])
    w["wd"] = ca(np.concatenate([d["L0_ffn_Wd"].transpose(0, 2, 1).reshape(1024, E), d["L0_ffn_Ws_d"].T]).reshape(9, P, E).transpose(1, 0, 2))
    chan = lambda a: ca(a.reshape(2, P, -1).transpose(1, 0, 2))
    w["norm_w"] = ca(d["L1_attn_norm_w"].reshape(P, 1))
    w["skip_w"], w["in_w"] = ca(d["L1_attn_skip_w"].T), ca(d["L1_attn_in_w"].T)
    w["conv_w"], w["conv_b"] = chan(d["L1_attn_conv_w"]), chan(d["L1_attn_conv_b"])
    w["wdbc"] = chan(np.concatenate([d["L1_attn_wd1"], d["L1_attn_wb"], d["L1_attn_wc"]]).T)
    w["wd2"], w["wd2_b"] = ca(d["L1_attn_wd2"].T), chan(d["L1_attn_wd2_b"])
    w["a_log"], w["w_d"] = chan(d["L1_attn_A_log"]), chan(d["L1_attn_W_D"])
    w["out_w"] = chan(d["L1_attn_out_w"].T)
    w["wr"], w["br"] = ca(d["L1_ffn_wr"]), ca(np.broadcast_to(d["L1_ffn_br"], (P, 8)))
    w1, w2, b1 = d["L1_ffn_w1"], d["L1_ffn_w2"].reshape(8, 4, P, E), d["L1_ffn_b1"].reshape(8, 4, P)
    w["w_rows"] = ca(np.concatenate([w1, w2.transpose(0, 2, 1, 3).reshape(8, P, 512), b1.transpose(0, 2, 1)], 2).reshape(8 * P, ROW1))
    w["b2"] = ca(d["L1_ffn_b2"])
    return w


def kernel(**inputs):
    import concourse.bacc as bacc
    from concourse.bass_utils import run_bass_kernel_spmd

    data = {n: np.asarray(v) for n, v in inputs.items()}
    arrays = {**host_constants(), **host_weights(data)}
    arrays["L0_attn_x"] = np.ascontiguousarray(data["L0_attn_x"].reshape(NTOK, E))
    nc = bacc.Bacc("TRN2", target_bir_lowering=False, num_devices=1)
    arrays = {f"in_{n}": v for n, v in arrays.items()}
    aps = {n[3:]: nc.dram_tensor(n, v.shape, mybir.dt.from_np(v.dtype), kind="ExternalInput").ap() for n, v in arrays.items()}
    out = nc.dram_tensor("out_0", (NTOK, E), F32, kind="ExternalOutput").ap()
    four_layers(nc, aps, out)
    r = run_bass_kernel_spmd(nc, [arrays], core_ids=[0])
    return r.results[0]["out_0"].reshape(B, S, E)
```
